# Optimizing a Trainium2 kernel written in Bass

```python
import numpy as np
import jax
import jax.numpy as jnp

def _softmax(x, axis=-1):
    return jax.nn.softmax(x, axis=axis)

def _gelu(x):
    return jax.nn.gelu(x, approximate=True)

def _silu(x):
    return jax.nn.silu(x)

def _sigmoid(x):
    return jax.nn.sigmoid(x)

def _layernorm(x, axis=-1, eps=1e-05):
    m = jnp.mean(x, axis=axis, keepdims=True)
    v = jnp.var(x, axis=axis, keepdims=True)
    return (x - m) / jnp.sqrt(v + eps)

def _scatter_add(tgt, idx, src, axis=0):
    return tgt.at[idx].add(src)

def _segment_sum(src, seg, n):
    return jax.ops.segment_sum(src, seg, n)
kernel_name = 'mk_vit_tower_d4_tok_img768_r4_8829eb'

def setup_inputs(seed: int=0):
    np.random.seed(seed)
    _w = jnp.asarray

    def _rec_inputs():
        import jax
        import jax.numpy as jnp
        _rk = jax.random.key(seed)
        x = -0.00016672 + 0.999947 * jax.random.normal(jax.random.fold_in(_rk, 1), (16, 96, 96, 3), jnp.float32)
        return x
    x = _rec_inputs()

    def _L0_tok_setup():
        import jax, jax.numpy as jnp
        import numpy as np
        P = 16
        D = 192

        def _patchify(x):
            B, H, W_, C = x.shape
            gh, gw = (H // P, W_ // P)
            x = x.reshape(B, gh, P, gw, P, C)
            x = x.transpose(0, 1, 3, 2, 4, 5)
            return x.reshape(B, gh * gw, P * P * C)
        key = jax.random.key(seed)
        k1, k2, k3 = jax.random.split(key, 3)
        B, H, W_, C = (64, 96, 96, 3)
        x = jax.random.normal(k1, (B, H, W_, C), dtype=jnp.float32)
        Wk = jax.random.normal(k2, (P * P * C, D), dtype=jnp.float32) * 0.02
        class_emb = jnp.zeros((1, 1, D), dtype=jnp.float32)
        N = H // P * (W_ // P)
        pos_emb = jax.random.normal(k3, (1, N + 1, D), dtype=jnp.float32) * 0.02
        return {'x': x, 'W': Wk, 'class_emb': class_emb, 'pos_emb': pos_emb}
    _L0_tok_all = _L0_tok_setup()
    _L0_tok_in = {k: v for k, v in _L0_tok_all.items() if k in ('W', 'class_emb', 'pos_emb')}
    del _L0_tok_all

    def _L0_attn_setup():
        import jax, jax.numpy as jnp
        import numpy as np
        import math
        D_MODEL = 192
        D_STATE = 16
        D_CONV = 4
        EXPAND = 2
        N_EXP = 8
        TOP_K = 2
        D_INNER = D_MODEL * EXPAND
        D_FF = 4 * D_MODEL
        B_SZ, T_LEN = (2, 256)
        EPS = 1e-06

        def _rms(x, g):
            return x * jax.lax.rsqrt(jnp.mean(x * x, axis=-1, keepdims=True) + EPS) * g
        key = jax.random.key(seed)
        ks = jax.random.split(key, 12)
        s = 0.02
        x = jax.random.normal(ks[0], (B_SZ, T_LEN, D_MODEL), jnp.float32)
        g_mamba = jnp.ones((D_MODEL,), jnp.float32)
        w_in = jax.random.normal(ks[1], (D_MODEL, 2 * D_INNER), jnp.float32) * s
        conv_w = jax.random.normal(ks[2], (D_INNER, D_CONV), jnp.float32) * s
        conv_b = jnp.zeros((D_INNER,), jnp.float32)
        w_xproj = jax.random.normal(ks[3], (D_INNER, 2 * D_STATE + 1), jnp.float32) * s
        w_dt = jax.random.normal(ks[4], (1, D_INNER), jnp.float32) * s
        b_dt = jnp.full((D_INNER,), math.log(0.001), jnp.float32)
        A_log = jnp.log(jnp.arange(1, D_STATE + 1, dtype=jnp.float32)) * jnp.ones((D_INNER, 1), jnp.float32)
        D_skip = jnp.ones((D_INNER,), jnp.float32)
        w_out = jax.random.normal(ks[5], (D_INNER, D_MODEL), jnp.float32) * s
        g_moe = jnp.ones((D_MODEL,), jnp.float32)
        w_router = jax.random.normal(ks[6], (D_MODEL, N_EXP), jnp.float32) * s
        g_exp = jnp.ones((N_EXP, D_MODEL), jnp.float32)
        w1 = jax.random.normal(ks[7], (N_EXP, D_MODEL, D_FF), jnp.float32) * s
        w3 = jax.random.normal(ks[8], (N_EXP, D_MODEL, D_FF), jnp.float32) * s
        w2 = jax.random.normal(ks[9], (N_EXP, D_FF, D_MODEL), jnp.float32) * s
        return dict(x=x, g_mamba=g_mamba, w_in=w_in, conv_w=conv_w, conv_b=conv_b, w_xproj=w_xproj, w_dt=w_dt, b_dt=b_dt, A_log=A_log, D_skip=D_skip, w_out=w_out, g_moe=g_moe, w_router=w_router, g_exp=g_exp, w1=w1, w3=w3, w2=w2)
    _L0_attn_all = _L0_attn_setup()
    _L0_attn_in = {k: v for k, v in _L0_attn_all.items() if k in ('g_mamba', 'w_in', 'conv_w', 'conv_b', 'w_xproj', 'w_dt', 'b_dt', 'A_log', 'D_skip', 'w_out', 'g_moe', 'w_router', 'g_exp', 'w1', 'w3', 'w2')}
    del _L0_attn_all

    def _L0_ffn_setup():
        import jax, jax.numpy as jnp
        import numpy as np
        N_EMBD = 192
        HIDDEN = 4 * N_EMBD
        N_EXPERTS = 8
        TOP_K = 2
        key = jax.random.key(seed)
        ks = jax.random.split(key, 4)
        B, T, C, E, H = (4, 512, N_EMBD, N_EXPERTS, HIDDEN)
        x = jax.random.normal(ks[0], (B, T, C), dtype=jnp.float32)
        gate_w = jax.random.normal(ks[1], (E, C), dtype=jnp.float32) * 0.02
        gate_b = jnp.zeros((E,), dtype=jnp.float32)
        w_fc = jax.random.normal(ks[2], (E, H, C), dtype=jnp.float32) * 0.02
        b_fc = jnp.zeros((E, H), dtype=jnp.float32)
        w_proj = jax.random.normal(ks[3], (E, C, H), dtype=jnp.float32) * 0.02
        b_proj = jnp.zeros((E, C), dtype=jnp.float32)
        return {'x': x, 'gate_w': gate_w, 'gate_b': gate_b, 'w_fc': w_fc, 'b_fc': b_fc, 'w_proj': w_proj, 'b_proj': b_proj}
    _L0_ffn_all = _L0_ffn_setup()
    _L0_ffn_in = {k: v for k, v in _L0_ffn_all.items() if k in ('gate_w', 'gate_b', 'w_fc', 'b_fc', 'w_proj', 'b_proj')}
    del _L0_ffn_all

    def _L1_attn_setup():
        import jax, jax.numpy as jnp
        import numpy as np
        import math
        EMBED_DIM = 192
        NUM_HEADS = 12
        N_QUBITS = 96
        D_K = N_QUBITS // NUM_HEADS
        key = jax.random.key(seed)
        k1, k2, k3 = jax.random.split(key, 3)
        x = jax.random.normal(k1, (8, 256, EMBED_DIM), dtype=jnp.float32)
        theta = jax.random.uniform(k2, (N_QUBITS,), dtype=jnp.float32, minval=-math.pi, maxval=math.pi)
        W_combine = jax.random.normal(k3, (EMBED_DIM, N_QUBITS), dtype=jnp.float32) / math.sqrt(N_QUBITS)
        return {'x': x, 'theta': theta, 'W_combine': W_combine}
    _L1_attn_all = _L1_attn_setup()
    _L1_attn_in = {k: v for k, v in _L1_attn_all.items() if k in ('theta', 'W_combine')}
    del _L1_attn_all

    def _L1_ffn_setup():
        import jax, jax.numpy as jnp
        import numpy as np
        B, S, D, F, E = (8, 512, 192, 768, 16)
        CAP = 64
        EPS = 1e-06

        def _switch_moe_block(x, ln_w, w_router, wi, wo):
            var = jnp.mean(jnp.square(x.astype(jnp.float32)), axis=-1, keepdims=True)
            normed = (x * jax.lax.rsqrt(var + EPS)).astype(x.dtype) * ln_w
            logits = jnp.einsum('bsd,de->bse', normed.astype(jnp.float32), w_router.astype(jnp.float32))
            probs = jax.nn.softmax(logits, axis=-1)
            expert_idx = jnp.argmax(probs, axis=-1)
            onehot = jax.nn.one_hot(expert_idx, E, dtype=jnp.float32)
            priority = jnp.cumsum(onehot, axis=1)
            keep = onehot * (priority <= CAP)
            pos = (priority - 1.0).astype(jnp.int32)
            dispatch = keep[..., None] * jax.nn.one_hot(pos, CAP, dtype=jnp.float32)
            expert_in = jnp.einsum('bsec,bsd->becd', dispatch, normed)
            h = jax.nn.relu(jnp.einsum('becd,edf->becf', expert_in, wi))
            expert_out = jnp.einsum('becf,efd->becd', h, wo)
            combined = jnp.einsum('bsec,becd->bsd', dispatch, expert_out)
            routed = jnp.sum(dispatch, axis=(2, 3)) > 0
            next_states = jnp.where(routed[..., None], combined.astype(x.dtype), normed)
            router_prob = jnp.max(probs, axis=-1, keepdims=True).astype(x.dtype)
            return x + router_prob * next_states
        key = jax.random.key(seed)
        k_x, k_r, k_wi, k_wo = jax.random.split(key, 4)
        x = jax.random.normal(k_x, (B, S, D), dtype=jnp.float32)
        ln_w = jnp.ones((D,), dtype=jnp.float32)
        w_router = jax.random.normal(k_r, (D, E), dtype=jnp.float32) * 0.02
        wi = jax.random.normal(k_wi, (E, D, F), dtype=jnp.float32) * D ** (-0.5)
        wo = jax.random.normal(k_wo, (E, F, D), dtype=jnp.float32) * F ** (-0.5)
        return {'x': x, 'ln_w': ln_w, 'w_router': w_router, 'wi': wi, 'wo': wo}
    _L1_ffn_all = _L1_ffn_setup()
    _L1_ffn_in = {k: v for k, v in _L1_ffn_all.items() if k in ('ln_w', 'w_router', 'wi', 'wo')}
    del _L1_ffn_all

    def _L2_attn_setup():
        import jax, jax.numpy as jnp
        import numpy as np
        import math
        B, L, D = (2, 512, 192)
        H, DK = (8, 64)
        DV = D // H
        N_POS = 32
        DFF = 2 * D
        EPS = 1e-05

        def _rel_basis(l: int, n: int) -> jnp.ndarray:
            pos = jnp.arange(l)
            distance = pos[None, :] - pos[:, None]
            pow_rate = jnp.exp(jnp.log(jnp.float32((l + 1) / 2.0)) / (n // 2))
            center_widths = pow_rate ** jnp.arange(1, n // 2 + 1, dtype=jnp.float32)
            d = distance[:, :, None].astype(jnp.float32)
            unsigned = (jnp.abs(d) <= center_widths).astype(jnp.float32)
            signed = jnp.sign(d) * unsigned
            return jnp.concatenate([unsigned, signed], axis=-1)

        def _rmsnorm(x, w):
            norm = jnp.mean(x * x, axis=-1, keepdims=True)
            return x * jax.lax.rsqrt(norm + EPS) * w
        key = jax.random.key(seed)
        ks = jax.random.split(key, 12)
        s = 0.02
        return {'x': jax.random.normal(ks[0], (B, L, D), jnp.float32), 'norm1_w': jnp.ones((D,), jnp.float32), 'norm2_w': jnp.ones((D,), jnp.float32), 'wq': jax.random.normal(ks[1], (D, H * DK), jnp.float32) * s, 'wk': jax.random.normal(ks[2], (D, H * DK), jnp.float32) * s, 'wv': jax.random.normal(ks[3], (D, H * DV), jnp.float32) * s, 'wo': jax.random.normal(ks[4], (H * DV, D), jnp.float32) * s, 'bo': jnp.zeros((D,), jnp.float32), 'u_param': jax.random.normal(ks[5], (H, DK), jnp.float32) * s, 'v_param': jax.random.normal(ks[6], (H, DK), jnp.float32) * s, 'w_pos': jax.random.normal(ks[7], (H, DK, N_POS), jnp.float32) * s, 'w1': jax.random.normal(ks[8], (D, DFF), jnp.float32) * s, 'b1': jnp.zeros((DFF,), jnp.float32), 'w2': jax.random.normal(ks[9], (DFF, D), jnp.float32) * s, 'b2': jnp.zeros((D,), jnp.float32)}
    _L2_attn_all = _L2_attn_setup()
    _L2_attn_in = {k: v for k, v in _L2_attn_all.items() if k in ('norm1_w', 'norm2_w', 'wq', 'wk', 'wv', 'wo', 'bo', 'u_param', 'v_param', 'w_pos', 'w1', 'b1', 'w2', 'b2')}
    del _L2_attn_all

    def _L2_ffn_setup():
        import jax, jax.numpy as jnp
        import numpy as np
        B, T, C = (2, 256, 192)
        H, NE, K = (768, 8, 2)
        key = jax.random.key(seed)
        k1, k2, k3, k4 = jax.random.split(key, 4)
        x = jax.random.normal(k1, (B, T, C), dtype=jnp.float32)
        w_fc = jax.random.normal(k2, (C, H * NE), dtype=jnp.float32) * 0.02
        w_proj = jax.random.normal(k3, (H * NE, C), dtype=jnp.float32) * (0.02 * (2 * 12) ** (-0.5))
        w_gate = jax.random.normal(k4, (C, NE), dtype=jnp.float32) * 0.02
        return {'x': x, 'w_fc': w_fc, 'w_proj': w_proj, 'w_gate': w_gate}
    _L2_ffn_all = _L2_ffn_setup()
    _L2_ffn_in = {k: v for k, v in _L2_ffn_all.items() if k in ('w_fc', 'w_proj', 'w_gate')}
    del _L2_ffn_all

    def _L3_attn_setup():
        import jax, jax.numpy as jnp
        import numpy as np
        EMBED_DIM = 192
        NUM_HEADS = 12
        HEAD_DIM = EMBED_DIM // NUM_HEADS
        SCALING = HEAD_DIM ** (-0.5)
        B, S = (2, 512)
        key = jax.random.key(seed)
        k1, k2, k3 = jax.random.split(key, 3)
        x_q = jax.random.normal(k1, (B, S, EMBED_DIM), dtype=jnp.float32)
        lim_qkv = (6.0 / (EMBED_DIM + 3 * EMBED_DIM)) ** 0.5
        lim_out = (6.0 / (2 * EMBED_DIM)) ** 0.5
        w_qkv = jax.random.uniform(k2, (3 * EMBED_DIM, EMBED_DIM), jnp.float32, -lim_qkv, lim_qkv)
        b_qkv = jnp.zeros((3 * EMBED_DIM,), jnp.float32)
        w_out = jax.random.uniform(k3, (EMBED_DIM, EMBED_DIM), jnp.float32, -lim_out, lim_out)
        b_out = jnp.zeros((EMBED_DIM,), jnp.float32)
        return {'x_q': x_q, 'w_qkv': w_qkv, 'b_qkv': b_qkv, 'w_out': w_out, 'b_out': b_out}
    _L3_attn_all = _L3_attn_setup()
    _L3_attn_in = {k: v for k, v in _L3_attn_all.items() if k in ('w_qkv', 'b_qkv', 'w_out', 'b_out')}
    del _L3_attn_all

    def _L3_ffn_setup():
        import jax, jax.numpy as jnp
        import numpy as np
        SEQ, BATCH, EMBED = (256, 2, 192)
        E = 16
        FFN_H = 384
        K_SHARED = 1
        K_ROUTE = 3
        LN_EPS = 1e-05
        NEG_INF = -1000000000.0
        key = jax.random.key(seed)
        ks = jax.random.split(key, 4)
        x = jax.random.normal(ks[0], (SEQ, BATCH, EMBED), dtype=jnp.float32)
        gate_w = jax.random.normal(ks[1], (EMBED, E), dtype=jnp.float32) * 0.02
        gate_b = jnp.zeros((E,), jnp.float32)
        fc1_w = jax.random.normal(ks[2], (E, EMBED, FFN_H), dtype=jnp.float32) * 0.02
        fc1_b = jnp.zeros((E, FFN_H), jnp.float32)
        ln_w = jnp.ones((E, FFN_H), jnp.float32)
        ln_b = jnp.zeros((E, FFN_H), jnp.float32)
        fc2_w = jax.random.normal(ks[3], (E, FFN_H, EMBED), dtype=jnp.float32) * 0.02
        fc2_b = jnp.zeros((E, EMBED), jnp.float32)
        return {'x': x, 'gate_w': gate_w, 'gate_b': gate_b, 'fc1_w': fc1_w, 'fc1_b': fc1_b, 'ln_w': ln_w, 'ln_b': ln_b, 'fc2_w': fc2_w, 'fc2_b': fc2_b}
    _L3_ffn_all = _L3_ffn_setup()
    _L3_ffn_in = {k: v for k, v in _L3_ffn_all.items() if k in ('gate_w', 'gate_b', 'fc1_w', 'fc1_b', 'ln_w', 'ln_b', 'fc2_w', 'fc2_b')}
    del _L3_ffn_all
    return {'x': x, 'L0_tok_W': _L0_tok_in['W'], 'L0_tok_class_emb': _L0_tok_in['class_emb'], 'L0_tok_pos_emb': _L0_tok_in['pos_emb'], 'L0_attn_g_mamba': _L0_attn_in['g_mamba'], 'L0_attn_w_in': _L0_attn_in['w_in'], 'L0_attn_conv_w': _L0_attn_in['conv_w'], 'L0_attn_conv_b': _L0_attn_in['conv_b'], 'L0_attn_w_xproj': _L0_attn_in['w_xproj'], 'L0_attn_w_dt': _L0_attn_in['w_dt'], 'L0_attn_b_dt': _L0_attn_in['b_dt'], 'L0_attn_A_log': _L0_attn_in['A_log'], 'L0_attn_D_skip': _L0_attn_in['D_skip'], 'L0_attn_w_out': _L0_attn_in['w_out'], 'L0_attn_g_moe': _L0_attn_in['g_moe'], 'L0_attn_w_router': _L0_attn_in['w_router'], 'L0_attn_g_exp': _L0_attn_in['g_exp'], 'L0_attn_w1': _L0_attn_in['w1'], 'L0_attn_w3': _L0_attn_in['w3'], 'L0_attn_w2': _L0_attn_in['w2'], 'L0_ffn_gate_w': _L0_ffn_in['gate_w'], 'L0_ffn_gate_b': _L0_ffn_in['gate_b'], 'L0_ffn_w_fc': _L0_ffn_in['w_fc'], 'L0_ffn_b_fc': _L0_ffn_in['b_fc'], 'L0_ffn_w_proj': _L0_ffn_in['w_proj'], 'L0_ffn_b_proj': _L0_ffn_in['b_proj'], 'L1_attn_theta': _L1_attn_in['theta'], 'L1_attn_W_combine': _L1_attn_in['W_combine'], 'L1_ffn_ln_w': _L1_ffn_in['ln_w'], 'L1_ffn_w_router': _L1_ffn_in['w_router'], 'L1_ffn_wi': _L1_ffn_in['wi'], 'L1_ffn_wo': _L1_ffn_in['wo'], 'L2_attn_norm1_w': _L2_attn_in['norm1_w'], 'L2_attn_norm2_w': _L2_attn_in['norm2_w'], 'L2_attn_wq': _L2_attn_in['wq'], 'L2_attn_wk': _L2_attn_in['wk'], 'L2_attn_wv': _L2_attn_in['wv'], 'L2_attn_wo': _L2_attn_in['wo'], 'L2_attn_bo': _L2_attn_in['bo'], 'L2_attn_u_param': _L2_attn_in['u_param'], 'L2_attn_v_param': _L2_attn_in['v_param'], 'L2_attn_w_pos': _L2_attn_in['w_pos'], 'L2_attn_w1': _L2_attn_in['w1'], 'L2_attn_b1': _L2_attn_in['b1'], 'L2_attn_w2': _L2_attn_in['w2'], 'L2_attn_b2': _L2_attn_in['b2'], 'L2_ffn_w_fc': _L2_ffn_in['w_fc'], 'L2_ffn_w_proj': _L2_ffn_in['w_proj'], 'L2_ffn_w_gate': _L2_ffn_in['w_gate'], 'L3_attn_w_qkv': _L3_attn_in['w_qkv'], 'L3_attn_b_qkv': _L3_attn_in['b_qkv'], 'L3_attn_w_out': _L3_attn_in['w_out'], 'L3_attn_b_out': _L3_attn_in['b_out'], 'L3_ffn_gate_w': _L3_ffn_in['gate_w'], 'L3_ffn_gate_b': _L3_ffn_in['gate_b'], 'L3_ffn_fc1_w': _L3_ffn_in['fc1_w'], 'L3_ffn_fc1_b': _L3_ffn_in['fc1_b'], 'L3_ffn_ln_w': _L3_ffn_in['ln_w'], 'L3_ffn_ln_b': _L3_ffn_in['ln_b'], 'L3_ffn_fc2_w': _L3_ffn_in['fc2_w'], 'L3_ffn_fc2_b': _L3_ffn_in['fc2_b']}

def reference(x, L0_tok_W, L0_tok_class_emb, L0_tok_pos_emb, L0_attn_g_mamba, L0_attn_w_in, L0_attn_conv_w, L0_attn_conv_b, L0_attn_w_xproj, L0_attn_w_dt, L0_attn_b_dt, L0_attn_A_log, L0_attn_D_skip, L0_attn_w_out, L0_attn_g_moe, L0_attn_w_router, L0_attn_g_exp, L0_attn_w1, L0_attn_w3, L0_attn_w2, L0_ffn_gate_w, L0_ffn_gate_b, L0_ffn_w_fc, L0_ffn_b_fc, L0_ffn_w_proj, L0_ffn_b_proj, L1_attn_theta, L1_attn_W_combine, L1_ffn_ln_w, L1_ffn_w_router, L1_ffn_wi, L1_ffn_wo, L2_attn_norm1_w, L2_attn_norm2_w, L2_attn_wq, L2_attn_wk, L2_attn_wv, L2_attn_wo, L2_attn_bo, L2_attn_u_param, L2_attn_v_param, L2_attn_w_pos, L2_attn_w1, L2_attn_b1, L2_attn_w2, L2_attn_b2, L2_ffn_w_fc, L2_ffn_w_proj, L2_ffn_w_gate, L3_attn_w_qkv, L3_attn_b_qkv, L3_attn_w_out, L3_attn_b_out, L3_ffn_gate_w, L3_ffn_gate_b, L3_ffn_fc1_w, L3_ffn_fc1_b, L3_ffn_ln_w, L3_ffn_ln_b, L3_ffn_fc2_w, L3_ffn_fc2_b):
    import jax
    import jax.numpy as jnp

    def _L0_tok_ref(x, W, class_emb, pos_emb):
        import jax, jax.numpy as jnp
        import numpy as np
        P = 16
        D = 192

        def _patchify(x):
            B, H, W_, C = x.shape
            gh, gw = (H // P, W_ // P)
            x = x.reshape(B, gh, P, gw, P, C)
            x = x.transpose(0, 1, 3, 2, 4, 5)
            return x.reshape(B, gh * gw, P * P * C)
        B = x.shape[0]
        patches = _patchify(x)
        proj = jnp.einsum('bnk,kd->bnd', patches, W)
        cls = jnp.broadcast_to(class_emb, (B, 1, D))
        tokens = jnp.concatenate((cls, proj), axis=1)
        return tokens + pos_emb

    def _L0_attn_ref(x, g_mamba, w_in, conv_w, conv_b, w_xproj, w_dt, b_dt, A_log, D_skip, w_out, g_moe, w_router, g_exp, w1, w3, w2):
        import jax, jax.numpy as jnp
        import numpy as np
        import math
        D_MODEL = 192
        D_STATE = 16
        D_CONV = 4
        EXPAND = 2
        N_EXP = 8
        TOP_K = 2
        D_INNER = D_MODEL * EXPAND
        D_FF = 4 * D_MODEL
        B_SZ, T_LEN = (2, 256)
        EPS = 1e-06

        def _rms(x, g):
            return x * jax.lax.rsqrt(jnp.mean(x * x, axis=-1, keepdims=True) + EPS) * g
        B, T, _ = x.shape
        residual = x
        h = _rms(x, g_mamba)
        xz = h @ w_in
        x_s, z = jnp.split(xz, 2, axis=-1)
        xpad = jnp.pad(x_s, ((0, 0), (D_CONV - 1, 0), (0, 0)))
        xc = conv_b + sum((xpad[:, k:k + T, :] * conv_w[:, k] for k in range(D_CONV)))
        xc = jax.nn.silu(xc)
        params = xc @ w_xproj
        B_coef = params[..., :D_STATE]
        C_coef = params[..., D_STATE:2 * D_STATE]
        log_dt = params[..., -1:]
        dt = jax.nn.softplus(log_dt @ w_dt + b_dt)
        A = -jnp.exp(A_log)
        dt_e = dt[..., None]
        A_bar = jnp.exp(dt_e * A)
        Bu = dt_e * B_coef[:, :, None, :] * xc[..., None]

        def step(hst, inp):
            Ab, bu, c = inp
            hst = Ab * hst + bu
            return (hst, jnp.einsum('bds,bs->bd', hst, c))
        h0 = jnp.zeros((B, D_INNER, D_STATE), x.dtype)
        _, ys = jax.lax.scan(step, h0, (jnp.swapaxes(A_bar, 0, 1), jnp.swapaxes(Bu, 0, 1), jnp.swapaxes(C_coef, 0, 1)))
        y = jnp.swapaxes(ys, 0, 1)
        y = y + xc * D_skip
        y = y * jax.nn.silu(z)
        x = residual + y @ w_out
        N = B * T
        x_flat = x.reshape(N, D_MODEL)
        h_flat = _rms(x_flat, g_moe)
        scores = h_flat @ w_router
        topk_vals, topk_idx = jax.lax.top_k(scores, TOP_K)
        weights = jax.nn.softmax(topk_vals, axis=-1)
        w_dense = jnp.sum(jax.nn.one_hot(topk_idx, N_EXP, dtype=x.dtype) * weights[..., None], axis=1)
        rms_x = x_flat * jax.lax.rsqrt(jnp.mean(x_flat * x_flat, axis=-1, keepdims=True) + EPS)
        he = rms_x[:, None, :] * g_exp
        a = jnp.einsum('ned,edf->nef', he, w1)
        b = jnp.einsum('ned,edf->nef', he, w3)
        ffn = jnp.einsum('nef,efd->ned', jax.nn.silu(a) * b, w2)
        tok_out = x_flat[:, None, :] + ffn
        out = jnp.einsum('ne,ned->nd', w_dense, tok_out)
        return out.reshape(B, T, D_MODEL)

    def _L0_ffn_ref(x, gate_w, gate_b, w_fc, b_fc, w_proj, b_proj):
        import jax, jax.numpy as jnp
        import numpy as np
        N_EMBD = 192
        HIDDEN = 4 * N_EMBD
        N_EXPERTS = 8
        TOP_K = 2
        B, T, C = x.shape
        E = gate_b.shape[0]
        xf = x.reshape(-1, C)
        scores = xf @ gate_w.T + gate_b
        top_s, top_i = jax.lax.top_k(scores, TOP_K)
        gates = jax.nn.softmax(top_s, axis=-1)
        comb = jnp.sum(jax.nn.one_hot(top_i, E, dtype=xf.dtype) * gates[..., None], axis=1)
        out = jnp.zeros_like(xf)
        for j in range(E):
            h = jax.nn.gelu(xf @ w_fc[j].T + b_fc[j], approximate=True)
            y = h @ w_proj[j].T + b_proj[j]
            out = out + comb[:, j:j + 1] * y
        return out.reshape(B, T, C)

    def _L1_attn_ref(x, theta, W_combine):
        import jax, jax.numpy as jnp
        import numpy as np
        import math
        EMBED_DIM = 192
        NUM_HEADS = 12
        N_QUBITS = 96
        D_K = N_QUBITS // NUM_HEADS
        B, S, _ = x.shape
        xs = x[..., :N_QUBITS]
        q_vecs = jnp.cos(xs) * jnp.cos(theta)
        q = q_vecs.reshape(B, S, NUM_HEADS, D_K).transpose(0, 2, 1, 3)
        scores = jnp.einsum('bhsd,bhtd->bhst', q, q) / math.sqrt(D_K)
        probs = jax.nn.softmax(scores, axis=-1)
        attn = jnp.einsum('bhst,bhtd->bhsd', probs, q)
        attn = attn.transpose(0, 2, 1, 3).reshape(B, S, N_QUBITS)
        return attn @ W_combine.T

    def _L1_ffn_ref(x, ln_w, w_router, wi, wo):
        import jax, jax.numpy as jnp
        import numpy as np
        B, S, D, F, E = (8, 512, 192, 768, 16)
        CAP = 64
        EPS = 1e-06

        def _switch_moe_block(x, ln_w, w_router, wi, wo):
            var = jnp.mean(jnp.square(x.astype(jnp.float32)), axis=-1, keepdims=True)
            normed = (x * jax.lax.rsqrt(var + EPS)).astype(x.dtype) * ln_w
            logits = jnp.einsum('bsd,de->bse', normed.astype(jnp.float32), w_router.astype(jnp.float32))
            probs = jax.nn.softmax(logits, axis=-1)
            expert_idx = jnp.argmax(probs, axis=-1)
            onehot = jax.nn.one_hot(expert_idx, E, dtype=jnp.float32)
            priority = jnp.cumsum(onehot, axis=1)
            keep = onehot * (priority <= CAP)
            pos = (priority - 1.0).astype(jnp.int32)
            dispatch = keep[..., None] * jax.nn.one_hot(pos, CAP, dtype=jnp.float32)
            expert_in = jnp.einsum('bsec,bsd->becd', dispatch, normed)
            h = jax.nn.relu(jnp.einsum('becd,edf->becf', expert_in, wi))
            expert_out = jnp.einsum('becf,efd->becd', h, wo)
            combined = jnp.einsum('bsec,becd->bsd', dispatch, expert_out)
            routed = jnp.sum(dispatch, axis=(2, 3)) > 0
            next_states = jnp.where(routed[..., None], combined.astype(x.dtype), normed)
            router_prob = jnp.max(probs, axis=-1, keepdims=True).astype(x.dtype)
            return x + router_prob * next_states
        return _switch_moe_block(x, ln_w, w_router, wi, wo)

    def _L2_attn_ref(x, norm1_w, norm2_w, wq, wk, wv, wo, bo, u_param, v_param, w_pos, w1, b1, w2, b2):
        import jax, jax.numpy as jnp
        import numpy as np
        import math
        B, L, D = (2, 512, 192)
        H, DK = (8, 64)
        DV = D // H
        N_POS = 32
        DFF = 2 * D
        EPS = 1e-05

        def _rel_basis(l: int, n: int) -> jnp.ndarray:
            pos = jnp.arange(l)
            distance = pos[None, :] - pos[:, None]
            pow_rate = jnp.exp(jnp.log(jnp.float32((l + 1) / 2.0)) / (n // 2))
            center_widths = pow_rate ** jnp.arange(1, n // 2 + 1, dtype=jnp.float32)
            d = distance[:, :, None].astype(jnp.float32)
            unsigned = (jnp.abs(d) <= center_widths).astype(jnp.float32)
            signed = jnp.sign(d) * unsigned
            return jnp.concatenate([unsigned, signed], axis=-1)

        def _rmsnorm(x, w):
            norm = jnp.mean(x * x, axis=-1, keepdims=True)
            return x * jax.lax.rsqrt(norm + EPS) * w
        b, l, _ = x.shape
        skip = x
        h1 = _rmsnorm(x, norm1_w)
        q = (h1 @ wq).reshape(b, l, H, DK)
        k = (h1 @ wk).reshape(b, l, H, DK)
        v = (h1 @ wv).reshape(b, l, H, DV)
        basis = _rel_basis(l, N_POS)
        scale = 1.0 / math.sqrt(DK)
        qw = jnp.einsum('bihd,hdn->bihn', q, w_pos)
        qr = jnp.einsum('bihn,ijn->bhij', qw, basis)
        uk = jnp.einsum('hd,bjhd->bhj', u_param, k)[:, :, None, :]
        vw = jnp.einsum('hd,hdn->hn', v_param, w_pos)
        vr = jnp.einsum('hn,ijn->hij', vw, basis)[None]
        bias = (qr + uk + vr) * scale
        scores = jnp.einsum('bihd,bjhd->bhij', q, k) * scale + bias
        attn = jax.nn.softmax(scores, axis=-1)
        out = jnp.einsum('bhij,bjhd->bihd', attn, v)
        out = out.reshape(b, l, H * DV) @ wo + bo
        x = out + skip
        skip = x
        h2 = _rmsnorm(x, norm2_w)
        h2 = jax.nn.gelu(h2 @ w1 + b1, approximate=False) @ w2 + b2
        return h2 + skip

    def _L2_ffn_ref(x, w_fc, w_proj, w_gate):
        import jax, jax.numpy as jnp
        import numpy as np
        B, T, C = (2, 256, 192)
        H, NE, K = (768, 8, 2)
        router_logits = jnp.einsum('btc,ce->bte', x, w_gate)
        router_probs = jax.nn.softmax(router_logits, axis=-1)
        top_p, top_i = jax.lax.top_k(router_probs, K)
        top_p = top_p / jnp.sum(top_p, axis=-1, keepdims=True)
        wf = w_fc.reshape(C, H, NE)
        h_all = jnp.einsum('btc,che->bthe', x, wf)
        h = jnp.take_along_axis(h_all, top_i[:, :, None, :], axis=-1)
        h = jax.nn.gelu(h, approximate=True)
        wp = w_proj.reshape(H, C, NE)
        o_all = jnp.einsum('bthk,hce->btcke', h, wp)
        o = jnp.take_along_axis(o_all, top_i[:, :, None, :, None], axis=-1)[..., 0]
        o = jnp.einsum('btck,btk->btc', o, top_p)
        return o

    def _L3_attn_ref(x_q, w_qkv, b_qkv, w_out, b_out):
        import jax, jax.numpy as jnp
        import numpy as np
        EMBED_DIM = 192
        NUM_HEADS = 12
        HEAD_DIM = EMBED_DIM // NUM_HEADS
        SCALING = HEAD_DIM ** (-0.5)
        B, S = (2, 512)
        b_sz, s_len, _ = x_q.shape
        qkv = x_q @ w_qkv.T + b_qkv
        qkv = qkv.reshape(b_sz, s_len, 3, NUM_HEADS, HEAD_DIM)
        q = qkv[:, :, 0].transpose(0, 2, 1, 3) * SCALING
        k = qkv[:, :, 1].transpose(0, 2, 1, 3)
        v = qkv[:, :, 2].transpose(0, 2, 1, 3)
        attn = jnp.einsum('bhsd,bhtd->bhst', q, k)
        attn = jax.nn.softmax(attn.astype(jnp.float32), axis=-1).astype(attn.dtype)
        out = jnp.einsum('bhst,bhtd->bhsd', attn, v)
        out = out.transpose(0, 2, 1, 3).reshape(b_sz, s_len, EMBED_DIM)
        return out @ w_out.T + b_out

    def _L3_ffn_ref(x, gate_w, gate_b, fc1_w, fc1_b, ln_w, ln_b, fc2_w, fc2_b):
        import jax, jax.numpy as jnp
        import numpy as np
        SEQ, BATCH, EMBED = (256, 2, 192)
        E = 16
        FFN_H = 384
        K_SHARED = 1
        K_ROUTE = 3
        LN_EPS = 1e-05
        NEG_INF = -1000000000.0
        S, B, D = x.shape
        T = S * B
        xf = x.reshape(T, D)
        scores = xf @ gate_w + gate_b
        scores = scores.at[:, :K_SHARED].set(NEG_INF)
        probs = jax.nn.softmax(scores, axis=-1)
        topv, topi = jax.lax.top_k(probs, K_ROUTE)
        combine = jnp.zeros((T, E), xf.dtype)
        combine = combine.at[jnp.arange(T)[:, None], topi].add(topv)
        combine = combine.at[:, :K_SHARED].add(1.0)
        h = jnp.einsum('td,edh->eth', xf, fc1_w) + fc1_b[:, None, :]
        h = jax.nn.gelu(h, approximate=False)
        mu = h.mean(-1, keepdims=True)
        var = h.var(-1, keepdims=True)
        h = (h - mu) * jax.lax.rsqrt(var + LN_EPS) * ln_w[:, None, :] + ln_b[:, None, :]
        y = jnp.einsum('eth,ehd->etd', h, fc2_w) + fc2_b[:, None, :]
        out = jnp.einsum('te,etd->td', combine, y)
        return out.reshape(S, B, D)
    h = _L0_tok_ref(x, L0_tok_W, L0_tok_class_emb, L0_tok_pos_emb)
    h = h + _L0_attn_ref(_layernorm(h, axis=-1), L0_attn_g_mamba, L0_attn_w_in, L0_attn_conv_w, L0_attn_conv_b, L0_attn_w_xproj, L0_attn_w_dt, L0_attn_b_dt, L0_attn_A_log, L0_attn_D_skip, L0_attn_w_out, L0_attn_g_moe, L0_attn_w_router, L0_attn_g_exp, L0_attn_w1, L0_attn_w3, L0_attn_w2)
    h = h + _L0_ffn_ref(_layernorm(h, axis=-1), L0_ffn_gate_w, L0_ffn_gate_b, L0_ffn_w_fc, L0_ffn_b_fc, L0_ffn_w_proj, L0_ffn_b_proj)
    h = h + _L1_attn_ref(_layernorm(h, axis=-1), L1_attn_theta, L1_attn_W_combine)
    h = h + _L1_ffn_ref(_layernorm(h, axis=-1), L1_ffn_ln_w, L1_ffn_w_router, L1_ffn_wi, L1_ffn_wo)
    h = h + _L2_attn_ref(_layernorm(h, axis=-1), L2_attn_norm1_w, L2_attn_norm2_w, L2_attn_wq, L2_attn_wk, L2_attn_wv, L2_attn_wo, L2_attn_bo, L2_attn_u_param, L2_attn_v_param, L2_attn_w_pos, L2_attn_w1, L2_attn_b1, L2_attn_w2, L2_attn_b2)
    h = h + _L2_ffn_ref(_layernorm(h, axis=-1), L2_ffn_w_fc, L2_ffn_w_proj, L2_ffn_w_gate)
    h = h + _L3_attn_ref(_layernorm(h, axis=-1), L3_attn_w_qkv, L3_attn_b_qkv, L3_attn_w_out, L3_attn_b_out)
    h = h + _L3_ffn_ref(_layernorm(h, axis=-1), L3_ffn_gate_w, L3_ffn_gate_b, L3_ffn_fc1_w, L3_ffn_fc1_b, L3_ffn_ln_w, L3_ffn_ln_b, L3_ffn_fc2_w, L3_ffn_fc2_b)
    return h

_drawn_inputs = setup_inputs


def setup_inputs(seed=0):
    import zlib

    import numpy as np

    out = dict(_drawn_inputs(seed))
    spreads = {'L0_tok_class_emb': (0.0, 0.1),
     'L0_attn_g_mamba': (1.0, 0.6),
     'L0_attn_conv_b': (0.0, 0.8),
     'L0_attn_b_dt': (-6.907755374908447, 0.6),
     'L0_attn_D_skip': (1.0, 0.6),
     'L0_attn_g_moe': (1.0, 0.6),
     'L0_attn_g_exp': (1.0, 0.6),
     'L0_ffn_gate_b': (0.0, 0.444),
     'L0_ffn_b_fc': (0.0, 2.0),
     'L0_ffn_b_proj': (0.0, 0.719),
     'L1_ffn_ln_w': (1.0, 0.6),
     'L2_attn_norm1_w': (1.0, 0.6),
     'L2_attn_norm2_w': (1.0, 0.6),
     'L2_attn_bo': (0.0, 1.008),
     'L2_attn_b1': (0.0, 0.8),
     'L2_attn_b2': (0.0, 0.974),
     'L3_attn_b_qkv': (0.0, 1.007),
     'L3_attn_b_out': (0.0, 1.129),
     'L3_ffn_gate_b': (0.0, 2.0),
     'L3_ffn_fc1_b': (0.0, 0.53),
     'L3_ffn_ln_w': (1.0, 0.6),
     'L3_ffn_ln_b': (0.0, 2.0),
     'L3_ffn_fc2_b': (0.0, 1.039)}
    factors = {'L0_attn_w_in': 8.0,
     'L0_attn_conv_w': 8.0,
     'L0_attn_w_xproj': 8.0,
     'L0_attn_w_dt': 8.0,
     'L0_attn_A_log': 8.0,
     'L0_attn_w_out': 8.0,
     'L0_attn_w_router': 5.413,
     'L0_attn_w1': 4.729,
     'L0_attn_w3': 4.699,
     'L0_attn_w2': 4.515,
     'L2_attn_wq': 8.0,
     'L2_attn_wk': 8.0,
     'L2_attn_wv': 6.544,
     'L2_attn_wo': 6.347,
     'L2_attn_u_param': 8.0,
     'L2_attn_v_param': 58.116,
     'L2_attn_w_pos': 8.0,
     'L2_attn_w1': 3.516,
     'L2_attn_w2': 3.383,
     'L2_ffn_w_fc': 8.0,
     'L2_ffn_w_proj': 8.0,
     'L2_ffn_w_gate': 8.0,
     'L3_ffn_gate_w': 11.811,
     'L0_ffn_w_fc': 5.176,
     'L1_ffn_w_router': 3.583,
     'L1_ffn_wi': 4.218,
     'L1_ffn_wo': 3.604,
     'L3_attn_w_qkv': 3.23}
    for name, (base, spread) in spreads.items():
        noise = np.random.default_rng([zlib.crc32(name.encode()), seed]).standard_normal(out[name].shape)
        drawn = base * np.exp(spread * noise) if base else spread * noise
        out[name] = jnp.asarray(drawn.astype(out[name].dtype))
    for name, factor in factors.items():
        out[name] = (out[name] * factor).astype(out[name].dtype)
    return out
```

```python
from contextlib import ExitStack

import numpy as np

import concourse.bass as bass
from concourse import mybir

F32 = mybir.dt.float32
ALU = mybir.AluOpType
ACT = mybir.ActivationFunctionType
AX = mybir.AxisListType

B, T, D = 16, 37, 192
N = B * T
P = 128
NT = (N + P - 1) // P
ROWS = [min(P, N - P * t) for t in range(NT)]
FULL = sum(r == P for r in ROWS)
LASTROWS = ROWS[-1]
NPAD = NT * P
HF = N // 2
KD = D // 2
PATCH = 768
KP = PATCH // P

DI, DS, DCONV = 384, 16, 4
NC_I = DI // P
FF = 768
NCH = FF // P
FH = 384
NFH = FH // P
NEG = -1e30
ARENA, LATE = 28000, 19848

PAIRS = B // 2
R2 = 64 + T
EXPERTS = [8, 8, 16, 8, 16]
QH = 12
LH, LDK, LDV = 8, 64, 24
NPOS = 32
NREL = 2 * T - 1

CONSTS = ["ident", "tok_onehot", "rev_iota", "head_mask12", "head_mask8", "khead12", "khead24", "rel_basis"]


def build(nc, io, out):
    with ExitStack() as ctx:
        def sb(name, shape):
            return ctx.enter_context(nc.sbuf_tensor(name, shape, F32))

        sems = {}

        def sem(name):
            if name not in sems:
                sems[name] = ctx.enter_context(nc.semaphore(name))
            return sems[name]

        X = sb("X", [P, NT, D])
        XN = sb("XN", [P, NT, D])
        XR = sb("XR", [P, NT, D])
        X2 = sb("X2", [P, NT, D])
        xT = sb("xT", [KD + 1, 2, N])
        xTg = sb("xTg", [KD, 2, 2, N])
        hT = sb("hT", [P, NCH, N])
        SIL = sb("SIL", [P, 2, N])
        WU = sb("WU", [KD + 1, 2, 2, 2 * FF])
        WD = sb("WD", [P, 2, NCH, D])
        stats = sb("stats", [P, NT, 6])
        meanvar = sb("meanvar", [P, NT, 2])
        var_eps = sb("var_eps", [P, NT])
        meansq = sb("meansq", [P, NT])
        rstd = sb("rstd", [P, NT])
        minus_half = sb("minus_half", [P, NT])
        ident = sb("ident", [P, P])
        arena = sb("arena", [P, ARENA])

        SC = sb("SC", [P, NT, 16])
        W1_ = sb("gate_work", [P, NT, 16])
        EQ = sb("gate_eq", [P, NT, 16])
        OH = sb("gate_onehot", [P, 3, NT, 16])
        MX = sb("gate_max", [P, 4, NT])
        TOPV = sb("gate_top", [P, 6, NT])
        COMB = sb("COMB", [P, NT, 16])
        CT = sb("combT", [16, N])
        rev = sb("rev", [P, 16])

        PH = ctx.enter_context(nc.psum_tensor("PH", [P, 4, 512], F32))
        PY = ctx.enter_context(nc.psum_tensor("PY", [P, 3, 512], F32))
        PG = ctx.enter_context(nc.psum_tensor("PG", [P, 512], F32))
        wide = [PH[:, 2 * c:2 * c + 2, :].rearrange("p a b -> p (a b)") for c in range(2)]

        def halves(buf, rows=P):
            return PH[0:rows, 2 * buf:2 * buf + 2, 0:HF]

        def two(ap):
            return ap.rearrange("p (h n) -> p h n", h=2)

        def ytile(t):
            return PY[0:ROWS[t], t // 2, (t % 2) * D:(t % 2) * D + D]

        def per_tile_groups(buf):
            full = buf[:, 0:FULL, :].rearrange("p (a b) d -> p a (b d)", b=2)
            return [(PY[:, 0:FULL // 2, 0:2 * D], full), (ytile(NT - 1), buf[0:LASTROWS, NT - 1, :])]

        loads = []

        late, early = [LATE], [24400]

        def place(name, shape, group):
            if group == 1:
                return sb(name, shape)
            n = int(np.prod(shape[1:]))
            at = late if group else early
            v = arena[0:shape[0], at[0]:at[0] + n]
            at[0] += n
            if len(shape) == 3:
                v = v.rearrange("p (a b) -> p a b", b=shape[2])
            return v

        def resident(name, shape, src, dst=None, group=0):
            buf = place(name, shape, group)
            loads.append((dst(buf) if dst else buf[:], src, group))
            return buf

        def kt(name, p, k, n):
            return io[name].rearrange("(k p) n -> p k n", p=p)

        def cols(name, p):
            return io[name]

        loads.append((ident[:], io["ident"], 0))
        loads.append((rev[:], io["rev_iota"], 0))
        onehot = resident("tok_onehot_s", [T + 1, NPAD], io["tok_onehot"])
        postab = resident("postab_s", [T + 1, D], io["postab"])
        g_mamba = resident("g_mamba_s", [KD, 2], io["g_mamba"], group=1)
        w_in = resident("w_in_s", [KD, 2, 2 * DI], kt("w_in", KD, 2, 2 * DI), group=0)
        conv_w = resident("conv_w_s", [P, NC_I, DCONV], io["conv_w"], group=1)
        conv_b = resident("conv_b_s", [P, NC_I], io["conv_b"], group=1)
        w_xproj = resident("w_xproj_s", [P, NC_I, 2 * DS + 1], kt("w_xproj", P, NC_I, 33), group=1)
        w_dt = resident("w_dt_s", [2 * DS + 1, DI], io["w_dt"], dst=lambda b: b[2 * DS:2 * DS + 1, :], group=1)
        b_dt = resident("b_dt_s", [P, NC_I], io["b_dt"], group=1)
        A_log = resident("A_log_s", [P, NC_I, DS], io["A_log"], group=1)
        D_skip = resident("D_skip_s", [P, NC_I], io["D_skip"], group=1)
        w_out0 = resident("w_out0_s", [P, NC_I, D], kt("w_out", P, NC_I, D), group=1)
        g_moe = resident("g_moe_s", [KD, 2], io["g_moe"], group=2)
        gate0 = resident("gate0_s", [KD, 2, 8], kt("router0", KD, 2, 8), group=2)
        g_exp = place("g_exp_s", [KD, 9, 2], 2)
        loads.append((g_exp[:, 0:8, :], io["g_exp"], 2))
        gate1 = place("gate1_s", [KD + 1, 2, 8], 2)
        loads.append((gate1[0:KD], kt("gate1", KD, 2, 8), 2))
        loads.append((gate1[KD:KD + 1, 1, :], io["gate1_b"], 2))
        b_fc = resident("b_fc_s", [P, 8 * NCH], io["b_fc"], group=2)
        b_proj = resident("b_proj_s", [8, D], io["b_proj"], group=2)
        theta = resident("theta_s", [96, 1], io["theta"], group=2)
        w_comb = resident("w_comb_s", [96, D], io["w_comb"], group=2)
        mask12 = resident("mask12_s", [3 * T, 3], io["head_mask12"], group=2)
        mask8 = resident("mask8_s", [2 * T, 2], io["head_mask8"], group=2)
        khead12 = resident("khead12_s", [96, 12], io["khead12"], group=2)
        khead24 = resident("khead24_s", [96, 6], io["khead24"], group=2)
        ln_w1 = resident("ln_w1_s", [KD, 2], io["ln_w1"], group=2)
        gate2 = resident("gate2_s", [KD, 2, 16], kt("router2", KD, 2, 16), group=2)
        norm1_w = resident("norm1_w_s", [KD, 2], io["norm1_w"], group=2)
        norm2_w = resident("norm2_w_s", [KD, 2], io["norm2_w"], group=2)
        wq = resident("wq_s", [KD, 2, LH * LDK], kt("wq", KD, 2, 512), group=2)
        wk = resident("wk_s", [KD, 2, LH * LDK], kt("wk", KD, 2, 512), group=2)
        wv = resident("wv_s", [KD, 2, D], kt("wv", KD, 2, D), group=2)
        wo = resident("wo_s", [KD, 2, D], kt("wo", KD, 2, D), group=2)
        bo = resident("bo_s", [1, D], io["bo"], group=2)
        u_par = resident("u_par_s", [P, 4], io["u_param"], group=2)
        v_par = resident("v_par_s", [P, 4], io["v_param"], group=2)
        wposT = resident("wposT_s", [NPOS, LH * LDK], io["w_posT"], group=2)
        basis = resident("basis_s", [NPOS, NREL], io["rel_basis"], group=2)
        fw1 = resident("fw1_s", [KD, 2, FH], kt("L2w1", KD, 2, FH), group=2)
        fb1 = resident("fb1_s", [P, NFH], io["L2b1"], group=2)
        fw2 = resident("fw2_s", [P, NFH, D], kt("L2w2", P, NFH, D), group=2)
        fb2 = resident("fb2_s", [1, D], io["L2b2"], group=2)
        gate3 = resident("gate3_s", [KD, 2, 8], kt("gate3", KD, 2, 8), group=2)
        wqkv = resident("wqkv_s", [KD, 2, 3 * D], kt("wqkv", KD, 2, 3 * D), group=2)
        bqk = resident("bqk_s", [KD, 4], io["bqk"], group=2)
        bv = resident("bv_s", [1, D], io["bv"], group=2)
        wo3 = resident("wo3_s", [KD, 2, D], kt("wo3", KD, 2, D), group=2)
        bo3 = resident("bo3_s", [1, D], io["bo3"], group=2)
        gate4 = place("gate4_s", [KD + 1, 2, 16], 2)
        loads.append((gate4[0:KD], kt("gate4", KD, 2, 16), 2))
        loads.append((gate4[KD:KD + 1, 1, :], io["gate4_b"], 2))
        lnw4 = resident("lnw4_s", [P, 16 * NFH], io["lnw4"], group=2)
        lnb4 = resident("lnb4_s", [P, 16 * NFH], io["lnb4"], group=2)
        b_fc2 = resident("b_fc2_s", [16, D], io["fc2_b"], group=2)
        ones_row = sb("ones_row", [1, P])
        NLOAD = [16 * sum(g == k for _, _, g in loads) for k in range(3)]

        def view(at, shape, rows=P):
            n = int(np.prod(shape))
            v = arena[0:rows, at:at + n]
            if len(shape) == 2:
                v = v.rearrange("p (a b) -> p a b", b=shape[1])
            elif len(shape) == 3:
                v = v.rearrange("p (a b c) -> p a b c", b=shape[1], c=shape[2])
            return v, at + n

        patches, a_ = view(0, [KP, NPAD])
        tokW, a_ = view(a_, [KP, D])
        BC, a_ = view(0, [2 * DS, N])
        DT, a_ = view(a_, [NC_I, N])
        DTX, a_ = view(a_, [NC_I, N])
        XC = hT[:, 0:NC_I, :]
        SZ = hT[:, NC_I:2 * NC_I, :]
        AN, a_ = view(a_, [NC_I, DS])
        YT, a_ = view(a_, [NC_I, N])
        PAR = xTg[0:33, 0, 0, :]
        assert a_ <= ARENA
        XS, a0 = view(0, [NC_I, B, T + 3])
        XCP, a0 = view(a0, [NC_I, N])
        SP_E, a1 = view(0, [NC_I, N])
        SP_U, a1 = view(a1, [NC_I, N])
        SP_L, a1 = view(a1, [NC_I, N])
        SP_R, a1 = view(a1, [NC_I, N])
        SP_D, a1 = view(a1, [NC_I, N])
        SP_Q, a1 = view(a1, [NC_I, N])
        assert a1 <= 2 * DS * N
        AB = SIL
        BU, a_ = view(a_, [2, N])
        HS, a_ = view(a_, [2, N])
        HC, a_ = view(a_, [2, N])
        assert a_ <= ARENA

        QT, b_ = view(0, [4, NPAD])
        KB, b_ = view(b_, [2, B, 6 * T])
        KM, _ = view(4 * NPAD, [4, B, 2 * T])
        VB, b_ = view(b_, [B, D])
        PM, b_ = view(b_, [2, QH * T])
        PTS, b_ = view(b_, [2, 512])
        OSB, b_ = view(b_, [2, D])
        OT, b_ = view(b_, [2, N])
        amax, b_ = view(b_, [2, QH])
        asum, b_ = view(b_, [2, QH])
        arinv, b_ = view(b_, [2, QH])
        CX, b2 = view(b_, [3, N], rows=96)
        QV, b2 = view(b2, [3, N], rows=P)
        cth = sb("cth", [96, 4])
        assert b2 <= LATE and late[0] <= ARENA, (b2, late)
        QV8, c_ = view(4 * NPAD + 8 * N, [4, N])
        assert c_ == 4 * NPAD + 2 * B * 6 * T
        WR, _ = view(c_, [4, 2 * NREL])
        RSB = hT.rearrange("p a n -> p (a n)")[:, 0:2 * LH * NREL].rearrange("p (a n) -> p a n", a=2)
        rel_dram = nc.dram_tensor("rel_scratch", (NPAD, LH * NREL), F32, kind="Internal").ap()

        FREE = 1
        COUNTED_FROM_FREE = ["scanned", "y_summed", "m0_silu", "m4_gelu"]
        COUNTED_FROM_FREE += [f"m{j}_{what}" for j in range(5) for what in ("hid", "out", "down")]

        block = ctx.enter_context(nc.Block())

        chain = {"v": 0}

        def link(v, ins):
            chain["v"] += 1
            ins.then_inc(sem("v_chain"), 1)
            v.wait_ge(sem("v_chain"), chain["v"])

        def norm_v(v, n, src, dst, eps, centred):
            for t in range(NT):
                last = v.bn_stats(stats[:, t, :], src[:, t, :])
            link(v, last)
            for t in range(NT):
                last = v.bn_aggr(meanvar[:, t, :], stats[:, t, :])
            link(v, last)
            if centred:
                v.tensor_scalar(var_eps[:], meanvar[:, :, 1], eps, None, ALU.add).then_inc(sem("var_ready"), 1)
            else:
                link(v, v.tensor_tensor(meansq[:], meanvar[:, :, 0], meanvar[:, :, 0], ALU.mult))
                v.scalar_tensor_tensor(var_eps[:], meansq[:], eps, meanvar[:, :, 1], ALU.add, ALU.add)\
                    .then_inc(sem("var_ready"), 1)
            v.wait_ge(sem("rstd_ready"), n + 1)
            for t in range(NT):
                if centred:
                    last = v.tensor_scalar(dst[:, t, :], src[:, t, :], meanvar[:, t, 0:1], rstd[:, t:t + 1],
                                           ALU.subtract, ALU.mult)
                else:
                    last = v.tensor_scalar(dst[:, t, :], src[:, t, :], rstd[:, t:t + 1], None, ALU.mult)
            last.then_inc(sem("normed"), 1)

        def norm_pool(p, n):
            p.wait_ge(sem("var_ready"), n + 1)
            p.tensor_tensor(rstd[:], var_eps[:], minus_half[:], ALU.pow).then_inc(sem("rstd_ready"), 1)

        def turn_pe(pe, m, n, src):
            pe.wait_ge(sem("normed"), n + 1)
            for c in range(2):
                for t in range(NT):
                    last = pe.transpose(wide[c][0:KD, t * P:t * P + ROWS[t]], src[0:ROWS[t], t, c * KD:(c + 1) * KD],
                                        ident[0:ROWS[t], 0:ROWS[t]])
                last.then_inc(sem("turned"), 1)

        def turn_v(v, m, g=None):
            v.wait_ge(sem("turned"), 2 * m + 1)
            if g is None:
                v.tensor_copy(xT[0:KD, 0, :], wide[0][0:KD, 0:N]).then_inc(sem("xT_v"), 1)
            else:
                v.tensor_scalar(xT[0:KD, 0, :], wide[0][0:KD, 0:N], g[:, 0:1], None, ALU.mult).then_inc(sem("xT_v"), 1)

        def turn_act(act, m, g=None):
            act.wait_ge(sem("turned"), 2 * m + 2)
            act.activation(xT[0:KD, 1, :], wide[1][0:KD, 0:N], ACT.Copy,
                           scale=1.0 if g is None else g[:, 1:2]).then_inc(sem("xT_a"), 1)

        def xT_ready(eng, m):
            eng.wait_ge(sem("xT_v"), m + 1)
            eng.wait_ge(sem("xT_a"), m + 1)

        def tokens_pe(pe):
            pe.wait_ge(sem("patches_in"), 16 * 2)
            pe.wait_ge(sem("weights0"), NLOAD[0])
            for t in range(NT):
                o = PY[:, t // 2, (t % 2) * D:(t % 2) * D + D]
                for k in range(KP):
                    pe.matmul(o, patches[:, k, t * P:(t + 1) * P], tokW[:, k, :], start=(k == 0), stop=False,
                              skip_group_check=True)
                last = pe.matmul(o, onehot[:, t * P:(t + 1) * P], postab[:, :], start=False, stop=True,
                                 skip_group_check=True)
            last.then_inc(sem("tokens_ready"), 1)

        def tokens_v(v):
            v.wait_ge(sem("tokens_ready"), 1)
            v.tensor_copy(X[:, 0:FULL, :].rearrange("p (a b) d -> p a (b d)", b=2), PY[:, 0:FULL // 2, 0:2 * D])
            link(v, v.tensor_copy(X[:, NT - 1, :], PY[:, 2, 0:D]))

        def mamba_pe(pe):
            turn_pe(pe, 0, 1, XR)
            xT_ready(pe, 0)
            for q in range(2 * NC_I):
                if q in (2, 3, 4):
                    pe.wait_ge(sem("xs_moved"), q - 1)
                if q == 5:
                    pe.wait_ge(sem("z_moved"), 1)
                for h in range(2):
                    for k in range(2):
                        last = pe.matmul(PH[:, 2 * (q % 2) + h, 0:HF], w_in[:, k, q * P:(q + 1) * P],
                                         xT[0:KD, k, h * HF:(h + 1) * HF], start=(k == 0), stop=(k == 1))
                last.then_inc(sem("xz_ready"), 1)
            pe.wait_ge(sem("z_moved"), 2)
            pe.wait_ge(sem("z_moved"), 3)
            pe.wait_ge(sem("xc_ready"), NC_I)
            for h in range(2):
                for c in range(NC_I):
                    last = pe.matmul(PH[0:33, h, 0:HF], w_xproj[:, c, :], XC[:, c, h * HF:(h + 1) * HF],
                                     start=(c == 0), stop=(c == NC_I - 1))
            last.then_inc(sem("params_ready"), 1)
            pe.wait_ge(sem("params_moved"), 1)
            for c in range(NC_I):
                for h in range(2):
                    o = [PH[:, 2 + h, 0:HF], PH[:, h, 0:HF], PY[:, h, 0:HF]][c]
                    last = pe.matmul(o, w_dt[32:33, c * P:(c + 1) * P], PAR[32:33, h * HF:(h + 1) * HF],
                                     start=True, stop=True)
                last.then_inc(sem("dt_ready"), 1)
            for q in range(2 * DS):
                if q == 0:
                    pe.wait_ge(sem("dt_used"), 2 * NC_I)
                if q >= 2:
                    pe.wait_ge(sem("spread_v" if q % 2 else "spread_a"), (q - 2) // 2 + 1)
                for h in range(2):
                    last = pe.matmul(PH[:, 2 * (q % 2) + h, 0:HF], ident[0:32, q:q + 1].to_broadcast([32, P]),
                                     PAR[0:32, h * HF:(h + 1) * HF], start=True, stop=True)
                last.then_inc(sem("bc_ready"), 1)
            for c in range(NC_I):
                if c == 0:
                    pe.wait_ge(sem("spread_v"), DS)
                    pe.wait_ge(sem("spread_a"), DS)
                if c >= 2:
                    pe.wait_ge(sem("y_gated"), c - 1)
                o = [PH[:, 2 * (c % 2) + h, 0:HF] for h in range(2)]
                pe.wait_ge(sem("xd_ready"), c + 1)
                for h in range(2):
                    pe.matmul(o[h], ident[:, :], YT[:, c, h * HF:(h + 1) * HF], start=True, stop=False,
                              skip_group_check=True)
                with pe.Fori(0, DS // 2) as i:
                    for k in range(2):
                        pe.wait_ge(sem("hc_ready"), i * 2 + (c * DS + k + 1))
                        for h in range(2):
                            last = pe.matmul(o[h], ident[:, :], HC[:, k, h * HF:(h + 1) * HF], start=False, stop=True,
                                             skip_group_check=True)
                        last.then_inc(sem("y_summed"), 1)
            pe.wait_ge(sem("y_gated"), NC_I)
            for t in range(NT):
                for c in range(NC_I):
                    last = pe.matmul(ytile(t), YT[:, c, t * P:t * P + ROWS[t]], w_out0[:, c, :],
                                     start=(c == 0), stop=(c == NC_I - 1), skip_group_check=True)
            last.then_inc(sem("mamba_out"), 1)

        def mamba_v(v):
            v.wait_ge(sem("weights1"), NLOAD[1])
            norm_v(v, 0, X, XN, 1e-5, True)
            link(v, v.memset(XS[:, :, :, 0:3], 0.0))
            v.wait_ge(sem("normed"), 1)
            norm_v(v, 1, XN, XR, 1e-6, False)
            turn_v(v, 0, g_mamba)
            link(v, v.memset(AB[:, :, :], 0.0))
            for c in range(NC_I):
                v.wait_ge(sem("xz_ready"), c + 1)
                v.tensor_copy(XS[:, c, :, 3:].rearrange("p (h b) t -> p h b t", h=2),
                              halves(c % 2).rearrange("p h (b t) -> p h b t", t=T)).then_inc(sem("xs_moved"), 1)
                v.wait_ge(sem("xs_moved"), c + 1)
                xc = XCP[:, c, :].rearrange("p (b t) -> p b t", t=T)
                link(v, v.tensor_scalar(xc, XS[:, c, :, 0:T], conv_w[:, c, 0:1], None, ALU.mult))
                for k in range(1, DCONV):
                    last = v.scalar_tensor_tensor(xc, XS[:, c, :, k:k + T], conv_w[:, c, k:k + 1], xc, ALU.mult, ALU.add)
                    if k < DCONV - 1:
                        link(v, last)
                last.then_inc(sem("conv_ready"), 1)
            v.wait_ge(sem("params_ready"), 1)
            v.tensor_copy(two(PAR), halves(0, 33)).then_inc(sem("params_moved"), 1)
            v.wait_ge(sem("sp_exp"), NC_I)
            v.tensor_scalar(SP_U[:], SP_E[:], 1.0, None, ALU.add).then_inc(sem("sp_u"), 1)
            v.wait_ge(sem("sp_u"), 1)
            link(v, v.tensor_scalar(SP_D[:], SP_U[:], -1.0, None, ALU.add))
            v.wait_ge(sem("sp_ln"), 1)
            v.scalar_tensor_tensor(SP_Q[:], SP_D[:], 0.0, SP_L[:], ALU.is_equal, ALU.add)
            link(v, v.scalar_tensor_tensor(SP_U[:], SP_D[:], 0.0, SP_D[:], ALU.is_equal, ALU.add))
            link(v, v.reciprocal(SP_L[:], SP_U[:]))
            link(v, v.tensor_tensor(SP_U[:], SP_E[:], SP_L[:], ALU.mult))
            link(v, v.tensor_tensor(SP_D[:], SP_U[:], SP_Q[:], ALU.mult))
            link(v, v.tensor_tensor(DT[:], SP_D[:], SP_R[:], ALU.add))
            v.tensor_tensor(DTX[:], DT[:], XC[:], ALU.mult).then_inc(sem("dt_final"), 1)
            v.wait_ge(sem("a_exp"), 1)
            v.tensor_scalar(AN[:], AN[:], -1.0, None, ALU.mult).then_inc(sem("a_ready"), 1)
            for c in range(NC_I):
                v.tensor_scalar(YT[:, c, :], XC[:, c, :], D_skip[:, c:c + 1], None, ALU.mult).then_inc(sem("xd_ready"), 1)
            for q in range(1, 2 * DS, 2):
                v.wait_ge(sem("bc_ready"), q + 1)
                v.tensor_copy(two(BC[:, q, :]), halves(1)).then_inc(sem("spread_v"), 1)
            for c in range(NC_I):
                if c == 0:
                    v.wait_ge(sem("spread_a"), DS)
                    v.wait_ge(sem("spread_v"), DS)
                with v.Fori(0, DS // 2) as i:
                    for k in range(2):
                        q = i * 2 + (c * DS + k)
                        v.wait_ge(sem("ab_ready"), q + 1)
                        v.wait_ge(sem("bu_ready"), q + 1)
                        v.tensor_tensor_scan(HS[:, k, :], AB[:, k, :], BU[:, k, :], 0.0, ALU.mult, ALU.add)\
                            .then_inc(sem("scanned"), 1)
                        v.wait_ge(sem("scanned"), FREE + q + 1)
                        if c > 0 or k > 0:
                            v.wait_ge(sem("y_summed"), FREE + i * 2 + (c * DS + k - 1))
                        else:
                            v.wait_ge(sem("y_summed"), FREE + i * 2)
                        v.tensor_tensor(HC[:, k, :], HS[:, k, :], BC[:, bass.ds(i * 2 + (DS + k), 1), :].rearrange("p a n -> p (a n)"),
                                        ALU.mult).then_inc(sem("hc_ready"), 1)
                v.wait_ge(sem("y_summed"), FREE + (c + 1) * DS)
                v.tensor_tensor(two(YT[:, c, :]), halves(c % 2), two(SZ[:, c, :]), ALU.mult).then_inc(sem("y_gated"), 1)
            v.wait_ge(sem("mamba_out"), 1)
            for ps, xn, x2 in zip([g[0] for g in per_tile_groups(XN)], [g[1] for g in per_tile_groups(XN)],
                                  [g[1] for g in per_tile_groups(X2)]):
                last = v.tensor_tensor(x2, ps, xn, ALU.add)
            link(v, last)

        def mamba_act(act):
            act.wait_ge(sem("weights1"), NLOAD[1])
            turn_act(act, 0, g_mamba)
            act.activation(AN[:], A_log[:], ACT.Exp).then_inc(sem("a_exp"), 1)
            for c in range(NC_I):
                act.wait_ge(sem("xz_ready"), NC_I + c + 1)
                act.activation(two(SZ[:, c, :]), halves((NC_I + c) % 2), ACT.Silu).then_inc(sem("z_moved"), 1)
            for c in range(NC_I):
                act.wait_ge(sem("conv_ready"), c + 1)
                act.activation(XC[:, c, :], XCP[:, c, :], ACT.Silu, bias=conv_b[:, c:c + 1]).then_inc(sem("xc_ready"), 1)
            for c in range(NC_I):
                o = [halves(1), halves(0), PY[:, 0:2, 0:HF]][c]
                act.wait_ge(sem("dt_ready"), c + 1)
                act.activation(two(SP_U[:, c, :]), o, ACT.Abs, bias=b_dt[:, c:c + 1]).then_inc(sem("dt_used"), 1)
                act.activation(two(SP_R[:, c, :]), o, ACT.Relu, bias=b_dt[:, c:c + 1]).then_inc(sem("dt_used"), 1)
            for c in range(NC_I):
                act.wait_ge(sem("dt_used"), 2 * c + 1)
                act.activation(SP_E[:, c, :], SP_U[:, c, :], ACT.Exp, scale=-1.0).then_inc(sem("sp_exp"), 1)
            act.wait_ge(sem("sp_u"), 1)
            act.activation(SP_L[:], SP_U[:], ACT.Ln).then_inc(sem("sp_ln"), 1)
            act.wait_ge(sem("dt_final"), 1)
            for q in range(0, 2 * DS, 2):
                act.wait_ge(sem("bc_ready"), q + 1)
                act.activation(two(BC[:, q, :]), halves(0), ACT.Copy).then_inc(sem("spread_a"), 1)
            act.wait_ge(sem("a_ready"), 1)
            for c in range(NC_I):
                dt = DT[:, c, :].rearrange("p (b t) -> p b t", t=T)[:, :, 1:T]
                with act.Fori(0, DS // 2) as i:
                    for k in range(2):
                        if c > 0 or k > 0:
                            act.wait_ge(sem("scanned"), FREE + i * 2 + (c * DS + k - 1))
                        else:
                            act.wait_ge(sem("scanned"), FREE + i * 2)
                        act.activation(AB[:, k, :].rearrange("p (b t) -> p b t", t=T)[:, :, 1:T], dt, ACT.Exp,
                                       scale=AN[:, c, bass.ds(i * 2 + k, 1)]).then_inc(sem("ab_ready"), 1)

        def mamba_pool(p):
            norm_pool(p, 0)
            norm_pool(p, 1)
            p.wait_ge(sem("spread_a"), DS)
            p.wait_ge(sem("spread_v"), DS)
            for c in range(NC_I):
                with p.Fori(0, DS // 2) as i:
                    for k in range(2):
                        if c > 0 or k > 0:
                            p.wait_ge(sem("scanned"), FREE + i * 2 + (c * DS + k - 1))
                        else:
                            p.wait_ge(sem("scanned"), FREE + i * 2)
                        p.tensor_tensor(BU[:, k, :], DTX[:, c, :],
                                        BC[:, bass.ds(i * 2 + k, 1), :].rearrange("p a n -> p (a n)"),
                                        ALU.mult).then_inc(sem("bu_ready"), 1)

        SOFT_PAIR, SOFT_TOP2, SOFT_TOP1, SHARED_TOP3 = range(4)

        def gate_pe(pe, j, E, w, src, bias):
            for t in range(NT):
                for k in range(2):
                    kk = KD + 1 if bias and k == 1 else KD
                    last = pe.matmul(PG[0:ROWS[t], t * 16:t * 16 + E], src[0:kk, k, t * P:t * P + ROWS[t]],
                                     w[0:kk, k, :], start=(k == 0), stop=(k == 1), skip_group_check=True)
            last.then_inc(sem("logits"), 1)

        def gate_act(act, j, kind):
            act.wait_ge(sem("gate_shifted"), j + 1)
            if kind == SOFT_PAIR:
                act.activation(TOPV[:, 1, :], TOPV[:, 0, :], ACT.Exp).then_inc(sem("gate_exp"), 1)
            else:
                act.activation(W1_[:], W1_[:], ACT.Exp).then_inc(sem("gate_exp"), 1)

        def gate_v(v, j, E, kind):
            pg = PG[:, 0:16 * NT].rearrange("p (t e) -> p t e", e=16)
            sc, wk_, eq = SC[:, :, 0:E], W1_[:, :, 0:E], EQ[:, :, 0:E]

            def over(ap):
                return ap.unsqueeze(2).to_broadcast([P, NT, E])

            v.wait_ge(sem("logits"), j + 1)
            v.tensor_copy(SC[:, 0:FULL, 0:E], pg[:, 0:FULL, 0:E])
            link(v, v.tensor_copy(SC[0:LASTROWS, NT - 1, 0:E], pg[0:LASTROWS, NT - 1, 0:E]))
            if kind == SHARED_TOP3:
                link(v, v.memset(SC[:, :, 0:1], -1e9))
            if kind == SOFT_PAIR:
                link(v, v.tensor_copy(wk_, sc))
            else:
                link(v, v.tensor_reduce(MX[:, 3, :], sc, AX.X, ALU.max))
                v.tensor_tensor(wk_, sc, over(MX[:, 3, :]), ALU.subtract).then_inc(sem("gate_shifted"), 1)
                v.wait_ge(sem("gate_exp"), j + 1)
                link(v, v.tensor_reduce(TOPV[:, 0, :], wk_, AX.X, ALU.add))
                link(v, v.reciprocal(TOPV[:, 1, :], TOPV[:, 0, :]))
                link(v, v.tensor_tensor(wk_, wk_, over(TOPV[:, 1, :]), ALU.mult))
            picks = {SOFT_PAIR: 2, SOFT_TOP2: 2, SOFT_TOP1: 1, SHARED_TOP3: 3}[kind]
            for r in range(picks):
                oh = OH[:, r, :, 0:E]
                link(v, v.tensor_reduce(MX[:, r, :], wk_, AX.X, ALU.max))
                link(v, v.tensor_tensor(eq, wk_, over(MX[:, r, :]), ALU.is_equal))
                link(v, v.tensor_tensor(eq, eq, rev[:, 0:E].unsqueeze(1).to_broadcast([P, NT, E]), ALU.mult))
                link(v, v.tensor_reduce(MX[:, 3, :], eq, AX.X, ALU.max))
                link(v, v.tensor_tensor(oh, eq, over(MX[:, 3, :]), ALU.is_equal))
                if r < picks - 1:
                    link(v, v.scalar_tensor_tensor(wk_, oh, NEG, wk_, ALU.mult, ALU.add))
            weight = [MX[:, r, :] for r in range(picks)]
            if kind == SOFT_PAIR:
                v.tensor_tensor(TOPV[:, 0, :], MX[:, 1, :], MX[:, 0, :], ALU.subtract).then_inc(sem("gate_shifted"), 1)
                v.wait_ge(sem("gate_exp"), j + 1)
                link(v, v.tensor_scalar(TOPV[:, 2, :], TOPV[:, 1, :], 1.0, None, ALU.add))
                link(v, v.reciprocal(TOPV[:, 3, :], TOPV[:, 2, :]))
                link(v, v.tensor_tensor(TOPV[:, 4, :], TOPV[:, 1, :], TOPV[:, 3, :], ALU.mult))
                weight = [TOPV[:, 3, :], TOPV[:, 4, :]]
            if kind == SOFT_TOP2:
                link(v, v.tensor_tensor(TOPV[:, 2, :], MX[:, 0, :], MX[:, 1, :], ALU.add))
                link(v, v.reciprocal(TOPV[:, 3, :], TOPV[:, 2, :]))
                v.tensor_tensor(TOPV[:, 4, :], MX[:, 0, :], TOPV[:, 3, :], ALU.mult)
                link(v, v.tensor_tensor(TOPV[:, 5, :], MX[:, 1, :], TOPV[:, 3, :], ALU.mult))
                weight = [TOPV[:, 4, :], TOPV[:, 5, :]]
            comb = COMB[:, :, 0:E]
            last = v.tensor_tensor(comb, OH[:, 0, :, 0:E], over(weight[0]), ALU.mult)
            for r in range(1, picks):
                link(v, last)
                link(v, v.tensor_tensor(eq, OH[:, r, :, 0:E], over(weight[r]), ALU.mult))
                last = v.tensor_tensor(comb, comb, eq, ALU.add)
            if kind == SHARED_TOP3:
                link(v, last)
                last = v.tensor_scalar(COMB[:, :, 0:1], COMB[:, :, 0:1], 1.0, None, ALU.add)
            last.then_inc(sem("comb_ready"), 1)
            v.wait_ge(sem("comb_ready"), j + 1)

        def outbias_pe(pe, n, j, E, bias):
            pe.wait_ge(sem("comb_ready"), j + 1)
            for t in range(NT):
                last = pe.transpose(wide[1][0:E, t * P:t * P + ROWS[t]], COMB[0:ROWS[t], t, 0:E],
                                    ident[0:ROWS[t], 0:ROWS[t]])
            last.then_inc(sem("comb_turned"), 1)
            pe.wait_ge(sem("combT_ready"), n + 1)
            for t in range(NT):
                last = pe.matmul(ytile(t), CT[0:E, t * P:t * P + ROWS[t]], bias[0:E, :], start=True, stop=True,
                                 skip_group_check=True)
            last.then_inc(sem("outbias"), 1)
            pe.wait_ge(sem("bias_added"), n + 1)

        def add_to(v, dst, other):
            for (ps, o), (_, d) in zip(per_tile_groups(other), per_tile_groups(dst)):
                last = v.tensor_tensor(d, ps, o, ALU.add)
            return last

        def outbias_v(v, n, E):
            v.wait_ge(sem("comb_turned"), n + 1)
            v.tensor_copy(CT[0:E, :], wide[1][0:E, 0:N]).then_inc(sem("combT_ready"), 1)
            v.wait_ge(sem("outbias"), n + 1)
            add_to(v, X, X).then_inc(sem("bias_added"), 1)
            v.wait_ge(sem("bias_added"), n + 1)

        def up_mm(pe, buf, k, at, src, bank_rows=P):
            for h in range(2):
                for c in range(2):
                    last = pe.matmul(PH[:, 2 * buf + h, 0:HF], WU[0:KD, k, c, at:at + P],
                                     src[0:KD, c, h * HF:(h + 1) * HF], start=(c == 0), stop=(c == 1))
            return last

        def down_mm(pe, j, k, e, chunks, ready):
            pe.wait_ge(sem(f"m{j}_wd{k}"), (e - k) * 8 + 16)
            pe.wait_ge(sem(f"m{j}_out"), FREE + e)
            for m in range(chunks):
                pe.wait_ge(sem(f"m{j}_hid"), FREE + ready(m))
                for t in range(NT):
                    last = pe.matmul(ytile(t), hT[:, m, t * P:t * P + ROWS[t]], WD[:, k, m, :],
                                     start=(m == 0 and t % 2 == 0), stop=(m == chunks - 1), skip_group_check=True)
            last.then_inc(sem(f"m{j}_down"), 1)

        def experts_load(sp, j, E, chunks, ups):
            def load(e, k):
                for name, at in ups:
                    n = io[name].shape[2]
                    sp.dma_start(WU[0:KD, k, :, at:at + n],
                                 io[name][bass.ds(e, 1)].rearrange("e (k p) n -> p (e k) n", p=KD))\
                        .then_inc(sem(f"m{j}_wu{k}"), 16)
                if j == 4:
                    sp.dma_start(WU[KD:KD + 1, k, 1, 0:FH], io["m4_up_b"][bass.ds(e, 1), :]).then_inc(sem(f"m{j}_wu{k}"), 16)
                sp.dma_start(WD[:, k, 0:chunks, :],
                             io[f"m{j}_down"][bass.ds(e, 1)].rearrange("e (k p) n -> p (e k) n", p=P))\
                    .then_inc(sem(f"m{j}_wd{k}"), 16)
            if j > 0:
                sp.wait_ge(sem(f"m{j - 1}_down"), FREE + EXPERTS[j - 1])
            for k in range(2):
                load(k, k)
            with sp.Fori(1, E // 2) as i:
                for k in range(2):
                    sp.wait_ge(sem(f"m{j}_down"), FREE + i * 2 + (k - 1))
                    load(i * 2 + k, k)

        def experts_pe(pe, j, E):
            with pe.Fori(0, E // 2) as i:
                for k in range(2):
                    e = i * 2 + k
                    pe.wait_ge(sem(f"m{j}_wu{k}"), i * 16 + 16)
                    for m in range(NCH):
                        pe.wait_ge(sem(f"m{j}_hid"), FREE + i * (2 * NCH) + (k * NCH + max(m - 1, 0)))
                        up_mm(pe, m % 2, k, m * P, xT).then_inc(sem(f"m{j}_up"), 1)
                    down_mm(pe, j, k, e, NCH, lambda m: i * (2 * NCH) + (k * NCH + m + 1))

        def experts_act(act, j, E, func, bias=None):
            with act.Fori(0, E // 2) as i:
                for k in range(2):
                    for m in range(NCH):
                        act.wait_ge(sem(f"m{j}_up"), i * (2 * NCH) + (k * NCH + m + 1))
                        b = 0.0 if bias is None else bias[:, bass.ds(i * (2 * NCH) + (k * NCH + m), 1)]
                        act.activation(two(hT[:, m, :]), halves(m % 2), func, bias=b).then_inc(sem(f"m{j}_hid"), 1)

        def expert_out(v, j, e, e_col):
            v.wait_ge(sem(f"m{j}_down"), FREE + e + 1)
            v.wait_ge(sem(f"m{j}_out"), FREE + e)
            for t in range(NT):
                x = X[0:ROWS[t], t, :]
                last = v.scalar_tensor_tensor(x, ytile(t), COMB[0:ROWS[t], t, bass.ds(e_col, 1)], x, ALU.mult, ALU.add)
            last.then_inc(sem(f"m{j}_out"), 1)

        def experts_v(v, j, E):
            with v.Fori(0, E // 2) as i:
                for k in range(2):
                    expert_out(v, j, i * 2 + k, i * 2 + k)
            v.wait_ge(sem(f"m{j}_out"), FREE + E)

        def moe0_pe(pe):
            turn_pe(pe, 1, 2, XR)
            pe.wait_ge(sem("gate0_in"), 1)
            gate_pe(pe, 0, 8, gate0, xTg[:, 1, :, :], False)
            with pe.Fori(0, 4) as i:
                for k in range(2):
                    pe.wait_ge(sem("m0_wu%d" % k), i * 32 + 32)
                    pe.wait_ge(sem("m0_xg"), i * 2 + (k + 1))
                    for m in range(NCH):
                        pe.wait_ge(sem("m0_silu"), FREE + i * 12 + (k * 6 + m))
                        up_mm(pe, 0, k, m * P, xTg[:, k, :, :]).then_inc(sem("m0_upa"), 1)
                        pe.wait_ge(sem("m0_hid"), FREE + i * 12 + (k * 6 + m))
                        up_mm(pe, 1, k, FF + m * P, xTg[:, k, :, :]).then_inc(sem("m0_upb"), 1)
                    down_mm(pe, 0, k, i * 2 + k, NCH, lambda m: i * 12 + (k * 6 + m + 1))

        def moe0_act(act):
            act.wait_ge(sem("weights2"), NLOAD[2])
            turn_act(act, 1)
            gate_act(act, 0, SOFT_PAIR)
            with act.Fori(0, 4) as i:
                for k in range(2):
                    for m in range(NCH):
                        act.wait_ge(sem("m0_upa"), i * 12 + (k * 6 + m + 1))
                        act.wait_ge(sem("m0_hid"), FREE + i * 12 + (k * 6 + max(m - 1, 0)))
                        act.activation(two(SIL[:, m % 2, :]), halves(0), ACT.Silu).then_inc(sem("m0_silu"), 1)

        def moe0_v(v):
            v.wait_ge(sem("weights2"), NLOAD[2])
            norm_v(v, 2, X2, XR, 1e-6, False)
            turn_v(v, 1)
            xT_ready(v, 1)

            def scaled(e, k):
                for c in range(2):
                    last = v.tensor_scalar(xTg[:, k, c, :], xT[0:KD, c, :],
                                           g_exp[:, bass.ds(e, 1), c], None, ALU.mult)
                return last

            for c in range(2):
                last = v.tensor_scalar(xTg[:, 1, c, :], xT[0:KD, c, :], g_moe[:, c:c + 1], None, ALU.mult)
            last.then_inc(sem("gate0_in"), 1)
            v.memset(g_exp[:, 8, :], 0.0)
            scaled(0, 0).then_inc(sem("m0_xg"), 1)
            gate_v(v, 0, 8, SOFT_PAIR)
            link(v, v.tensor_reduce(TOPV[:, 0, :], COMB[:, :, 0:8], AX.X, ALU.add))
            for t in range(NT):
                last = v.scalar_tensor_tensor(X[:, t, :], X2[:, t, :], TOPV[:, 0, t:t + 1], X[:, t, :], ALU.mult, ALU.add)
            link(v, last)
            with v.Fori(0, 4) as i:
                for k in range(2):
                    v.wait_ge(sem("m0_down"), FREE + i * 2)
                    scaled(i * 2 + (k + 1), 1 - k).then_inc(sem("m0_xg"), 1)
                    for m in range(NCH):
                        v.wait_ge(sem("m0_upb"), i * 12 + (k * 6 + m + 1))
                        v.wait_ge(sem("m0_silu"), FREE + i * 12 + (k * 6 + m + 1))
                        v.tensor_tensor(two(hT[:, m, :]), halves(1), two(SIL[:, m % 2, :]), ALU.mult)\
                            .then_inc(sem("m0_hid"), 1)
                    expert_out(v, 0, i * 2 + k, i * 2 + k)
            v.wait_ge(sem("m0_out"), FREE + 8)

        def moe1_pe(pe):
            turn_pe(pe, 2, 3, XN)
            xT_ready(pe, 2)
            gate_pe(pe, 1, 8, gate1, xT, True)
            outbias_pe(pe, 0, 1, 8, b_proj)
            experts_pe(pe, 1, 8)

        def moe1_act(act):
            turn_act(act, 2)
            gate_act(act, 1, SOFT_PAIR)
            act.wait_ge(sem("combT_ready"), 1)
            experts_act(act, 1, 8, ACT.Gelu_apprx_tanh, b_fc)

        def moe1_v(v):
            norm_v(v, 3, X, XN, 1e-5, True)
            turn_v(v, 2)
            gate_v(v, 1, 8, SOFT_PAIR)
            outbias_v(v, 0, 8)
            experts_v(v, 1, 8)

        def moe2_pe(pe):
            turn_pe(pe, 4, 6, XR)
            xT_ready(pe, 4)
            gate_pe(pe, 2, 16, gate2, xT, False)
            experts_pe(pe, 2, 16)

        def moe2_act(act):
            turn_act(act, 4, ln_w1)
            gate_act(act, 2, SOFT_TOP1)
            experts_act(act, 2, 16, ACT.Relu)

        def moe2_v(v):
            norm_v(v, 5, X, XN, 1e-5, True)
            v.wait_ge(sem("normed"), 6)
            norm_v(v, 6, XN, XR, 1e-6, False)
            link(v, v.tensor_tensor(X[:], X[:], XN[:], ALU.add))
            turn_v(v, 4, ln_w1)
            gate_v(v, 2, 16, SOFT_TOP1)
            experts_v(v, 2, 16)

        def moe3_pe(pe):
            turn_pe(pe, 7, 10, XN)
            xT_ready(pe, 7)
            gate_pe(pe, 3, 8, gate3, xT, False)
            experts_pe(pe, 3, 8)

        def moe3_act(act):
            turn_act(act, 7)
            gate_act(act, 3, SOFT_TOP2)
            experts_act(act, 3, 8, ACT.Gelu_apprx_tanh)

        def moe3_v(v):
            norm_v(v, 10, X, XN, 1e-5, True)
            turn_v(v, 7)
            gate_v(v, 3, 8, SOFT_TOP2)
            experts_v(v, 3, 8)

        HG, _ = view(0, [2, NT, FH])

        def m4_up(pe, e, k, w):
            pe.wait_ge(sem(f"m4_wu{k}"), w * 32 + 32)
            for t in range(NT):
                pe.wait_ge(sem("m4_gelu"), FREE + e * NT + max(t - 1, 0))
                for c in range(2):
                    kk = KD + c
                    last = pe.matmul(PH[0:ROWS[t], t % 2, 0:FH], xT[0:kk, c, t * P:t * P + ROWS[t]],
                                     WU[0:kk, k, c, 0:FH], start=(c == 0), stop=(c == 1))
                last.then_inc(sem("m4_up"), 1)

        def m4_turn_down(pe, e, k):
            pe.wait_ge(sem("m4_normed"), e + 1)
            for m in range(NFH):
                if m < 2:
                    pe.wait_ge(sem("m4_hid"), FREE + e * 4)
                else:
                    pe.wait_ge(sem("m4_hid"), FREE + e * 4 + 1)
                for t in range(FULL):
                    last = pe.transpose(PH[:, 2 + m % 2, t * P:(t + 1) * P], HG[:, k, t, m * P:(m + 1) * P], ident[:, :])
                last.then_inc(sem("m4_turned"), 1)
                if m == 0:
                    for q in range(NFH):
                        last = pe.transpose(PG[:, q * P:q * P + LASTROWS], HG[0:LASTROWS, k, NT - 1, q * P:(q + 1) * P],
                                            ident[0:LASTROWS, 0:LASTROWS])
                    last.then_inc(sem("m4_turned"), 1)
            down_mm(pe, 4, k, e, NFH, lambda m: e * 4 + max(2, m + 2))

        def m4_gelu(act, e, k):
            for t in range(NT):
                act.wait_ge(sem("m4_up"), e * NT + (t + 1))
                act.activation(HG[0:ROWS[t], k, t, :], PH[0:ROWS[t], t % 2, 0:FH], ACT.Gelu).then_inc(sem("m4_gelu"), 1)

        def m4_norm(v, e, k):
            for t in range(NT):
                v.wait_ge(sem("m4_gelu"), FREE + e * NT + (t + 1))
                last = v.bn_stats(stats[0:ROWS[t], t, :], HG[0:ROWS[t], k, t, :])
            last.then_inc(sem("m4_stats"), 1)
            v.wait_ge(sem("m4_stats"), e + 1)
            half = [stats[:, :, k] for k in range(6)]
            v.tensor_tensor(meanvar[:, :, 0], half[1], half[4], ALU.add)
            v.tensor_tensor(meansq[:], half[1], half[4], ALU.subtract)
            v.tensor_tensor(var_eps[:], half[2], half[5], ALU.add).then_inc(sem("m4_sums"), 1)
            v.wait_ge(sem("m4_sums"), e + 1)
            v.tensor_scalar(meanvar[:, :, 0], meanvar[:, :, 0], 0.5, None, ALU.mult)
            v.tensor_tensor(meansq[:], meansq[:], meansq[:], ALU.mult)
            v.tensor_scalar(var_eps[:], var_eps[:], 1.0 / FH, 1e-5, ALU.mult, ALU.add).then_inc(sem("m4_scaled"), 1)
            v.wait_ge(sem("m4_scaled"), e + 1)
            v.scalar_tensor_tensor(var_eps[:], meansq[:], 0.25, var_eps[:], ALU.mult, ALU.add).then_inc(sem("m4_var"), 1)
            v.wait_ge(sem("m4_rstd"), e + 1)
            for t in range(NT):
                r = ROWS[t]
                last = v.tensor_scalar(HG[0:r, k, t, :], HG[0:r, k, t, :], meanvar[0:r, t, 0:1], rstd[0:r, t:t + 1],
                                       ALU.subtract, ALU.mult)
            last.then_inc(sem("m4_normed"), 1)

        def m4_to_hT(v, e):
            def moved(dst, src, m):
                return v.tensor_scalar(dst, src, lnw4[:, bass.ds(e * NFH + m, 1)], lnb4[:, bass.ds(e * NFH + m, 1)],
                                       ALU.mult, ALU.add)
            v.wait_ge(sem("m4_down"), FREE + e)
            for m in range(NFH):
                v.wait_ge(sem("m4_turned"), e * 4 + (1 if m == 0 else m + 2))
                moved(hT[:, m, 0:FULL * P], PH[:, 2 + m % 2, :], m).then_inc(sem("m4_hid"), 1)
                if m == 0:
                    v.wait_ge(sem("m4_turned"), e * 4 + 2)
                    for q in range(NFH):
                        last = moved(hT[:, q, FULL * P:N], PG[:, q * P:q * P + LASTROWS], q)
                    last.then_inc(sem("m4_hid"), 1)

        def moe4_pe(pe):
            turn_pe(pe, 9, 12, XN)
            xT_ready(pe, 9)
            gate_pe(pe, 4, 16, gate4, xT, True)
            outbias_pe(pe, 1, 4, 16, b_fc2)
            m4_up(pe, 0, 0, 0)
            with pe.Fori(0, 7) as i:
                m4_up(pe, i * 2 + 1, 1, i)
                m4_turn_down(pe, i * 2, 0)
                m4_up(pe, i * 2 + 2, 0, i + 1)
                m4_turn_down(pe, i * 2 + 1, 1)
            m4_up(pe, 15, 1, 7)
            m4_turn_down(pe, 14, 0)
            m4_turn_down(pe, 15, 1)

        def moe4_act(act):
            turn_act(act, 9)
            gate_act(act, 4, SHARED_TOP3)
            act.wait_ge(sem("combT_ready"), 2)
            m4_gelu(act, 0, 0)
            with act.Fori(0, 7) as i:
                for k in range(2):
                    e = i * 2 + (k + 1)
                    act.wait_ge(sem("m4_hid"), FREE + i * 8 + 4 * k)
                    m4_gelu(act, e, 1 - k)
            act.wait_ge(sem("m4_hid"), FREE + 56)
            m4_gelu(act, 15, 1)

        def moe4_v(v):
            norm_v(v, 12, X, XN, 1e-5, True)
            turn_v(v, 9)
            gate_v(v, 4, 16, SHARED_TOP3)
            outbias_v(v, 1, 16)
            m4_norm(v, 0, 0)
            with v.Fori(0, 7) as i:
                for k in range(2):
                    e = i * 2 + k
                    m4_to_hT(v, e)
                    m4_norm(v, i * 2 + (k + 1), 1 - k)
                    expert_out(v, 4, e, e)
            m4_to_hT(v, 14)
            m4_norm(v, 15, 1)
            expert_out(v, 4, 14, 14)
            m4_to_hT(v, 15)
            expert_out(v, 4, 15, 15)
            v.wait_ge(sem("m4_out"), FREE + 16)

        def moe4_pool(p):
            norm_pool(p, 12)
            with p.Fori(0, 16) as e:
                p.wait_ge(sem("m4_var"), e + 1)
                p.tensor_tensor(rstd[:], var_eps[:], minus_half[:], ALU.pow).then_inc(sem("m4_rstd"), 1)

        HEADS, HG_, DV = [12, 8, 12], [3, 2, 3], [8, 24, 16]
        ESCALE = [float(8) ** -0.5, float(LDK) ** -0.5, 1.0]
        GROUPS = 4

        def rows_of(s):
            return 64 if s == 0 else T

        def scores_pe(pe, a, p):
            if p >= 2:
                pe.wait_ge(sem("at_sub"), 8 * a + p - 1)
            S = PH[:, p % 2, :]
            for s in range(2):
                b, r = 2 * p + s, rows_of(s)
                o = S[64 * s:64 * s + r, :]
                if a == 0:
                    last = pe.matmul(o[:, 0:QH * T], QT[0:96, 0, b * T:b * T + r],
                                     KB[0:96, :, :, :].rearrange("p c b n -> p (c b n)")[:, b * QH * T:(b + 1) * QH * T],
                                     start=True, stop=True, skip_group_check=True)
                elif a == 1:
                    for c in range(4):
                        last = pe.matmul(o[:, 2 * c * T:2 * (c + 1) * T], QT[:, c, b * T:b * T + r],
                                         KM[:, c, b, :], start=True, stop=True, skip_group_check=True)
                else:
                    for c in range(2):
                        last = pe.matmul(o[:, c * 6 * T:(c + 1) * 6 * T], QT[0:96, c, b * T:b * T + r],
                                         KB[0:96, c, b, :], start=True, stop=True, skip_group_check=True)
            last.then_inc(sem("at_scores"), 1)

        def values_pe(pe, a, p):
            if p >= 1:
                pe.wait_ge(sem("at_vb"), 8 * a + p)
            hg, w = HG_[a], HEADS[a] * DV[a]
            for s in range(2):
                b = 2 * p + s
                o = PY[0:hg * T, 2, s * D:s * D + w]

                if a == 0:
                    last = pe.matmul(o, REP(a, 0)[:, b, :], ident[0:96, 0:96], start=True, stop=True,
                                     skip_group_check=True)
                else:
                    for c in range(2):
                        w_ = wv[:, c, :] if a == 1 else wqkv[:, c, 2 * D:3 * D]
                        last = pe.matmul(o, REP(a, c)[:, b, :], w_, start=(c == 0), stop=(a == 1 and c == 1),
                                         skip_group_check=True)
                    if a == 2:
                        last = pe.matmul(o, ones_row[0:1, 0:hg * T], bv[0:1, :], start=False, stop=True,
                                         skip_group_check=True)
            last.then_inc(sem("at_values"), 1)

        def turn_probs_pe(pe, a, p):
            pe.wait_ge(sem("at_exp"), 8 * a + p + 1)
            if p >= 2:
                pe.wait_ge(sem("at_pts"), 8 * a + p - 1)
            g = HG_[a] * T
            for q in range(GROUPS):
                last = pe.transpose(PH[0:g, 2 + p % 2, q * P:q * P + R2], PM[0:R2, p % 2, q * g:(q + 1) * g],
                                    ident[0:R2, 0:R2])
            last.then_inc(sem("at_pt"), 1)

        def mix_pe(pe, a, p):
            pe.wait_ge(sem("at_pts"), 8 * a + p + 1)
            pe.wait_ge(sem("at_vb"), 8 * a + p + 1)
            if p >= 2:
                pe.wait_ge(sem("at_osb"), 8 * a + p - 1)
            g, w = HG_[a] * T, HG_[a] * DV[a]
            for s in range(2):
                b, r = 2 * p + s, rows_of(s)
                for q in range(GROUPS):
                    last = pe.matmul(PY[64 * s:64 * s + r, p % 2, q * w:(q + 1) * w],
                                     PTS[0:g, p % 2, q * P + 64 * s:q * P + 64 * s + r],
                                     VB[0:g, b, q * w:(q + 1) * w], start=True, stop=True, skip_group_check=True)
            last.then_inc(sem("at_o"), 1)

        def turn_out_pe(pe, a, p):
            pe.wait_ge(sem("at_osb"), 8 * a + p + 1)
            if p >= 1:
                pe.wait_ge(sem("at_ot"), 8 * a + p)
            for c in range(1 if a == 0 else 2):
                last = pe.transpose(PG[0:96, c * P:c * P + R2], OSB[0:R2, p % 2, c * 96:(c + 1) * 96], ident[0:R2, 0:R2])
            last.then_inc(sem("at_turned"), 1)

        def REP(a, c):
            n, at = B * HG_[a] * T, 2 * LH * NREL if a == 1 else 0
            flat = hT[0:96].rearrange("p a n -> p (a n)")[:, at + c * n:at + (c + 1) * n]
            return flat.rearrange("p (b n) -> p b n", b=B)

        def repeat_act(act, a):
            for c in range(1 if a == 0 else 2):
                src = (QT[0:96, 0, 0:N] if a == 0 else xT[0:96, c, :]).rearrange("p (b j) -> p b j", j=T)
                act.activation(REP(a, c).rearrange("p b (g j) -> p b g j", j=T),
                               src.unsqueeze(2).to_broadcast([96, B, HG_[a], T]), ACT.Copy).then_inc(sem("at_rep"), 1)

        def pairs_pe(pe, a):
            pe.wait_ge(sem("at_rep"), [1, 3, 5][a])
            for p in range(PAIRS + 3):
                if p < PAIRS:
                    values_pe(pe, a, p)
                    scores_pe(pe, a, p)
                if 0 <= p - 1 < PAIRS:
                    turn_probs_pe(pe, a, p - 1)
                if 0 <= p - 2 < PAIRS:
                    mix_pe(pe, a, p - 2)
                if 0 <= p - 3 < PAIRS:
                    turn_out_pe(pe, a, p - 3)
            pe.wait_ge(sem("at_ot"), 8 * (a + 1))

        def pairs_v(v, a):
            H, hg, dv = HEADS[a], HG_[a], DV[a]
            mask = mask8 if a == 1 else mask12

            def heads(ap):
                return ap.rearrange("p (h j) -> p h j", j=T)

            def over(ap, n):
                return ap.unsqueeze(2).to_broadcast([R2, H, n])

            for p in range(PAIRS + 2):
                if p < PAIRS:
                    v.wait_ge(sem("at_values"), 8 * a + p + 1)
                    for s in range(2):
                        last = v.tensor_tensor(
                            VB[0:hg * T, 2 * p + s, 0:H * dv].rearrange("p (g h d) -> p g h d", g=GROUPS, h=hg),
                            PY[0:hg * T, 2, s * D:s * D + H * dv].rearrange("p (g h d) -> p g h d", g=GROUPS, h=hg),
                            mask[:, :].unsqueeze(1).unsqueeze(3).to_broadcast([hg * T, GROUPS, hg, dv]), ALU.mult)
                    last.then_inc(sem("at_vb"), 1)
                    v.wait_ge(sem("at_scores"), 8 * a + p + 1)
                    if p >= 2:
                        v.wait_ge(sem("at_pt"), 8 * a + p - 1)
                    S, M = PH[0:R2, p % 2, 0:H * T], PM[0:R2, p % 2, 0:H * T]
                    if a == 1:
                        v.wait_ge(sem("rel_in"), 16 * B)
                        link(v, v.tensor_tensor(M, S, RB8[0:R2, p, :], ALU.add))
                        S = M
                    link(v, v.tensor_reduce(amax[0:R2, p % 2, 0:H], heads(S), AX.X, ALU.max))
                    v.tensor_tensor(heads(M), heads(S), over(amax[0:R2, p % 2, 0:H], T), ALU.subtract)\
                        .then_inc(sem("at_sub"), 1)
                if 0 <= p - 1 < PAIRS:
                    q = p - 1
                    v.wait_ge(sem("at_exp"), 8 * a + q + 1)
                    link(v, v.tensor_reduce(asum[0:R2, q % 2, 0:H], heads(PM[0:R2, q % 2, 0:H * T]), AX.X, ALU.add))
                    link(v, v.reciprocal(arinv[0:R2, q % 2, 0:H], asum[0:R2, q % 2, 0:H]))
                if 0 <= p - 2 < PAIRS:
                    q = p - 2
                    v.wait_ge(sem("at_o"), 8 * a + q + 1)
                    if q >= 2:
                        v.wait_ge(sem("at_turned"), 8 * a + q - 1)
                    v.tensor_tensor(OSB[0:R2, q % 2, 0:H * dv].rearrange("p (h d) -> p h d", d=dv),
                                    PY[0:R2, q % 2, 0:H * dv].rearrange("p (h d) -> p h d", d=dv),
                                    over(arinv[0:R2, q % 2, 0:H], dv), ALU.mult).then_inc(sem("at_osb"), 1)

        def pairs_act(act, a):
            g, nc_ = HG_[a] * T, 1 if a == 0 else 2
            for p in range(PAIRS + 3):
                if p < PAIRS:
                    M = PM[0:R2, p % 2, 0:HEADS[a] * T]
                    act.wait_ge(sem("at_sub"), 8 * a + p + 1)
                    act.activation(M, M, ACT.Exp, scale=ESCALE[a]).then_inc(sem("at_exp"), 1)
                if 0 <= p - 1 < PAIRS:
                    q = p - 1
                    act.wait_ge(sem("at_pt"), 8 * a + q + 1)
                    if q >= 2:
                        act.wait_ge(sem("at_o"), 8 * a + q - 1)
                    act.activation(PTS[0:g, q % 2, :].rearrange("p (q r) -> p q r", q=GROUPS)[:, :, 0:R2],
                                   PH[0:g, 2 + q % 2, :].rearrange("p (q r) -> p q r", q=GROUPS)[:, :, 0:R2],
                                   ACT.Copy).then_inc(sem("at_pts"), 1)
                if 0 <= p - 3 < PAIRS:
                    q = p - 3
                    act.wait_ge(sem("at_turned"), 8 * a + q + 1)
                    for c in range(nc_):
                        last = act.activation(
                            OT[0:96, c, q * 2 * T:(q + 1) * 2 * T].rearrange("p (s j) -> p s j", s=2),
                            PG[0:96, c * P:(c + 1) * P].rearrange("p (s j) -> p s j", s=2)[:, :, 0:T], ACT.Copy)
                    last.then_inc(sem("at_ot"), 1)

        def project_pe(pe, a, w, bias):
            for t in range(NT):
                n = 1 if a == 0 else 2
                for c in range(n):
                    last = pe.matmul(ytile(t), OT[0:96, c, t * P:t * P + ROWS[t]], w[0:96, c, :] if n > 1 else w[:, :],
                                     start=(c == 0), stop=(bias is None and c == n - 1), skip_group_check=True)
                if bias is not None:
                    last = pe.matmul(ytile(t), ones_row[0:1, 0:ROWS[t]], bias[0:1, :], start=False, stop=True,
                                     skip_group_check=True)
            last.then_inc(sem("projected"), 1)

        TWO_PI = 2 * np.pi
        C1 = 6.28125
        C2 = float(np.float32(np.round((TWO_PI - C1) * 2 ** 20) / 2 ** 20))
        C3 = TWO_PI - C1 - C2
        ROUND = 1.5 * 2 ** 23
        XTH = CX.rearrange("p a n -> p (a n)")[:, 0:N + 1]
        KTH = QV.rearrange("p a n -> p (a n)")[0:96, 0:N + 1]
        SINS = QV.rearrange("p a n -> p (a n)")[0:96, N + 1:2 * N + 2]

        def cos_pe(pe):
            turn_pe(pe, 3, 4, XN)
            pe.wait_ge(sem("q_ready"), 1)
            pairs_pe(pe, 0)
            project_pe(pe, 0, w_comb, None)

        def cos_act(act):
            turn_act(act, 3)
            act.wait_ge(sem("angles"), 1)
            act.activation(SINS, XTH, ACT.Sin).then_inc(sem("sines"), 1)
            act.wait_ge(sem("q_made"), 1)
            repeat_act(act, 0)
            pairs_act(act, 0)

        def cos_v(v):
            norm_v(v, 4, X, XN, 1e-5, True)
            turn_v(v, 3)
            xT_ready(v, 3)
            v.tensor_copy(XTH[:, 0:N], xT[0:96, 0, :])
            link(v, v.tensor_copy(XTH[:, N:N + 1], theta[:, :]))
            link(v, v.tensor_scalar(KTH, XTH, 1.0 / TWO_PI, ROUND, ALU.mult, ALU.add))
            link(v, v.tensor_scalar(KTH, KTH, -ROUND, None, ALU.add))
            for cc in (C1, C2, C3):
                link(v, v.scalar_tensor_tensor(XTH, KTH, -cc, XTH, ALU.mult, ALU.add))
            link(v, v.scalar_tensor_tensor(XTH, XTH, -1.0, XTH, ALU.mult, ALU.min))
            v.tensor_scalar(XTH, XTH, np.pi / 2, None, ALU.add).then_inc(sem("angles"), 1)
            v.wait_ge(sem("sines"), 1)
            link(v, v.tensor_copy(cth[:, 0:1], SINS[:, N:N + 1]))
            v.tensor_scalar(QT[0:96, 0, 0:N], SINS[:, 0:N], cth[:, 0:1], None, ALU.mult).then_inc(sem("q_made"), 1)
            v.wait_ge(sem("q_made"), 1)
            v.tensor_tensor(KB[0:96].rearrange("p c b n -> p (c b n)").rearrange("p (b h j) -> p b h j", b=B, h=QH),
                            QT[0:96, 0, 0:N].rearrange("p (b j) -> p b j", j=T).unsqueeze(2).to_broadcast([96, B, QH, T]),
                            khead12[:, :].unsqueeze(1).unsqueeze(3).to_broadcast([96, B, QH, T]), ALU.mult)\
                .then_inc(sem("q_ready"), 1)
            pairs_v(v, 0)
            v.wait_ge(sem("projected"), 1)
            link(v, add_to(v, X, X))

        RB8, _r = view(b_, [PAIRS, LH * T])
        assert _r <= LATE

        def rel_pe(pe):
            turn_pe(pe, 5, 8, XR)
            xT_ready(pe, 5)
            for c in range(4):
                last = pe.matmul(PG[:, c * P:c * P + NREL], wposT[:, c * P:(c + 1) * P], basis[:, :], start=True, stop=True,
                                 skip_group_check=True)
            last.then_inc(sem("wr_ready"), 1)
            for q in range(8):
                w, c = (wq, wk)[q // 4], q % 4
                if q >= 2:
                    pe.wait_ge(sem("qk_moved"), q - 1)
                for h in range(2):
                    for k in range(2):
                        last = pe.matmul(PH[:, 2 * (q % 2) + h, 0:HF], w[:, k, c * P:(c + 1) * P],
                                         xT[0:KD, k, h * HF:(h + 1) * HF], start=(k == 0), stop=(k == 1))
                last.then_inc(sem("qk_ready"), 1)
            pe.wait_ge(sem("wr_moved"), 1)
            for t in range(NT):
                pe.wait_ge(sem("qk_moved"), 8)
                if t >= 2:
                    pe.wait_ge(sem("rel_moved"), t - 1)
                for c in range(4):
                    o = PH[0:ROWS[t], 2 * (t % 2) + c // 2, (c % 2) * 2 * NREL:(c % 2 + 1) * 2 * NREL]
                    last = pe.matmul(o, QV8[:, c, t * P:t * P + ROWS[t]], WR[:, c, :],
                                     start=True, stop=True, skip_group_check=True)
                last.then_inc(sem("rel_ready"), 1)
            pe.wait_ge(sem("rel_moved"), NT)
            pairs_pe(pe, 1)
            project_pe(pe, 1, wo, bo)
            turn_pe(pe, 6, 9, XR)
            xT_ready(pe, 6)
            for m in range(NFH):
                if m >= 2:
                    pe.wait_ge(sem("ffn_hid"), m - 1)
                for h in range(2):
                    for c in range(2):
                        last = pe.matmul(PH[:, 2 * (m % 2) + h, 0:HF], fw1[:, c, m * P:(m + 1) * P],
                                         xT[0:KD, c, h * HF:(h + 1) * HF], start=(c == 0), stop=(c == 1))
                last.then_inc(sem("ffn_up"), 1)
            for m in range(NFH):
                pe.wait_ge(sem("ffn_hid"), m + 1)
                for t in range(NT):
                    pe.matmul(ytile(t), hT[:, m, t * P:t * P + ROWS[t]], fw2[:, m, :], start=(m == 0 and t % 2 == 0),
                              stop=False, skip_group_check=True)
            for t in range(NT):
                last = pe.matmul(ytile(t), ones_row[0:1, 0:ROWS[t]], fb2[0:1, :], start=False, stop=True,
                                 skip_group_check=True)
            last.then_inc(sem("ffn_out"), 1)

        def rel_act(act):
            turn_act(act, 5, norm1_w)
            for q in range(4):
                act.wait_ge(sem("qk_ready"), q + 1)
                act.activation(two(QV8[:, q, 0:N]), halves(q % 2), ACT.Identity, bias=v_par[:, q:q + 1]).then_inc(sem("qv_moved"), 1)
            xT_ready(act, 5)
            repeat_act(act, 1)
            pairs_act(act, 1)
            turn_act(act, 6, norm2_w)
            for m in range(NFH):
                act.wait_ge(sem("ffn_up"), m + 1)
                act.activation(two(hT[:, m, :]), halves(m % 2), ACT.Gelu, bias=fb1[:, m:m + 1]).then_inc(sem("ffn_hid"), 1)

        def rel_v(v):
            norm_v(v, 7, X, XN, 1e-5, True)
            v.wait_ge(sem("normed"), 8)
            norm_v(v, 8, XN, XR, 1e-5, False)
            turn_v(v, 5, norm1_w)
            v.memset(KM[:], 0.0)
            v.memset(WR[:], 0.0)
            v.memset(RB8[32:64], 0.0).then_inc(sem("rel_clear"), 1)
            v.wait_ge(sem("rel_clear"), 1)
            v.wait_ge(sem("wr_ready"), 1)
            for z in range(2):
                last = v.tensor_copy(WR[64 * z:64 * z + 64, :, z * NREL:(z + 1) * NREL],
                                     PG[64 * z:64 * z + 64, :].rearrange("p (c r) -> p c r", c=4)[:, :, 0:NREL])
            last.then_inc(sem("wr_moved"), 1)
            for q in range(8):
                v.wait_ge(sem("qk_ready"), q + 1)
                if q < 4:
                    v.wait_ge(sem("qv_moved"), q + 1)
                    v.tensor_scalar(two(QT[:, q, 0:N]), halves(q % 2), u_par[:, q:q + 1], None, ALU.add).then_inc(sem("qk_moved"), 1)
                else:
                    for z in range(2):
                        last = v.tensor_copy(
                            KM[64 * z:64 * z + 64, q - 4, :, z * T:(z + 1) * T].rearrange("p (h b) j -> p h b j", h=2),
                            halves(q % 2)[64 * z:64 * z + 64].rearrange("p h (b j) -> p h b j", j=T))
                    last.then_inc(sem("qk_moved"), 1)
            for t in range(NT):
                v.wait_ge(sem("rel_ready"), t + 1)
                if t >= 2:
                    v.wait_ge(sem(f"rel_out{t % 2}"), 16 * (t // 2))
                v.tensor_copy(RSB[0:ROWS[t], t % 2, :].rearrange("p (a n) -> p a n", a=2),
                              PH[0:ROWS[t], 2 * (t % 2):2 * (t % 2) + 2, 0:4 * NREL]).then_inc(sem("rel_moved"), 1)
            pairs_v(v, 1)
            v.wait_ge(sem("projected"), 2)
            link(v, add_to(v, X2, XN))
            norm_v(v, 9, X2, XR, 1e-5, False)
            link(v, v.tensor_tensor(X[:], X[:], X2[:], ALU.add))
            turn_v(v, 6, norm2_w)
            v.wait_ge(sem("ffn_out"), 1)
            link(v, add_to(v, X, X))

        def rel_sp(sp):
            for t in range(NT):
                sp.wait_ge(sem("rel_moved"), t + 1)
                sp.dma_start(rel_dram[t * P:t * P + ROWS[t], :], RSB[0:ROWS[t], t % 2, :]).then_inc(sem(f"rel_out{t % 2}"), 16)
            sp.wait_ge(sem("rel_out0"), 16 * 3)
            sp.wait_ge(sem("rel_out1"), 16 * 2)
            sp.wait_ge(sem("rel_clear"), 1)
            for b in range(B):
                src = bass.AP(tensor=rel_dram.tensor, offset=b * T * LH * NREL + T - 1,
                              ap=[[LH * NREL - 1, T], [NREL, LH], [1, T]])
                sp.dma_start(RB8[64 * (b % 2):64 * (b % 2) + T, b // 2, :].rearrange("p (h j) -> p h j", j=T), src)\
                    .then_inc(sem("rel_in"), 16)

        def plain_pe(pe):
            turn_pe(pe, 8, 11, XN)
            xT_ready(pe, 8)
            for q in range(4):
                if q >= 2:
                    pe.wait_ge(sem("pqk_moved"), q - 1)
                for h in range(2):
                    for k in range(2):
                        last = pe.matmul(PH[0:96, 2 * (q % 2) + h, 0:HF], wqkv[:, k, q * 96:(q + 1) * 96],
                                         xT[0:KD, k, h * HF:(h + 1) * HF], start=(k == 0), stop=(k == 1))
                last.then_inc(sem("pqk_ready"), 1)
            pe.wait_ge(sem("pqk_moved"), 4)
            pairs_pe(pe, 2)
            project_pe(pe, 2, wo3, bo3)

        def plain_act(act):
            turn_act(act, 8)
            xT_ready(act, 8)
            repeat_act(act, 2)
            pairs_act(act, 2)

        def plain_v(v):
            norm_v(v, 11, X, XN, 1e-5, True)
            turn_v(v, 8)
            for q in range(4):
                v.wait_ge(sem("pqk_ready"), q + 1)
                if q < 2:
                    last = v.tensor_scalar(two(QT[0:96, q, 0:N]), halves(q % 2, 96), bqk[:, q:q + 1], float(16) ** -0.5,
                                           ALU.add, ALU.mult)
                else:
                    for h in range(6):
                        last = v.tensor_scalar(
                            KB[0:96, q - 2, :, h * T:(h + 1) * T].rearrange("p (h b) j -> p h b j", h=2),
                            halves(q % 2, 96).rearrange("p h (b j) -> p h b j", j=T),
                            bqk[:, q:q + 1], khead24[:, h:h + 1], ALU.add, ALU.mult)
                last.then_inc(sem("pqk_moved"), 1)
            pairs_v(v, 2)
            v.wait_ge(sem("projected"), 3)
            link(v, add_to(v, X, X))

        @block.sync
        def _(sp):
            sp.dma_start(patches[:], io["patches"]).then_inc(sem("patches_in"), 16)
            sp.dma_start(tokW[:], kt("tokW", P, KP, D)).then_inc(sem("patches_in"), 16)
            for group in range(3):
                if group == 2:
                    sp.wait_ge(sem("mamba_out"), 1)
                for dst, src, g in loads:
                    if g == group:
                        sp.dma_start(dst, src).then_inc(sem(f"weights{g}"), 16)
            experts_load(sp, 0, 8, NCH, [("m0_w1", 0), ("m0_w3", FF)])
            experts_load(sp, 1, 8, NCH, [("m1_up", 0)])
            experts_load(sp, 2, 16, NCH, [("m2_up", 0)])
            rel_sp(sp)
            experts_load(sp, 3, 8, NCH, [("m3_up", 0)])
            experts_load(sp, 4, 16, NFH, [("m4_up", 0)])
            sp.wait_ge(sem("done"), 1)
            sp.dma_start(out[0:FULL * P, :].rearrange("(t p) d -> p t d", p=P), X[:, 0:FULL, :]).then_inc(sem("out_written"), 16)
            sp.dma_start(out[FULL * P:N, :], X[0:LASTROWS, FULL, :]).then_inc(sem("out_written"), 16)
            sp.wait_ge(sem("out_written"), 32)

        @block.tensor
        def _(pe):
            tokens_pe(pe)
            mamba_pe(pe)
            moe0_pe(pe)
            moe1_pe(pe)
            cos_pe(pe)
            moe2_pe(pe)
            rel_pe(pe)
            moe3_pe(pe)
            plain_pe(pe)
            moe4_pe(pe)

        @block.vector
        def _(v):
            v.memset(xT[KD:KD + 1, :, :], 1.0)
            v.memset(ones_row[:], 1.0)
            v.memset(minus_half[:], -0.5)
            v.memset(X2[:, NT - 1, :], 0.0)
            link(v, v.memset(SC[:], 0.0))
            tokens_v(v)
            mamba_v(v)
            moe0_v(v)
            moe1_v(v)
            cos_v(v)
            moe2_v(v)
            rel_v(v)
            moe3_v(v)
            plain_v(v)
            moe4_v(v)
            v.memset(ones_row[:], 1.0).then_inc(sem("done"), 1)

        @block.scalar
        def _(act):
            mamba_act(act)
            moe0_act(act)
            moe1_act(act)
            cos_act(act)
            moe2_act(act)
            rel_act(act)
            moe3_act(act)
            plain_act(act)
            moe4_act(act)

        @block.gpsimd
        def _(p):
            for name in COUNTED_FROM_FREE:
                p.sem_inc(sem(name), FREE)
            mamba_pool(p)
            norm_pool(p, 2)
            norm_pool(p, 3)
            norm_pool(p, 4)
            norm_pool(p, 5)
            norm_pool(p, 6)
            norm_pool(p, 7)
            norm_pool(p, 8)
            norm_pool(p, 9)
            norm_pool(p, 10)
            norm_pool(p, 11)
            moe4_pool(p)


def prepare(i):
    f = {k: np.asarray(v) for k, v in i.items()}
    c = np.ascontiguousarray
    a = {}
    x = f["x"].reshape(B, 6, 16, 6, 16, 3).transpose(2, 4, 5, 0, 1, 3).reshape(PATCH, B, T - 1)
    pt = np.zeros((PATCH, NPAD), np.float32)
    pt[:, :N].reshape(PATCH, B, T)[:, :, 1:] = x
    a["patches"] = c(pt.reshape(KP, P, NPAD).transpose(1, 0, 2))
    a["tokW"] = f["L0_tok_W"]
    oh = np.zeros((T + 1, NPAD), np.float32)
    for n in range(N):
        oh[n % T, n] = 1
        if n % T == 0:
            oh[T, n] = 1
    a["tok_onehot"] = oh
    a["postab"] = np.concatenate([f["L0_tok_pos_emb"][0], f["L0_tok_class_emb"][0]], 0)
    a["ident"] = np.eye(P, dtype=np.float32)
    a["rev_iota"] = np.tile(np.arange(16, 0, -1, dtype=np.float32), (P, 1))
    a["head_mask12"] = np.kron(np.eye(3), np.ones((T, 1))).astype(np.float32)
    a["head_mask8"] = np.kron(np.eye(2), np.ones((T, 1))).astype(np.float32)
    a["khead12"] = np.kron(np.eye(12), np.ones((8, 1))).astype(np.float32)
    a["khead24"] = np.kron(np.eye(6), np.ones((16, 1))).astype(np.float32)
    one = np.float32
    rate = np.exp(np.log(one((T + 1) / 2.0)) / one(NPOS // 2))
    width = rate ** np.arange(1, NPOS // 2 + 1, dtype=np.float32)
    dist = np.arange(-(T - 1), T, dtype=np.float32)
    unsigned = (np.abs(dist)[None, :] <= width[:, None]).astype(np.float32)
    a["rel_basis"] = np.concatenate([unsigned, np.sign(dist)[None, :] * unsigned], 0)

    def colsof(v, p):
        return c(v.reshape(-1, p).T)

    L = "L0_attn_"
    a["g_mamba"] = colsof(f[L + "g_mamba"], KD)
    a["w_in"] = f[L + "w_in"]
    a["conv_w"] = c(f[L + "conv_w"].reshape(NC_I, P, DCONV).transpose(1, 0, 2))
    a["conv_b"] = colsof(f[L + "conv_b"], P)
    a["w_xproj"] = f[L + "w_xproj"]
    a["w_dt"] = f[L + "w_dt"]
    a["b_dt"] = colsof(f[L + "b_dt"], P)
    a["A_log"] = c(f[L + "A_log"].reshape(NC_I, P, DS).transpose(1, 0, 2))
    a["D_skip"] = colsof(f[L + "D_skip"], P)
    a["w_out"] = f[L + "w_out"]
    a["g_moe"] = colsof(f[L + "g_moe"], KD)
    a["router0"] = f[L + "w_router"]
    a["g_exp"] = c(f[L + "g_exp"].reshape(8, 2, KD).transpose(2, 0, 1))
    a["m0_w1"], a["m0_w3"], a["m0_down"] = f[L + "w1"], f[L + "w3"], f[L + "w2"]
    L = "L0_ffn_"
    a["gate1"] = c(f[L + "gate_w"].T)
    a["gate1_b"] = f[L + "gate_b"][None]
    a["b_fc"] = c(f[L + "b_fc"].reshape(8, NCH, P).transpose(2, 0, 1).reshape(P, -1))
    a["m1_up"] = c(f[L + "w_fc"].transpose(0, 2, 1))
    a["m1_down"] = c(f[L + "w_proj"].transpose(0, 2, 1))
    a["b_proj"] = f[L + "b_proj"]
    a["theta"] = f["L1_attn_theta"][:, None]
    a["w_comb"] = c(f["L1_attn_W_combine"].T)
    a["ln_w1"] = colsof(f["L1_ffn_ln_w"], KD)
    a["router2"] = f["L1_ffn_w_router"]
    a["m2_up"], a["m2_down"] = f["L1_ffn_wi"], f["L1_ffn_wo"]
    L = "L2_attn_"
    a["norm1_w"], a["norm2_w"] = colsof(f[L + "norm1_w"], KD), colsof(f[L + "norm2_w"], KD)
    a["wq"], a["wk"], a["wv"], a["wo"] = (f[L + k] for k in ("wq", "wk", "wv", "wo"))
    a["bo"] = f[L + "bo"][None]
    a["u_param"] = colsof(f[L + "u_param"].reshape(-1), P)
    a["v_param"] = colsof(f[L + "v_param"].reshape(-1), P)
    a["w_posT"] = c(f[L + "w_pos"].reshape(LH * LDK, NPOS).T)
    a["L2w1"], a["L2w2"] = f[L + "w1"], f[L + "w2"]
    a["L2b1"] = colsof(f[L + "b1"], P)
    a["L2b2"] = f[L + "b2"][None]
    L = "L2_ffn_"
    a["gate3"] = f[L + "w_gate"]
    a["m3_up"] = c(f[L + "w_fc"].reshape(D, FF, 8).transpose(2, 0, 1))
    a["m3_down"] = c(f[L + "w_proj"].reshape(FF, D, 8).transpose(2, 0, 1))
    L = "L3_attn_"
    a["wqkv"] = c(f[L + "w_qkv"].T)
    a["bqk"] = colsof(f[L + "b_qkv"][:2 * D], KD)
    a["bv"] = f[L + "b_qkv"][None, 2 * D:]
    a["wo3"] = c(f[L + "w_out"].T)
    a["bo3"] = f[L + "b_out"][None]
    L = "L3_ffn_"
    a["gate4"] = f[L + "gate_w"]
    a["gate4_b"] = f[L + "gate_b"][None]
    a["m4_up"], a["m4_down"] = f[L + "fc1_w"], f[L + "fc2_w"]
    a["m4_up_b"] = f[L + "fc1_b"]
    a["lnw4"] = c(f[L + "ln_w"].reshape(16, NFH, P).transpose(2, 0, 1).reshape(P, -1))
    a["lnb4"] = c(f[L + "ln_b"].reshape(16, NFH, P).transpose(2, 0, 1).reshape(P, -1))
    a["fc2_b"] = f[L + "fc2_b"]
    return {k: c(v) for k, v in a.items()}


def kernel(**inputs):
    import concourse.bacc as _bacc
    from concourse import mybir as _mybir
    from concourse.bass_utils import run_bass_kernel_spmd as _run

    nc = _bacc.Bacc("TRN2", target_bir_lowering=False, num_devices=1)
    arrays = {f"in_{k}": v for k, v in prepare(inputs).items()}
    io = {k[3:]: nc.dram_tensor(k, v.shape, _mybir.dt.from_np(v.dtype), kind="ExternalInput").ap()
          for k, v in arrays.items()}
    out = nc.dram_tensor("out_0", (N, D), F32, kind="ExternalOutput").ap()
    build(nc, io, out)
    r = _run(nc, [arrays], core_ids=[0])
    return r.results[0]["out_0"].reshape(B, T, D)
```

```python
from contextlib import ExitStack

import numpy as np

import concourse.bass as bass
from concourse import mybir

F32 = mybir.dt.float32
ALU = mybir.AluOpType
ACT = mybir.ActivationFunctionType
AX = mybir.AxisListType

B, T, D = 16, 37, 192
N = B * T
P = 128
NT = (N + P - 1) // P
ROWS = [min(P, N - P * t) for t in range(NT)]
FULL = sum(r == P for r in ROWS)
LASTROWS = ROWS[-1]
NPAD = NT * P
HF = N // 2
KD = D // 2
PATCH = 768
KP = PATCH // P

DI, DS, DCONV = 384, 16, 4
NC_I = DI // P
FF = 768
NCH = FF // P
FH = 384
NFH = FH // P
NEG = -1e30
ROUND = 1.5 * 2 ** 23
ARENA, LATE = 28000, 19848

PAIRS = B // 2
R2 = 64 + T
EXPERTS = [8, 8, 16, 8, 16]
PICKS = [2, 2, 1, 2, 3]
CHUNKS = [NCH, NCH, NCH, NCH, NFH]
CPB = 3
BUFS = 4
NBLK = [(N * PICKS[j] - EXPERTS[j]) // P + EXPERTS[j] for j in range(4)] + [(N * 3 - 15) // P + 15 + NT]
COPIES = [2, 2, 1, 2, 4]
UP_DMAS, DOWN_DMAS = [3, 1, 1, 1, 2], [1, 2, 1, 1, 2]
UP_BANKS = [2, 2, 2, 2, 1]
EMPTY = 4096
QH = 12
LH, LDK, LDV = 8, 64, 24
NPOS = 32
NREL = 2 * T - 1

CONSTS = ["ident", "before", "steps128", "iota", "row_less_empty", "shared_rows", "tok_onehot", "rev_iota", "head_mask12", "head_mask8", "khead12", "khead24", "rel_basis"]


def build(nc, io, out):
    with ExitStack() as ctx:
        def sb(name, shape, dtype=F32):
            return ctx.enter_context(nc.sbuf_tensor(name, shape, dtype))

        sems = {}

        def sem(name):
            if name not in sems:
                sems[name] = ctx.enter_context(nc.semaphore(name))
            return sems[name]

        X = sb("X", [P, NT, D])
        XN = sb("XN", [P, NT, D])
        XR = sb("XR", [P, NT, D])
        X2 = sb("X2", [P, NT, D])
        xT = sb("xT", [KD + 1, 2, N])
        xTg = sb("xTg", [KD, 2, 2, N])
        hT = sb("hT", [P, NCH, N])
        SIL = sb("SIL", [P, 2, N])
        out_rows = sb("out_rows", [P, BUFS, D])
        XGT = sb("XGT", [KD + 1, BUFS, 2, P])
        ECOLS = sb("ECOLS", [P, BUFS, 6])
        hstats = sb("hstats", [P, BUFS, 6])
        hwork = sb("hwork", [P, BUFS, 5])
        hmean = sb("hmean", [P, BUFS, 1])
        hvar = sb("hvar", [P, BUFS, 1])
        hrstd = sb("hrstd", [P, BUFS, 1])
        zeros = sb("zeros", [P, D])
        XIN = sb("XIN", [P, BUFS, D])
        stats = sb("stats", [P, NT, 6])
        meanvar = sb("meanvar", [P, NT, 2])
        var_eps = sb("var_eps", [P, NT])
        meansq = sb("meansq", [P, NT])
        rstd = sb("rstd", [P, NT])
        minus_half = sb("minus_half", [P, NT])
        ident = sb("ident", [P, P])
        arena = sb("arena", [P, ARENA])

        SC = sb("SC", [P, NT, 16])
        W1_ = sb("gate_work", [P, NT, 16])
        EQ = sb("gate_eq", [P, NT, 16])
        OH = sb("gate_onehot", [P, 3, NT, 16])
        MX = sb("gate_max", [P, 4, NT])
        TOPV = sb("gate_top", [P, 6, NT])
        COMB = sb("COMB", [P, NT, 16])
        CT = sb("combT", [16, N])
        rev = sb("rev", [P, 16])
        PW = sb("pick_weight", [P, 3, NT])
        MS = sb("picks_sum", [P, NT, 16])
        OVER = sb("over_steps", [P, 16, NT])
        RANK = sb("RANK", [P, NT, 16])
        OHR = sb("onehot_rank", [P, 3, NT, 16])
        nblk = sb("nblk", [P, 16])
        blkend = sb("blkend", [P, 16])
        blkbase = sb("blkbase", [P, 16])
        block_f = sb("block_f", [1, NBLK[4]])
        block_e = sb("block_e", [1, NBLK[4]], mybir.dt.int32)
        slot_f = sb("slot_f", [P, 3, NT])
        blk_f = sb("blk_f", [P, 3, NT])
        place_f = sb("place_f", [P, 3, NT])
        rows_of_blk = sb("rows_of_blk", [P, NBLK[4]], mybir.dt.uint32)
        shared_rows = sb("shared_rows", [P, NT], mybir.dt.int32)
        in_row = sb("in_row", [P, BUFS], mybir.dt.uint32)
        out_row = sb("out_row", [P, BUFS], mybir.dt.uint32)
        row_less_empty = sb("row_less_empty", [P, 3, NT])
        iota = sb("iota", [P, P])
        before = sb("before", [P, P])
        ones = sb("ones", [P, P])
        steps128 = sb("steps128", [P, NT])

        PH = ctx.enter_context(nc.psum_tensor("PH", [P, 4, 512], F32))
        PY = ctx.enter_context(nc.psum_tensor("PY", [P, 3, 512], F32))
        PG = ctx.enter_context(nc.psum_tensor("PG", [P, 512], F32))
        wide = [PH[:, 2 * c:2 * c + 2, :].rearrange("p a b -> p (a b)") for c in range(2)]

        def halves(buf, rows=P):
            return PH[0:rows, 2 * buf:2 * buf + 2, 0:HF]

        def two(ap):
            return ap.rearrange("p (h n) -> p h n", h=2)

        def ytile(t):
            return PY[0:ROWS[t], t // 2, (t % 2) * D:(t % 2) * D + D]

        def per_tile_groups(buf):
            full = buf[:, 0:FULL, :].rearrange("p (a b) d -> p a (b d)", b=2)
            return [(PY[:, 0:FULL // 2, 0:2 * D], full), (ytile(NT - 1), buf[0:LASTROWS, NT - 1, :])]

        loads = []

        late, early = [LATE], [24400]

        def place(name, shape, group):
            if group == 1:
                return sb(name, shape)
            n = int(np.prod(shape[1:]))
            at = late if group else early
            v = arena[0:shape[0], at[0]:at[0] + n]
            at[0] += n
            if len(shape) == 3:
                v = v.rearrange("p (a b) -> p a b", b=shape[2])
            return v

        def resident(name, shape, src, dst=None, group=0):
            buf = place(name, shape, group)
            loads.append((dst(buf) if dst else buf[:], src, group))
            return buf

        def kt(name, p, k, n):
            return io[name].rearrange("(k p) n -> p k n", p=p)

        def cols(name, p):
            return io[name]

        loads.append((ident[:], io["ident"], 0))
        loads.append((rev[:], io["rev_iota"], 0))
        loads.append((before[:], io["before"], 2))
        loads.append((steps128[:], io["steps128"], 2))
        loads.append((iota[:], io["iota"], 2))
        loads.append((row_less_empty[:], io["row_less_empty"], 2))
        loads.append((shared_rows[:], io["shared_rows"], 2))
        onehot = resident("tok_onehot_s", [T + 1, NPAD], io["tok_onehot"])
        postab = resident("postab_s", [T + 1, D], io["postab"])
        g_mamba = resident("g_mamba_s", [KD, 2], io["g_mamba"], group=1)
        w_in = resident("w_in_s", [KD, 2, 2 * DI], kt("w_in", KD, 2, 2 * DI), group=0)
        conv_w = resident("conv_w_s", [P, NC_I, DCONV], io["conv_w"], group=1)
        conv_b = resident("conv_b_s", [P, NC_I], io["conv_b"], group=1)
        w_xproj = resident("w_xproj_s", [P, NC_I, 2 * DS + 1], kt("w_xproj", P, NC_I, 33), group=1)
        w_dt = resident("w_dt_s", [2 * DS + 1, DI], io["w_dt"], dst=lambda b: b[2 * DS:2 * DS + 1, :], group=1)
        b_dt = resident("b_dt_s", [P, NC_I], io["b_dt"], group=1)
        A_log = resident("A_log_s", [P, NC_I, DS], io["A_log"], group=1)
        D_skip = resident("D_skip_s", [P, NC_I], io["D_skip"], group=1)
        w_out0 = resident("w_out0_s", [P, NC_I, D], kt("w_out", P, NC_I, D), group=1)
        g_moe = resident("g_moe_s", [KD, 2], io["g_moe"], group=2)
        gate0 = resident("gate0_s", [KD, 2, 8], kt("router0", KD, 2, 8), group=2)
        gate1 = place("gate1_s", [KD + 1, 2, 8], 2)
        loads.append((gate1[0:KD], kt("gate1", KD, 2, 8), 2))
        loads.append((gate1[KD:KD + 1, 1, :], io["gate1_b"], 2))
        b_proj = resident("b_proj_s", [8, D], io["b_proj"], group=2)
        theta = resident("theta_s", [96, 1], io["theta"], group=2)
        w_comb = resident("w_comb_s", [96, D], io["w_comb"], group=2)
        mask12 = resident("mask12_s", [3 * T, 3], io["head_mask12"], group=2)
        mask8 = resident("mask8_s", [2 * T, 2], io["head_mask8"], group=2)
        khead12 = resident("khead12_s", [96, 12], io["khead12"], group=2)
        khead24 = resident("khead24_s", [96, 6], io["khead24"], group=2)
        ln_w1 = resident("ln_w1_s", [KD, 2], io["ln_w1"], group=2)
        gate2 = resident("gate2_s", [KD, 2, 16], kt("router2", KD, 2, 16), group=2)
        norm1_w = resident("norm1_w_s", [KD, 2], io["norm1_w"], group=2)
        norm2_w = resident("norm2_w_s", [KD, 2], io["norm2_w"], group=2)
        wq = resident("wq_s", [KD, 2, LH * LDK], kt("wq", KD, 2, 512), group=2)
        wk = resident("wk_s", [KD, 2, LH * LDK], kt("wk", KD, 2, 512), group=2)
        wv = resident("wv_s", [KD, 2, D], kt("wv", KD, 2, D), group=2)
        wo = resident("wo_s", [KD, 2, D], kt("wo", KD, 2, D), group=2)
        bo = resident("bo_s", [1, D], io["bo"], group=2)
        u_par = resident("u_par_s", [P, 4], io["u_param"], group=2)
        v_par = resident("v_par_s", [P, 4], io["v_param"], group=2)
        wposT = resident("wposT_s", [NPOS, LH * LDK], io["w_posT"], group=2)
        basis = resident("basis_s", [NPOS, NREL], io["rel_basis"], group=2)
        fw1 = resident("fw1_s", [KD, 2, FH], kt("L2w1", KD, 2, FH), group=2)
        fb1 = resident("fb1_s", [P, NFH], io["L2b1"], group=2)
        fw2 = resident("fw2_s", [P, NFH, D], kt("L2w2", P, NFH, D), group=2)
        fb2 = resident("fb2_s", [1, D], io["L2b2"], group=2)
        gate3 = resident("gate3_s", [KD, 2, 8], kt("gate3", KD, 2, 8), group=2)
        wqkv = resident("wqkv_s", [KD, 2, 3 * D], kt("wqkv", KD, 2, 3 * D), group=2)
        bqk = resident("bqk_s", [KD, 4], io["bqk"], group=2)
        bv = resident("bv_s", [1, D], io["bv"], group=2)
        wo3 = resident("wo3_s", [KD, 2, D], kt("wo3", KD, 2, D), group=2)
        bo3 = resident("bo3_s", [1, D], io["bo3"], group=2)
        gate4 = place("gate4_s", [KD + 1, 2, 16], 2)
        loads.append((gate4[0:KD], kt("gate4", KD, 2, 16), 2))
        loads.append((gate4[KD:KD + 1, 1, :], io["gate4_b"], 2))
        b_fc2 = resident("b_fc2_s", [16, D], io["fc2_b"], group=2)
        ones_row = ones[0:1, :]
        NLOAD = [16 * sum(g == k for _, _, g in loads) for k in range(3)]

        def view(at, shape, rows=P):
            n = int(np.prod(shape))
            v = arena[0:rows, at:at + n]
            if len(shape) == 2:
                v = v.rearrange("p (a b) -> p a b", b=shape[1])
            elif len(shape) == 3:
                v = v.rearrange("p (a b c) -> p a b c", b=shape[1], c=shape[2])
            return v, at + n

        patches, a_ = view(0, [KP, NPAD])
        tokW, a_ = view(a_, [KP, D])
        BC, a_ = view(0, [2 * DS, N])
        DT, a_ = view(a_, [NC_I, N])
        DTX, a_ = view(a_, [NC_I, N])
        XC = hT[:, 0:NC_I, :]
        SZ = hT[:, NC_I:2 * NC_I, :]
        AN, a_ = view(a_, [NC_I, DS])
        YT, a_ = view(a_, [NC_I, N])
        PAR = xTg[0:33, 0, 0, :]
        assert a_ <= ARENA
        XS, a0 = view(0, [NC_I, B, T + 3])
        XCP, a0 = view(a0, [NC_I, N])
        SP_E, a1 = view(0, [NC_I, N])
        SP_U, a1 = view(a1, [NC_I, N])
        SP_L, a1 = view(a1, [NC_I, N])
        SP_R, a1 = view(a1, [NC_I, N])
        SP_D, a1 = view(a1, [NC_I, N])
        SP_Q, a1 = view(a1, [NC_I, N])
        assert a1 <= 2 * DS * N
        AB = SIL
        BU, a_ = view(a_, [2, N])
        HS, a_ = view(a_, [2, N])
        HC, a_ = view(a_, [2, N])
        assert a_ <= ARENA

        QT, b_ = view(0, [4, NPAD])
        KB, b_ = view(b_, [2, B, 6 * T])
        KM, _ = view(4 * NPAD, [4, B, 2 * T])
        VB, b_ = view(b_, [B, D])
        PM, b_ = view(b_, [2, QH * T])
        PTS, b_ = view(b_, [2, 512])
        OSB, b_ = view(b_, [2, D])
        OT, b_ = view(b_, [2, N])
        amax, b_ = view(b_, [2, QH])
        asum, b_ = view(b_, [2, QH])
        arinv, b_ = view(b_, [2, QH])
        CX, b2 = view(b_, [3, N], rows=96)
        QV, b2 = view(b2, [3, N], rows=P)
        cth = sb("cth", [96, 4])
        assert b2 <= LATE and late[0] <= ARENA, (b2, late)
        QV8, c_ = view(4 * NPAD + 8 * N, [4, N])
        assert c_ == 4 * NPAD + 2 * B * 6 * T
        WR, _ = view(c_, [4, 2 * NREL])
        RSB = hT.rearrange("p a n -> p (a n)")[:, 0:2 * LH * NREL].rearrange("p (a n) -> p a n", a=2)

        w_up, w_down, YK, PLACE, IN_BLK = [], [], [], [], []
        for j in range(5):
            width = [2 * FF, FF, FF, FF, FH][j]
            v_, d_ = view(0, [BUFS, 2, width], rows=KD + 1)
            w_up.append(v_)
            v_, d_ = view(d_, [BUFS, CHUNKS[j], D])
            w_down.append(v_)
            v_, _ = view(d_, [PICKS[j] * NT, P])
            PLACE.append(v_)
            v_, _ = view(d_ + PICKS[j] * NT * P, [PICKS[j] * NT, NBLK[j]])
            IN_BLK.append(v_)
            v_, d_ = view(d_, [COPIES[j], NT, D])
            YK.append(v_)
            assert d_ <= LATE
        HID = hT.rearrange("p a n -> p (a n)")[:, 0:BUFS * NCH * P].rearrange("p (s m n) -> p s m n", s=BUFS, m=NCH)
        HG, d_ = view(d_, [BUFS, FH])
        assert d_ <= LATE
        BELOW = arena[0:1, 0:NBLK[4] * 16].rearrange("p (b e) -> p b e", e=16)
        XD = nc.dram_tensor("moe_inputs", (4 * NPAD, D), F32, kind="Internal").ap()
        YD = nc.dram_tensor("moe_outputs", (4 * NPAD, D), F32, kind="Internal").ap()
        rel_dram = nc.dram_tensor("rel_scratch", (NPAD, LH * NREL), F32, kind="Internal").ap()

        FREE = 1
        COUNTED_FROM_FREE = ["scanned", "y_summed"]

        block = ctx.enter_context(nc.Block())

        chain = {"v": 0}

        def link(v, ins):
            chain["v"] += 1
            ins.then_inc(sem("v_chain"), 1)
            v.wait_ge(sem("v_chain"), chain["v"])

        def norm_v(v, n, src, dst, eps, centred):
            for t in range(NT):
                last = v.bn_stats(stats[:, t, :], src[:, t, :])
            link(v, last)
            for t in range(NT):
                last = v.bn_aggr(meanvar[:, t, :], stats[:, t, :])
            link(v, last)
            if centred:
                v.tensor_scalar(var_eps[:], meanvar[:, :, 1], eps, None, ALU.add).then_inc(sem("var_ready"), 1)
            else:
                link(v, v.tensor_tensor(meansq[:], meanvar[:, :, 0], meanvar[:, :, 0], ALU.mult))
                v.scalar_tensor_tensor(var_eps[:], meansq[:], eps, meanvar[:, :, 1], ALU.add, ALU.add)\
                    .then_inc(sem("var_ready"), 1)
            v.wait_ge(sem("rstd_ready"), n + 1)
            for t in range(NT):
                if centred:
                    last = v.tensor_scalar(dst[:, t, :], src[:, t, :], meanvar[:, t, 0:1], rstd[:, t:t + 1],
                                           ALU.subtract, ALU.mult)
                else:
                    last = v.tensor_scalar(dst[:, t, :], src[:, t, :], rstd[:, t:t + 1], None, ALU.mult)
            last.then_inc(sem("normed"), 1)

        def norm_pool(p, n):
            p.wait_ge(sem("var_ready"), n + 1)
            p.tensor_tensor(rstd[:], var_eps[:], minus_half[:], ALU.pow).then_inc(sem("rstd_ready"), 1)

        def turn_pe(pe, m, n, src):
            pe.wait_ge(sem("normed"), n + 1)
            for c in range(2):
                for t in range(NT):
                    last = pe.transpose(wide[c][0:KD, t * P:t * P + ROWS[t]], src[0:ROWS[t], t, c * KD:(c + 1) * KD],
                                        ident[0:ROWS[t], 0:ROWS[t]])
                last.then_inc(sem("turned"), 1)

        def turn_v(v, m, g=None):
            v.wait_ge(sem("turned"), 2 * m + 1)
            if g is None:
                v.tensor_copy(xT[0:KD, 0, :], wide[0][0:KD, 0:N]).then_inc(sem("xT_v"), 1)
            else:
                v.tensor_scalar(xT[0:KD, 0, :], wide[0][0:KD, 0:N], g[:, 0:1], None, ALU.mult).then_inc(sem("xT_v"), 1)

        def turn_act(act, m, g=None):
            act.wait_ge(sem("turned"), 2 * m + 2)
            act.activation(xT[0:KD, 1, :], wide[1][0:KD, 0:N], ACT.Copy,
                           scale=1.0 if g is None else g[:, 1:2]).then_inc(sem("xT_a"), 1)

        def xT_ready(eng, m):
            eng.wait_ge(sem("xT_v"), m + 1)
            eng.wait_ge(sem("xT_a"), m + 1)

        def tokens_pe(pe):
            pe.wait_ge(sem("patches_in"), 16 * 2)
            pe.wait_ge(sem("weights0"), NLOAD[0])
            for t in range(NT):
                o = PY[:, t // 2, (t % 2) * D:(t % 2) * D + D]
                for k in range(KP):
                    pe.matmul(o, patches[:, k, t * P:(t + 1) * P], tokW[:, k, :], start=(k == 0), stop=False,
                              skip_group_check=True)
                last = pe.matmul(o, onehot[:, t * P:(t + 1) * P], postab[:, :], start=False, stop=True,
                                 skip_group_check=True)
            last.then_inc(sem("tokens_ready"), 1)

        def tokens_v(v):
            v.wait_ge(sem("tokens_ready"), 1)
            v.tensor_copy(X[:, 0:FULL, :].rearrange("p (a b) d -> p a (b d)", b=2), PY[:, 0:FULL // 2, 0:2 * D])
            link(v, v.tensor_copy(X[:, NT - 1, :], PY[:, 2, 0:D]))

        def mamba_pe(pe):
            turn_pe(pe, 0, 1, XR)
            xT_ready(pe, 0)
            for q in range(2 * NC_I):
                if q in (2, 3, 4):
                    pe.wait_ge(sem("xs_moved"), q - 1)
                if q == 5:
                    pe.wait_ge(sem("z_moved"), 1)
                for h in range(2):
                    for k in range(2):
                        last = pe.matmul(PH[:, 2 * (q % 2) + h, 0:HF], w_in[:, k, q * P:(q + 1) * P],
                                         xT[0:KD, k, h * HF:(h + 1) * HF], start=(k == 0), stop=(k == 1))
                last.then_inc(sem("xz_ready"), 1)
            pe.wait_ge(sem("z_moved"), 2)
            pe.wait_ge(sem("z_moved"), 3)
            pe.wait_ge(sem("xc_ready"), NC_I)
            for h in range(2):
                for c in range(NC_I):
                    last = pe.matmul(PH[0:33, h, 0:HF], w_xproj[:, c, :], XC[:, c, h * HF:(h + 1) * HF],
                                     start=(c == 0), stop=(c == NC_I - 1))
            last.then_inc(sem("params_ready"), 1)
            pe.wait_ge(sem("params_moved"), 1)
            for c in range(NC_I):
                for h in range(2):
                    o = [PH[:, 2 + h, 0:HF], PH[:, h, 0:HF], PY[:, h, 0:HF]][c]
                    last = pe.matmul(o, w_dt[32:33, c * P:(c + 1) * P], PAR[32:33, h * HF:(h + 1) * HF],
                                     start=True, stop=True)
                last.then_inc(sem("dt_ready"), 1)
            for q in range(2 * DS):
                if q == 0:
                    pe.wait_ge(sem("dt_used"), 2 * NC_I)
                if q >= 2:
                    pe.wait_ge(sem("spread_v" if q % 2 else "spread_a"), (q - 2) // 2 + 1)
                for h in range(2):
                    last = pe.matmul(PH[:, 2 * (q % 2) + h, 0:HF], ident[0:32, q:q + 1].to_broadcast([32, P]),
                                     PAR[0:32, h * HF:(h + 1) * HF], start=True, stop=True)
                last.then_inc(sem("bc_ready"), 1)
            for c in range(NC_I):
                if c == 0:
                    pe.wait_ge(sem("spread_v"), DS)
                    pe.wait_ge(sem("spread_a"), DS)
                if c >= 2:
                    pe.wait_ge(sem("y_gated"), c - 1)
                o = [PH[:, 2 * (c % 2) + h, 0:HF] for h in range(2)]
                pe.wait_ge(sem("xd_ready"), c + 1)
                for h in range(2):
                    pe.matmul(o[h], ident[:, :], YT[:, c, h * HF:(h + 1) * HF], start=True, stop=False,
                              skip_group_check=True)
                with pe.Fori(0, DS // 2) as i:
                    for k in range(2):
                        pe.wait_ge(sem("hc_ready"), i * 2 + (c * DS + k + 1))
                        for h in range(2):
                            last = pe.matmul(o[h], ident[:, :], HC[:, k, h * HF:(h + 1) * HF], start=False, stop=True,
                                             skip_group_check=True)
                        last.then_inc(sem("y_summed"), 1)
            pe.wait_ge(sem("y_gated"), NC_I)
            for t in range(NT):
                for c in range(NC_I):
                    last = pe.matmul(ytile(t), YT[:, c, t * P:t * P + ROWS[t]], w_out0[:, c, :],
                                     start=(c == 0), stop=(c == NC_I - 1), skip_group_check=True)
            last.then_inc(sem("mamba_out"), 1)

        def mamba_v(v):
            v.wait_ge(sem("weights1"), NLOAD[1])
            norm_v(v, 0, X, XN, 1e-5, True)
            link(v, v.memset(XS[:, :, :, 0:3], 0.0))
            v.wait_ge(sem("normed"), 1)
            norm_v(v, 1, XN, XR, 1e-6, False)
            turn_v(v, 0, g_mamba)
            link(v, v.memset(AB[:, :, :], 0.0))
            for c in range(NC_I):
                v.wait_ge(sem("xz_ready"), c + 1)
                v.tensor_copy(XS[:, c, :, 3:].rearrange("p (h b) t -> p h b t", h=2),
                              halves(c % 2).rearrange("p h (b t) -> p h b t", t=T)).then_inc(sem("xs_moved"), 1)
                v.wait_ge(sem("xs_moved"), c + 1)
                xc = XCP[:, c, :].rearrange("p (b t) -> p b t", t=T)
                link(v, v.tensor_scalar(xc, XS[:, c, :, 0:T], conv_w[:, c, 0:1], None, ALU.mult))
                for k in range(1, DCONV):
                    last = v.scalar_tensor_tensor(xc, XS[:, c, :, k:k + T], conv_w[:, c, k:k + 1], xc, ALU.mult, ALU.add)
                    if k < DCONV - 1:
                        link(v, last)
                last.then_inc(sem("conv_ready"), 1)
            v.wait_ge(sem("params_ready"), 1)
            v.tensor_copy(two(PAR), halves(0, 33)).then_inc(sem("params_moved"), 1)
            v.wait_ge(sem("sp_exp"), NC_I)
            v.tensor_scalar(SP_U[:], SP_E[:], 1.0, None, ALU.add).then_inc(sem("sp_u"), 1)
            v.wait_ge(sem("sp_u"), 1)
            link(v, v.tensor_scalar(SP_D[:], SP_U[:], -1.0, None, ALU.add))
            v.wait_ge(sem("sp_ln"), 1)
            v.scalar_tensor_tensor(SP_Q[:], SP_D[:], 0.0, SP_L[:], ALU.is_equal, ALU.add)
            link(v, v.scalar_tensor_tensor(SP_U[:], SP_D[:], 0.0, SP_D[:], ALU.is_equal, ALU.add))
            link(v, v.reciprocal(SP_L[:], SP_U[:]))
            link(v, v.tensor_tensor(SP_U[:], SP_E[:], SP_L[:], ALU.mult))
            link(v, v.tensor_tensor(SP_D[:], SP_U[:], SP_Q[:], ALU.mult))
            link(v, v.tensor_tensor(DT[:], SP_D[:], SP_R[:], ALU.add))
            v.tensor_tensor(DTX[:], DT[:], XC[:], ALU.mult).then_inc(sem("dt_final"), 1)
            v.wait_ge(sem("a_exp"), 1)
            v.tensor_scalar(AN[:], AN[:], -1.0, None, ALU.mult).then_inc(sem("a_ready"), 1)
            for c in range(NC_I):
                v.tensor_scalar(YT[:, c, :], XC[:, c, :], D_skip[:, c:c + 1], None, ALU.mult).then_inc(sem("xd_ready"), 1)
            for q in range(1, 2 * DS, 2):
                v.wait_ge(sem("bc_ready"), q + 1)
                v.tensor_copy(two(BC[:, q, :]), halves(1)).then_inc(sem("spread_v"), 1)
            for c in range(NC_I):
                if c == 0:
                    v.wait_ge(sem("spread_a"), DS)
                    v.wait_ge(sem("spread_v"), DS)
                with v.Fori(0, DS // 2) as i:
                    for k in range(2):
                        q = i * 2 + (c * DS + k)
                        v.wait_ge(sem("ab_ready"), q + 1)
                        v.wait_ge(sem("bu_ready"), q + 1)
                        v.tensor_tensor_scan(HS[:, k, :], AB[:, k, :], BU[:, k, :], 0.0, ALU.mult, ALU.add)\
                            .then_inc(sem("scanned"), 1)
                        v.wait_ge(sem("scanned"), FREE + q + 1)
                        if c > 0 or k > 0:
                            v.wait_ge(sem("y_summed"), FREE + i * 2 + (c * DS + k - 1))
                        else:
                            v.wait_ge(sem("y_summed"), FREE + i * 2)
                        v.tensor_tensor(HC[:, k, :], HS[:, k, :], BC[:, bass.ds(i * 2 + (DS + k), 1), :].rearrange("p a n -> p (a n)"),
                                        ALU.mult).then_inc(sem("hc_ready"), 1)
                v.wait_ge(sem("y_summed"), FREE + (c + 1) * DS)
                v.tensor_tensor(two(YT[:, c, :]), halves(c % 2), two(SZ[:, c, :]), ALU.mult).then_inc(sem("y_gated"), 1)
            v.wait_ge(sem("mamba_out"), 1)
            for ps, xn, x2 in zip([g[0] for g in per_tile_groups(XN)], [g[1] for g in per_tile_groups(XN)],
                                  [g[1] for g in per_tile_groups(X2)]):
                last = v.tensor_tensor(x2, ps, xn, ALU.add)
            link(v, last)

        def mamba_act(act):
            act.wait_ge(sem("weights1"), NLOAD[1])
            turn_act(act, 0, g_mamba)
            act.activation(AN[:], A_log[:], ACT.Exp).then_inc(sem("a_exp"), 1)
            for c in range(NC_I):
                act.wait_ge(sem("xz_ready"), NC_I + c + 1)
                act.activation(two(SZ[:, c, :]), halves((NC_I + c) % 2), ACT.Silu).then_inc(sem("z_moved"), 1)
            for c in range(NC_I):
                act.wait_ge(sem("conv_ready"), c + 1)
                act.activation(XC[:, c, :], XCP[:, c, :], ACT.Silu, bias=conv_b[:, c:c + 1]).then_inc(sem("xc_ready"), 1)
            for c in range(NC_I):
                o = [halves(1), halves(0), PY[:, 0:2, 0:HF]][c]
                act.wait_ge(sem("dt_ready"), c + 1)
                act.activation(two(SP_U[:, c, :]), o, ACT.Abs, bias=b_dt[:, c:c + 1]).then_inc(sem("dt_used"), 1)
                act.activation(two(SP_R[:, c, :]), o, ACT.Relu, bias=b_dt[:, c:c + 1]).then_inc(sem("dt_used"), 1)
            for c in range(NC_I):
                act.wait_ge(sem("dt_used"), 2 * c + 1)
                act.activation(SP_E[:, c, :], SP_U[:, c, :], ACT.Exp, scale=-1.0).then_inc(sem("sp_exp"), 1)
            act.wait_ge(sem("sp_u"), 1)
            act.activation(SP_L[:], SP_U[:], ACT.Ln).then_inc(sem("sp_ln"), 1)
            act.wait_ge(sem("dt_final"), 1)
            for q in range(0, 2 * DS, 2):
                act.wait_ge(sem("bc_ready"), q + 1)
                act.activation(two(BC[:, q, :]), halves(0), ACT.Copy).then_inc(sem("spread_a"), 1)
            act.wait_ge(sem("a_ready"), 1)
            for c in range(NC_I):
                dt = DT[:, c, :].rearrange("p (b t) -> p b t", t=T)[:, :, 1:T]
                with act.Fori(0, DS // 2) as i:
                    for k in range(2):
                        if c > 0 or k > 0:
                            act.wait_ge(sem("scanned"), FREE + i * 2 + (c * DS + k - 1))
                        else:
                            act.wait_ge(sem("scanned"), FREE + i * 2)
                        act.activation(AB[:, k, :].rearrange("p (b t) -> p b t", t=T)[:, :, 1:T], dt, ACT.Exp,
                                       scale=AN[:, c, bass.ds(i * 2 + k, 1)]).then_inc(sem("ab_ready"), 1)

        def mamba_pool(p):
            norm_pool(p, 0)
            norm_pool(p, 1)
            p.wait_ge(sem("spread_a"), DS)
            p.wait_ge(sem("spread_v"), DS)
            for c in range(NC_I):
                with p.Fori(0, DS // 2) as i:
                    for k in range(2):
                        if c > 0 or k > 0:
                            p.wait_ge(sem("scanned"), FREE + i * 2 + (c * DS + k - 1))
                        else:
                            p.wait_ge(sem("scanned"), FREE + i * 2)
                        p.tensor_tensor(BU[:, k, :], DTX[:, c, :],
                                        BC[:, bass.ds(i * 2 + k, 1), :].rearrange("p a n -> p (a n)"),
                                        ALU.mult).then_inc(sem("bu_ready"), 1)

        SOFT_PAIR, SOFT_TOP2, SOFT_TOP1, SHARED_TOP3 = range(4)

        def gate_pe(pe, j, E, w, src, bias):
            for t in range(NT):
                for k in range(2):
                    kk = KD + 1 if bias and k == 1 else KD
                    last = pe.matmul(PG[0:ROWS[t], t * 16:t * 16 + E], src[0:kk, k, t * P:t * P + ROWS[t]],
                                     w[0:kk, k, :], start=(k == 0), stop=(k == 1), skip_group_check=True)
            last.then_inc(sem("logits"), 1)

        def gate_act(act, j, kind):
            act.wait_ge(sem("gate_shifted"), j + 1)
            if kind == SOFT_PAIR:
                act.activation(TOPV[:, 1, :], TOPV[:, 0, :], ACT.Exp).then_inc(sem("gate_exp"), 1)
            else:
                act.activation(W1_[:], W1_[:], ACT.Exp).then_inc(sem("gate_exp"), 1)

        def gate_v(v, j, E, kind):
            pg = PG[:, 0:16 * NT].rearrange("p (t e) -> p t e", e=16)
            sc, wk_, eq = SC[:, :, 0:E], W1_[:, :, 0:E], EQ[:, :, 0:E]

            def over(ap):
                return ap.unsqueeze(2).to_broadcast([P, NT, E])

            v.wait_ge(sem("logits"), j + 1)
            v.tensor_copy(SC[:, 0:FULL, 0:E], pg[:, 0:FULL, 0:E])
            link(v, v.tensor_copy(SC[0:LASTROWS, NT - 1, 0:E], pg[0:LASTROWS, NT - 1, 0:E]))
            if kind == SHARED_TOP3:
                link(v, v.memset(SC[:, :, 0:1], -1e9))
            if kind == SOFT_PAIR:
                link(v, v.tensor_copy(wk_, sc))
            else:
                link(v, v.tensor_reduce(MX[:, 3, :], sc, AX.X, ALU.max))
                v.tensor_tensor(wk_, sc, over(MX[:, 3, :]), ALU.subtract).then_inc(sem("gate_shifted"), 1)
                v.wait_ge(sem("gate_exp"), j + 1)
                link(v, v.tensor_reduce(TOPV[:, 0, :], wk_, AX.X, ALU.add))
                link(v, v.reciprocal(TOPV[:, 1, :], TOPV[:, 0, :]))
                link(v, v.tensor_tensor(wk_, wk_, over(TOPV[:, 1, :]), ALU.mult))
            if kind == SHARED_TOP3:
                link(v, v.memset(W1_[:, :, 0:1], -1.0))
            picks = {SOFT_PAIR: 2, SOFT_TOP2: 2, SOFT_TOP1: 1, SHARED_TOP3: 3}[kind]
            for r in range(picks):
                oh = OH[:, r, :, 0:E]
                link(v, v.tensor_reduce(MX[:, r, :], wk_, AX.X, ALU.max))
                link(v, v.tensor_tensor(eq, wk_, over(MX[:, r, :]), ALU.is_equal))
                link(v, v.tensor_tensor(eq, eq, rev[:, 0:E].unsqueeze(1).to_broadcast([P, NT, E]), ALU.mult))
                link(v, v.tensor_reduce(MX[:, 3, :], eq, AX.X, ALU.max))
                link(v, v.tensor_tensor(oh, eq, over(MX[:, 3, :]), ALU.is_equal))
                if r < picks - 1:
                    link(v, v.scalar_tensor_tensor(wk_, oh, NEG, wk_, ALU.mult, ALU.add))
            if kind == SOFT_PAIR:
                v.tensor_tensor(TOPV[:, 0, :], MX[:, 1, :], MX[:, 0, :], ALU.subtract).then_inc(sem("gate_shifted"), 1)
                v.wait_ge(sem("gate_exp"), j + 1)
                link(v, v.tensor_scalar(TOPV[:, 2, :], TOPV[:, 1, :], 1.0, None, ALU.add))
                link(v, v.reciprocal(PW[:, 0, :], TOPV[:, 2, :]))
                last = v.tensor_tensor(PW[:, 1, :], TOPV[:, 1, :], PW[:, 0, :], ALU.mult)
            elif kind == SOFT_TOP2:
                link(v, v.tensor_tensor(TOPV[:, 2, :], MX[:, 0, :], MX[:, 1, :], ALU.add))
                link(v, v.reciprocal(TOPV[:, 3, :], TOPV[:, 2, :]))
                v.tensor_tensor(PW[:, 0, :], MX[:, 0, :], TOPV[:, 3, :], ALU.mult)
                last = v.tensor_tensor(PW[:, 1, :], MX[:, 1, :], TOPV[:, 3, :], ALU.mult)
            else:
                last = v.tensor_copy(PW[:, 0:picks, :], MX[:, 0:picks, :])
            if j not in (1, 4):
                link(v, last)
                return
            link(v, last)
            weight = [PW[:, r, :] for r in range(picks)]
            comb = COMB[:, :, 0:E]
            last = v.tensor_tensor(comb, OH[:, 0, :, 0:E], over(weight[0]), ALU.mult)
            for r in range(1, picks):
                link(v, last)
                link(v, v.tensor_tensor(eq, OH[:, r, :, 0:E], over(weight[r]), ALU.mult))
                last = v.tensor_tensor(comb, comb, eq, ALU.add)
            if kind == SHARED_TOP3:
                link(v, last)
                last = v.tensor_scalar(COMB[:, :, 0:1], COMB[:, :, 0:1], 1.0, None, ALU.add)
            last.then_inc(sem("comb_ready"), 1)

        def outbias_pe(pe, n, j, E, bias):
            pe.wait_ge(sem("comb_ready"), n + 1)
            for t in range(NT):
                last = pe.transpose(wide[1][0:E, t * P:t * P + ROWS[t]], COMB[0:ROWS[t], t, 0:E],
                                    ident[0:ROWS[t], 0:ROWS[t]])
            last.then_inc(sem("comb_turned"), 1)
            pe.wait_ge(sem("combT_ready"), n + 1)
            for t in range(NT):
                last = pe.matmul(ytile(t), CT[0:E, t * P:t * P + ROWS[t]], bias[0:E, :], start=True, stop=True,
                                 skip_group_check=True)
            last.then_inc(sem("outbias"), 1)
            pe.wait_ge(sem("bias_added"), n + 1)

        def add_to(v, dst, other):
            for (ps, o), (_, d) in zip(per_tile_groups(other), per_tile_groups(dst)):
                last = v.tensor_tensor(d, ps, o, ALU.add)
            return last

        def outbias_v(v, n, E):
            v.wait_ge(sem("comb_turned"), n + 1)
            v.tensor_copy(CT[0:E, :], wide[1][0:E, 0:N]).then_inc(sem("combT_ready"), 1)
            v.wait_ge(sem("outbias"), n + 1)
            add_to(v, X, X).then_inc(sem("bias_added"), 1)
            v.wait_ge(sem("bias_added"), n + 1)

        def older(b, n):
            return not isinstance(b, int) or b >= n

        def blocks(eng, first, end, step):
            groups = (end - first) // BUFS
            if groups:
                with eng.Fori(0, groups) as i:
                    for k in range(BUFS):
                        step(i * BUFS + (first + k), (first + k) % BUFS)
            for b in range(first + groups * BUFS, end):
                step(b, b % BUFS)

        def arrived(eng, name, per, j, b, s):
            base = sum(16 * per[i] * ((NBLK[i] - s + BUFS - 1) // BUFS) for i in range(j))
            n = 16 * per[j]
            if isinstance(b, int):
                eng.wait_ge(sem(f"{name}{s}"), base + n * (b // BUFS + 1))
            else:
                eng.wait_ge(sem(f"{name}{s}"), (b - s) * (n // BUFS) + (base + n))

        def count_pe(pe, j, E):
            pe.wait_ge(sem("picked"), j + 1)
            pg = PG[:, 0:16 * (NT + 1)].rearrange("p (t e) -> p t e", e=16)
            m = OH[:, 0] if PICKS[j] == 1 else MS[:]
            pe.matmul(pg[:, 0:FULL, 0:E], before[:], m[:, 0:FULL, 0:E], start=True, stop=False, skip_group_check=True)
            pe.matmul(pg[:, FULL, 0:E], before[0:LASTROWS, :], m[0:LASTROWS, FULL, 0:E], start=False, stop=False,
                      skip_group_check=True)
            for d in range(1, NT):
                pe.matmul(pg[:, d:NT, 0:E], ones[:], m[:, 0:NT - d, 0:E], start=False, stop=False, skip_group_check=True)
            for t in range(NT):
                last = pe.matmul(pg[:, NT, 0:E], ones[0:ROWS[t], :], m[0:ROWS[t], t, 0:E], start=False,
                                 stop=(t == NT - 1), skip_group_check=True)
            last.then_inc(sem("counted"), 1)

        def slots_v(v, j, E):
            K, nb = PICKS[j], NBLK[j]
            if K > 1:
                last = v.tensor_tensor(MS[:, :, 0:E], OH[:, 0, :, 0:E], OH[:, 1, :, 0:E], ALU.add)
                for r in range(2, K):
                    link(v, last)
                    last = v.tensor_tensor(MS[:, :, 0:E], MS[:, :, 0:E], OH[:, r, :, 0:E], ALU.add)
                last.then_inc(sem("picked"), 1)
            else:
                v.memset(MS[:, 0, 0:1], 0.0).then_inc(sem("picked"), 1)
            v.wait_ge(sem("counted"), j + 1)
            pg = PG[:, 0:16 * (NT + 1)].rearrange("p (t e) -> p t e", e=16)
            link(v, v.tensor_tensor(OVER[:, 0:E, :], pg[:, NT, 0:E].unsqueeze(2).to_broadcast([P, E, NT]),
                                    steps128[:].unsqueeze(1).to_broadcast([P, E, NT]), ALU.is_gt))
            link(v, v.tensor_reduce(nblk[:, 0:E], OVER[:, 0:E, :], AX.X, ALU.add))
            if j == 4:
                link(v, v.memset(nblk[:, 0:1], float(NT)))
            link(v, v.tensor_tensor_scan(blkend[:, 0:E], ones[:, 0:E], nblk[:, 0:E], 0.0, ALU.mult, ALU.add))
            v.tensor_tensor(BELOW[0:1, 0:nb, 0:E], blkend[0:1, 0:E].unsqueeze(1).to_broadcast([1, nb, E]),
                            iota[0:1, 0:nb].unsqueeze(2).to_broadcast([1, nb, E]), ALU.is_le)
            link(v, v.tensor_tensor(blkbase[:, 0:E], blkend[:, 0:E], nblk[:, 0:E], ALU.subtract))
            v.tensor_reduce(block_f[0:1, 0:nb], BELOW[0:1, 0:nb, 0:E], AX.X, ALU.add)
            link(v, v.scalar_tensor_tensor(RANK[:, :, 0:E], blkbase[:, 0:E].unsqueeze(1).to_broadcast([P, NT, E]),
                                           float(P), pg[:, 0:NT, 0:E], ALU.mult, ALU.add))
            v.tensor_scalar(block_e[0:1, 0:nb], block_f[0:1, 0:nb], float(E - 1), None, ALU.min)\
                .then_inc(sem("blocks_known"), 1)
            link(v, v.tensor_tensor(OHR[:, 0:K, :, 0:E], OH[:, 0:K, :, 0:E],
                                    RANK[:, :, 0:E].unsqueeze(1).to_broadcast([P, K, NT, E]), ALU.mult))
            link(v, v.tensor_reduce(slot_f[:, 0:K, :], OHR[:, 0:K, :, 0:E], AX.X, ALU.add))
            link(v, v.tensor_scalar(blk_f[:, 0:K, :], slot_f[:, 0:K, :], 1.0 / P, -63.5 / P, ALU.mult, ALU.add))
            link(v, v.tensor_scalar(blk_f[:, 0:K, :], blk_f[:, 0:K, :], ROUND, ROUND, ALU.add, ALU.subtract))
            link(v, v.scalar_tensor_tensor(place_f[:, 0:K, :], blk_f[:, 0:K, :], -float(P), slot_f[:, 0:K, :],
                                           ALU.mult, ALU.add))
            blk, row = (a[:, 0:K, :].rearrange("p k t -> p (k t)").unsqueeze(2).to_broadcast([P, K * NT, nb])
                        for a in (blk_f, row_less_empty))
            link(v, v.tensor_tensor(IN_BLK[j][:], iota[:, 0:nb].unsqueeze(1).to_broadcast([P, K * NT, nb]), blk,
                                    ALU.is_equal))
            v.tensor_tensor(IN_BLK[j][:], IN_BLK[j][:], row, ALU.mult)
            for r in range(K):
                for t in range(NT):
                    v.tensor_scalar(PLACE[j][:, r * NT + t, :], iota[:], place_f[:, r, t:t + 1], None, ALU.is_equal)\
                        .then_inc(sem("placed"), 1)
            if j == 4:
                v.tensor_copy(rows_of_blk[:, 0:NT], shared_rows[:])
            v.wait_ge(sem("filled"), j + 1)
            v.tensor_scalar(rows_of_blk[:, first_blk(j):nb], PG[:, P + first_blk(j):P + nb], float(EMPTY), None, ALU.add)\
                .then_inc(sem("rows_known"), 1)

        def first_blk(j):
            return NT if j == 4 else 0

        def fill_pe(pe, j):
            K, nb = PICKS[j], NBLK[j]
            for q in range(K * NT):
                pe.wait_ge(sem("placed"), NT * sum(PICKS[0:j]) + q + 1)
                n = ROWS[q % NT]
                last = pe.matmul(PG[:, P:P + nb], PLACE[j][0:n, q, :], IN_BLK[j][0:n, q, :], start=(q == 0),
                                 stop=(q == K * NT - 1))
            last.then_inc(sem("filled"), 1)

        def experts_sp(sp, j, n, src, ups):
            nb, chunks = NBLK[j], CHUNKS[j]
            WU, WD = w_up[j], w_down[j]
            lag = 2 if j == 4 else 1

            def expert(b):
                return sp.value_load(block_e[0:1, bass.ds(b, 1)], min_val=0, max_val=EXPERTS[j] - 1)

            def load_cols(e, s, done):
                rows, n = io[f"m{j}_cols"].shape[1:]
                sp.dma_start(ECOLS[0:rows, s, 0:n], io[f"m{j}_cols"][bass.ds(e, 1)].rearrange("e p n -> (e p) n"))\
                    .then_inc(done, 16)

            def load_up(b, s):
                e = expert(b)
                if older(b, BUFS):
                    sp.wait_ge(sem(f"m{j}_up" if j else "m0_upb"), (b - (BUFS - 1)) * UP_BANKS[j])
                for name, at in ups:
                    n = io[name].shape[2]
                    sp.dma_start(WU[0:KD, s, :, at:at + n],
                                 io[name][bass.ds(e, 1)].rearrange("e (k p) n -> p (e k) n", p=KD))\
                        .then_inc(sem(f"up_in{s}"), 16)
                if j == 4:
                    sp.dma_start(WU[KD:KD + 1, s, 1, :], io["m4_up_b"][bass.ds(e, 1), :]).then_inc(sem(f"up_in{s}"), 16)
                if j == 0:
                    load_cols(e, s, sem(f"up_in{s}"))

            def load_down(b, s):
                e = expert(b)
                if older(b, BUFS):
                    sp.wait_ge(sem(f"m{j}_down"), b - (BUFS - 1))
                if j in (1, 4):
                    load_cols(e, s, sem(f"down_in{s}"))
                sp.dma_start(WD[:, s, :, :], io[f"m{j}_down"][bass.ds(e, 1)].rearrange("e (k p) n -> p (e k) n", p=P))\
                    .then_inc(sem(f"down_in{s}"), 16)

            def step(b, s):
                load_up(b, s)
                load_down(b - lag, (s - lag) % BUFS)

            sp.wait_ge(sem("normed"), n + 1)
            for r in range(COPIES[j]):
                sp.dma_start(XD[r * NPAD:(r + 1) * NPAD, :].rearrange("(t p) d -> p t d", p=P), src[:])\
                    .then_inc(sem("x_stored"), 16)
            sp.wait_ge(sem("blocks_known"), j + 1)
            for b in range(BUFS):
                load_up(b, b)
                if b >= lag:
                    load_down(b - lag, b - lag)
            for b in range(BUFS, BUFS + lag):
                step(b, b % BUFS)
            blocks(sp, BUFS + lag, nb, step)
            for b in range(nb - lag, nb):
                load_down(b, b % BUFS)
            for s in range(BUFS):
                last = [b for b in range(nb) if b % BUFS == s][-1]
                arrived(sp, "y_stored", [1] * 5, j, last, s)
            for r in range(COPIES[j]):
                sp.dma_start(YK[j][:, r, :, :], YD[r * NPAD:(r + 1) * NPAD, :].rearrange("(t p) d -> p t d", p=P))\
                    .then_inc(sem(f"y_back{r}"), 16)

        def experts_pool(p, j, rstd_of=None):
            nb, base = NBLK[j], sum(NBLK[0:j])

            def gather(b, s):
                p.tensor_copy(in_row[:, s:s + 1], rows_of_blk[:, bass.ds(b, 1)]).then_inc(sem("in_row"), 1)
                p.wait_ge(sem("in_row"), b + (base + 1))
                p.sem_inc(sem("waited"), 1)
                p.indirect_dma_start(out=XIN[:, s, :], out_offset=None, in_=XD[0:COPIES[j] * NPAD, :],
                                     in_offset=bass.IndirectOffsetOnAxis(in_row[:, s:s + 1], 0),
                                     bounds_check=4 * NPAD - 1, oob_is_err=False).then_inc(sem(f"rows_in{s}"), 16)

            def scatter(b, s):
                p.wait_ge(sem(f"m{j}_out"), b + 1)
                p.tensor_copy(out_row[:, s:s + 1], rows_of_blk[:, bass.ds(b, 1)]).then_inc(sem("out_row"), 1)
                p.wait_ge(sem("out_row"), b + (base + 1))
                p.sem_inc(sem("waited"), 1)
                p.indirect_dma_start(out=YD, out_offset=bass.IndirectOffsetOnAxis(out_row[:, s:s + 1], 0),
                                     in_=out_rows[:, s, :], in_offset=None,
                                     bounds_check=4 * NPAD - 1, oob_is_err=False).then_inc(sem(f"y_stored{s}"), 16)

            lead = 2 if j == 4 else 1

            def step(b, s):
                if not (isinstance(b, int) and b + lead + BUFS >= nb):
                    p.wait_ge(sem(f"m{j}_xturned"), b + (lead + 1))
                    gather(b + (lead + BUFS), (s + lead) % BUFS)
                if rstd_of and not (isinstance(b, int) and b + 2 >= nb):
                    rstd_of(b + 2, (s + 2) % BUFS)
                scatter(b, s)

            p.wait_ge(sem("x_stored"), 16 * sum(COPIES[0:j + 1]))
            p.wait_ge(sem("rows_known"), j + 1)
            if j == 0:
                p.wait_ge(sem("zeroed"), 16)
            for b in range(BUFS):
                gather(b, b)
            for b in range(BUFS, BUFS + lead):
                p.wait_ge(sem(f"m{j}_xturned"), b - (BUFS - 1))
                gather(b, b % BUFS)
                if rstd_of:
                    rstd_of(b - BUFS, b - BUFS)
            blocks(p, 0, nb - BUFS - lead, step)
            for b in range(nb - BUFS - lead, nb):
                step(b, b % BUFS)

        def combine_v(v, j):
            for r in range(PICKS[j]):
                v.wait_ge(sem(f"y_back{r}"), 16 * sum(c > r for c in COPIES[0:j + 1]))
                for t in range(NT):
                    x = X[0:ROWS[t], t, :]
                    last = v.scalar_tensor_tensor(x, YK[j][0:ROWS[t], r, t, :], PW[0:ROWS[t], r, t:t + 1], x,
                                                  ALU.mult, ALU.add)
                link(v, last)
            if j == 4:
                v.wait_ge(sem("y_back3"), 16)
                link(v, v.tensor_tensor(X[:], X[:], YK[j][:, 3, :, :], ALU.add))

        def turned_block(b):
            return (PG if b % 2 == 0 else PY[:, 2, :])[0:KD, 0:2 * P]

        def turn_block_pe(pe, j, b, s):
            arrived(pe, "rows_in", [1] * 5, j, b, s)
            if older(b, 2):
                pe.wait_ge(sem(f"m{j}_xg"), b - 1)
            for c in range(2):
                last = pe.transpose(turned_block(s)[:, c * P:(c + 1) * P], XIN[:, s, c * KD:(c + 1) * KD], ident[:, :])
            last.then_inc(sem(f"m{j}_xturned"), 1)

        def block_input(eng, j, b, s, gain):
            eng.wait_ge(sem(f"m{j}_xturned"), b + 1)
            src = turned_block(s)
            if gain is None:
                last = eng.tensor_copy(XGT[0:KD, s, :, :].rearrange("p c n -> p (c n)"), src)
            else:
                for c in range(2):
                    last = eng.tensor_scalar(XGT[0:KD, s, c, :], src[:, c * P:(c + 1) * P], gain[:, c:c + 1], None, ALU.mult)
            last.then_inc(sem(f"m{j}_xg"), 1)

        def up_bank(pe, j, bank, s, at):
            for q in range(CPB):
                for c in range(2):
                    last = pe.matmul(PH[:, bank, q * P:(q + 1) * P], w_up[j][0:KD, s, c, at + q * P:at + (q + 1) * P],
                                     XGT[0:KD, s, c, :], start=(c == 0), stop=(c == 1), skip_group_check=True)
            return last

        def down_block(pe, j, b, s, ready):
            if older(b, 2):
                pe.wait_ge(sem(f"m{j}_out"), b - 1)
            arrived(pe, "down_in", DOWN_DMAS, j, b, s)
            pe.wait_ge(sem(f"m{j}_hid"), ready)
            for m in range(CHUNKS[j]):
                last = pe.matmul(PY[:, s % 2, 0:D], HID[:, s, m, :], w_down[j][:, s, m, :], start=(m == 0),
                                 stop=(m == CHUNKS[j] - 1))
            last.then_inc(sem(f"m{j}_down"), 1)

        def out_block(v, j, b, s):
            if older(b, BUFS):
                arrived(v, "y_stored", [1] * 5, j, b - BUFS, s)
            v.wait_ge(sem(f"m{j}_down"), b + 1)
            v.tensor_copy(out_rows[:, s, :], PY[:, s % 2, 0:D])\
                .then_inc(sem(f"m{j}_out"), 1)

        def up_block(pe, j, b, s):
            arrived(pe, "up_in", UP_DMAS, j, b, s)
            pe.wait_ge(sem(f"m{j}_xg"), b + 1)
            for h in range(2):
                if older(b, 2):
                    pe.wait_ge(sem(f"m{j}_hid"), b * 2 + (h - 3))
                up_bank(pe, j, 2 * (s % 2) + h, s, h * CPB * P).then_inc(sem(f"m{j}_up"), 1)

        def experts_pe(pe, j):
            nb = NBLK[j]

            def step(b, s):
                if not (isinstance(b, int) and b + 2 >= nb):
                    turn_block_pe(pe, j, b + 2, (s + 2) % BUFS)
                if not (isinstance(b, int) and b + 1 >= nb):
                    up_block(pe, j, b + 1, (s + 1) % BUFS)
                down_block(pe, j, b, s, b * 2 + 2)

            turn_block_pe(pe, j, 0, 0)
            turn_block_pe(pe, j, 1, 1)
            up_block(pe, j, 0, 0)
            for b in range(2):
                step(b, b)
            blocks(pe, 2, nb - 2, step)
            for b in range(nb - 2, nb):
                step(b, b % BUFS)

        def experts_act(act, j, func, bias=False):
            def step(b, s):
                if bias:
                    arrived(act, "down_in", DOWN_DMAS, j, b, s)
                for h in range(2):
                    act.wait_ge(sem(f"m{j}_up"), b * 2 + (h + 1))
                    src = PH[:, 2 * (s % 2) + h, 0:CPB * P]
                    if bias:
                        for q in range(CPB):
                            m = h * CPB + q
                            last = act.activation(HID[:, s, m, :], src[:, q * P:(q + 1) * P], func,
                                                  bias=ECOLS[:, s, m:m + 1])
                    else:
                        last = act.activation(HID[:, s, h * CPB:(h + 1) * CPB, :].rearrange("p m n -> p (m n)"), src, func)
                    last.then_inc(sem(f"m{j}_hid"), 1)
            blocks(act, 0, NBLK[j], step)

        def experts_v(v, j, gain=None):
            nb = NBLK[j]

            def step(b, s):
                if not (isinstance(b, int) and b + 2 >= nb):
                    block_input(v, j, b + 2, (s + 2) % BUFS, gain)
                out_block(v, j, b, s)

            for b in range(2):
                block_input(v, j, b, b, gain)
            for b in range(BUFS):
                step(b, b)
            blocks(v, BUFS, nb - 2, step)
            for b in range(nb - 2, nb):
                step(b, b % BUFS)

        def moe0_pe(pe):
            turn_pe(pe, 1, 2, XR)
            pe.wait_ge(sem("gate0_in"), 1)
            gate_pe(pe, 0, 8, gate0, xTg[:, 1, :, :], False)
            count_pe(pe, 0, 8)
            fill_pe(pe, 0)
            nb = NBLK[0]

            def up(b, s):
                arrived(pe, "up_in", UP_DMAS, 0, b, s)
                pe.wait_ge(sem("m0_xg"), b + 1)
                for h in range(2):
                    if older(b, 1):
                        pe.wait_ge(sem("m0_silu"), b * 2 + (h - 1))
                    up_bank(pe, 0, 2 * h, s, h * CPB * P).then_inc(sem("m0_upa"), 1)
                    if older(b, 1):
                        pe.wait_ge(sem("m0_hid"), b * 2 + (h - 1))
                    up_bank(pe, 0, 2 * h + 1, s, FF + h * CPB * P).then_inc(sem("m0_upb"), 1)

            def step(b, s):
                if not (isinstance(b, int) and b + 2 >= nb):
                    turn_block_pe(pe, 0, b + 2, (s + 2) % BUFS)
                if not (isinstance(b, int) and b + 1 >= nb):
                    up(b + 1, (s + 1) % BUFS)
                down_block(pe, 0, b, s, b * 2 + 2)

            turn_block_pe(pe, 0, 0, 0)
            turn_block_pe(pe, 0, 1, 1)
            up(0, 0)
            for b in range(2):
                step(b, b)
            blocks(pe, 2, nb - 2, step)
            for b in range(nb - 2, nb):
                step(b, b % BUFS)

        def moe0_act(act):
            act.wait_ge(sem("weights2"), NLOAD[2])
            turn_act(act, 1)
            gate_act(act, 0, SOFT_PAIR)

            def step(b, s):
                for h in range(2):
                    act.wait_ge(sem("m0_upa"), b * 2 + (h + 1))
                    if older(b, 1):
                        act.wait_ge(sem("m0_hid"), b * 2 + (h - 1))
                    act.activation(SIL[:, h, 0:CPB * P], PH[:, 2 * h, 0:CPB * P], ACT.Silu).then_inc(sem("m0_silu"), 1)
            for b in range(2):
                step(b, b)
            blocks(act, 2, NBLK[0], step)

        def moe0_v(v):
            v.wait_ge(sem("weights2"), NLOAD[2])
            norm_v(v, 2, X2, XR, 1e-6, False)
            turn_v(v, 1)
            xT_ready(v, 1)
            for c in range(2):
                last = v.tensor_scalar(xTg[:, 1, c, :], xT[0:KD, c, :], g_moe[:, c:c + 1], None, ALU.mult)
            last.then_inc(sem("gate0_in"), 1)
            gate_v(v, 0, 8, SOFT_PAIR)
            slots_v(v, 0, 8)
            link(v, v.tensor_tensor(TOPV[:, 0, :], PW[:, 0, :], PW[:, 1, :], ALU.add))
            for t in range(NT):
                last = v.scalar_tensor_tensor(X[:, t, :], X2[:, t, :], TOPV[:, 0, t:t + 1], X[:, t, :], ALU.mult, ALU.add)
            link(v, last)
            nb = NBLK[0]

            def scaled_input(b, s):
                arrived(v, "up_in", UP_DMAS, 0, b, s)
                block_input(v, 0, b, s, ECOLS[0:KD, s, 0:2])

            def products(b, s):
                for h in range(2):
                    v.wait_ge(sem("m0_upb"), b * 2 + (h + 1))
                    v.wait_ge(sem("m0_silu"), b * 2 + (h + 1))
                    v.tensor_tensor(HID[:, s, h * CPB:(h + 1) * CPB, :].rearrange("p m n -> p (m n)"),
                                    PH[:, 2 * h + 1, 0:CPB * P], SIL[:, h, 0:CPB * P], ALU.mult).then_inc(sem("m0_hid"), 1)

            def step(b, s):
                if not (isinstance(b, int) and b + 2 >= nb):
                    scaled_input(b + 2, (s + 2) % BUFS)
                if not (isinstance(b, int) and b + 1 >= nb):
                    products(b + 1, (s + 1) % BUFS)
                out_block(v, 0, b, s)

            scaled_input(0, 0)
            scaled_input(1, 1)
            products(0, 0)
            for b in range(BUFS):
                step(b, b)
            blocks(v, BUFS, nb - 2, step)
            for b in range(nb - 2, nb):
                step(b, b % BUFS)
            combine_v(v, 0)

        def moe1_pe(pe):
            turn_pe(pe, 2, 3, XN)
            xT_ready(pe, 2)
            gate_pe(pe, 1, 8, gate1, xT, True)
            count_pe(pe, 1, 8)
            fill_pe(pe, 1)
            outbias_pe(pe, 0, 1, 8, b_proj)
            experts_pe(pe, 1)

        def moe1_act(act):
            turn_act(act, 2)
            gate_act(act, 1, SOFT_PAIR)
            experts_act(act, 1, ACT.Gelu_apprx_tanh, bias=True)

        def moe1_v(v):
            norm_v(v, 3, X, XN, 1e-5, True)
            turn_v(v, 2)
            gate_v(v, 1, 8, SOFT_PAIR)
            slots_v(v, 1, 8)
            outbias_v(v, 0, 8)
            experts_v(v, 1)
            combine_v(v, 1)

        def moe2_pe(pe):
            turn_pe(pe, 4, 6, XR)
            xT_ready(pe, 4)
            gate_pe(pe, 2, 16, gate2, xT, False)
            count_pe(pe, 2, 16)
            fill_pe(pe, 2)
            experts_pe(pe, 2)

        def moe2_act(act):
            turn_act(act, 4, ln_w1)
            gate_act(act, 2, SOFT_TOP1)
            experts_act(act, 2, ACT.Relu)

        def moe2_v(v):
            norm_v(v, 5, X, XN, 1e-5, True)
            v.wait_ge(sem("normed"), 6)
            norm_v(v, 6, XN, XR, 1e-6, False)
            link(v, v.tensor_tensor(X[:], X[:], XN[:], ALU.add))
            turn_v(v, 4, ln_w1)
            gate_v(v, 2, 16, SOFT_TOP1)
            slots_v(v, 2, 16)
            experts_v(v, 2, ln_w1)
            combine_v(v, 2)

        def moe3_pe(pe):
            turn_pe(pe, 7, 10, XN)
            xT_ready(pe, 7)
            gate_pe(pe, 3, 8, gate3, xT, False)
            count_pe(pe, 3, 8)
            fill_pe(pe, 3)
            experts_pe(pe, 3)

        def moe3_act(act):
            turn_act(act, 7)
            gate_act(act, 3, SOFT_TOP2)
            experts_act(act, 3, ACT.Gelu_apprx_tanh)

        def moe3_v(v):
            norm_v(v, 10, X, XN, 1e-5, True)
            turn_v(v, 7)
            gate_v(v, 3, 8, SOFT_TOP2)
            slots_v(v, 3, 8)
            experts_v(v, 3)
            combine_v(v, 3)

        def m4_up(pe, b, s):
            arrived(pe, "up_in", UP_DMAS, 4, b, s)
            pe.wait_ge(sem("m4_xg"), b + 1)
            if older(b, 2):
                pe.wait_ge(sem("m4_gelu"), b - 1)
            for c in range(2):
                kk = KD + c
                last = pe.matmul(PH[:, s % 2, 0:FH], XGT[0:kk, s, c, :], w_up[4][0:kk, s, c, :],
                                 start=(c == 0), stop=(c == 1))
            last.then_inc(sem("m4_up"), 1)

        def m4_turn(pe, b, s):
            pe.wait_ge(sem("m4_normed"), b + 1)
            if older(b, 2):
                pe.wait_ge(sem("m4_hid"), b - 1)
            for m in range(NFH):
                last = pe.transpose(PH[:, 2 + s % 2, m * P:(m + 1) * P], HG[:, s, m * P:(m + 1) * P], ident[:, :])
            last.then_inc(sem("m4_turned"), 1)

        def m4_norm(v, b, s):
            v.wait_ge(sem("m4_gelu"), b + 1)
            v.bn_stats(hstats[:, s, :], HG[:, s, :]).then_inc(sem("m4_stats"), 1)
            v.wait_ge(sem("m4_stats"), b + 1)
            half = [hstats[:, s, q:q + 1] for q in range(6)]
            v.tensor_tensor(hwork[:, s, 0:1], half[1], half[4], ALU.add)
            v.tensor_tensor(hwork[:, s, 1:2], half[1], half[4], ALU.subtract)
            v.tensor_tensor(hwork[:, s, 2:3], half[2], half[5], ALU.add).then_inc(sem("m4_sums"), 1)
            v.wait_ge(sem("m4_sums"), b + 1)
            v.tensor_scalar(hmean[:, s, :], hwork[:, s, 0:1], 0.5, None, ALU.mult)
            v.tensor_tensor(hwork[:, s, 3:4], hwork[:, s, 1:2], hwork[:, s, 1:2], ALU.mult)
            v.tensor_scalar(hwork[:, s, 4:5], hwork[:, s, 2:3], 1.0 / FH, 1e-5, ALU.mult, ALU.add)\
                .then_inc(sem("m4_scaled"), 1)
            v.wait_ge(sem("m4_scaled"), b + 1)
            v.scalar_tensor_tensor(hvar[:, s, :], hwork[:, s, 3:4], 0.25, hwork[:, s, 4:5], ALU.mult, ALU.add)\
                .then_inc(sem("m4_var"), 1)

        def m4_normalise(v, b, s):
            v.wait_ge(sem("m4_rstd"), b + 1)
            v.tensor_scalar(HG[:, s, :], HG[:, s, :], hmean[:, s, :], hrstd[:, s, :], ALU.subtract, ALU.mult)\
                .then_inc(sem("m4_normed"), 1)

        def m4_hidden(v, b, s):
            arrived(v, "down_in", DOWN_DMAS, 4, b, s)
            v.wait_ge(sem("m4_turned"), b + 1)
            for m in range(NFH):
                last = v.tensor_scalar(HID[:, s, m, :], PH[:, 2 + s % 2, m * P:(m + 1) * P], ECOLS[:, s, m:m + 1],
                                       ECOLS[:, s, NFH + m:NFH + m + 1], ALU.mult, ALU.add)
            last.then_inc(sem("m4_hid"), 1)

        def moe4_pe(pe):
            turn_pe(pe, 9, 12, XN)
            xT_ready(pe, 9)
            gate_pe(pe, 4, 16, gate4, xT, True)
            count_pe(pe, 4, 16)
            fill_pe(pe, 4)
            outbias_pe(pe, 1, 4, 16, b_fc2)
            nb = NBLK[4]

            def step(b, s):
                m4_turn(pe, b, s)
                if not (isinstance(b, int) and b + 3 >= nb):
                    turn_block_pe(pe, 4, b + 3, (s + 3) % BUFS)
                if not (isinstance(b, int) and b + 2 >= nb):
                    m4_up(pe, b + 2, (s + 2) % BUFS)
                down_block(pe, 4, b, s, b + 1)

            for b in range(3):
                turn_block_pe(pe, 4, b, b)
            m4_up(pe, 0, 0)
            m4_up(pe, 1, 1)
            for b in range(3):
                step(b, b)
            blocks(pe, 3, nb - 3, step)
            for b in range(nb - 3, nb):
                step(b, b % BUFS)

        def moe4_act(act):
            turn_act(act, 9)
            gate_act(act, 4, SHARED_TOP3)
            nb = NBLK[4]

            def input_(b, s):
                act.wait_ge(sem("m4_xturned"), b + 1)
                act.activation(XGT[0:KD, s, :, :].rearrange("p c n -> p (c n)"), turned_block(s), ACT.Copy)\
                    .then_inc(sem("m4_xg"), 1)

            def gelu(b, s):
                act.wait_ge(sem("m4_up"), b + 1)
                act.activation(HG[:, s, :], PH[:, s % 2, 0:FH], ACT.Gelu).then_inc(sem("m4_gelu"), 1)

            def step(b, s):
                if not (isinstance(b, int) and b + 3 >= nb):
                    input_(b + 3, (s + 3) % BUFS)
                if not (isinstance(b, int) and b + 2 >= nb):
                    gelu(b + 2, (s + 2) % BUFS)

            for b in range(3):
                input_(b, b)
            gelu(0, 0)
            gelu(1, 1)
            blocks(act, 0, nb - 3, step)
            step(nb - 3, (nb - 3) % BUFS)

        def moe4_v(v):
            norm_v(v, 12, X, XN, 1e-5, True)
            v.memset(XGT[KD:KD + 1, :, :, :], 1.0)
            turn_v(v, 9)
            gate_v(v, 4, 16, SHARED_TOP3)
            slots_v(v, 4, 16)
            outbias_v(v, 1, 16)
            nb = NBLK[4]

            def step(b, s):
                m4_hidden(v, b, s)
                if not (isinstance(b, int) and b + 2 >= nb):
                    m4_norm(v, b + 2, (s + 2) % BUFS)
                out_block(v, 4, b, s)
                if not (isinstance(b, int) and b + 2 >= nb):
                    m4_normalise(v, b + 2, (s + 2) % BUFS)

            for b in range(2):
                m4_norm(v, b, b)
                m4_normalise(v, b, b)
            for b in range(BUFS):
                step(b, b)
            blocks(v, BUFS, nb - 2, step)
            for b in range(nb - 2, nb):
                step(b, b % BUFS)
            combine_v(v, 4)

        def m4_rstd(p, b, s):
            p.wait_ge(sem("m4_var"), b + 1)
            p.tensor_tensor(hrstd[:, s, :], hvar[:, s, :], minus_half[:, 0:1], ALU.pow).then_inc(sem("m4_rstd"), 1)

        HEADS, HG_, DV = [12, 8, 12], [3, 2, 3], [8, 24, 16]
        ESCALE = [float(8) ** -0.5, float(LDK) ** -0.5, 1.0]
        GROUPS = 4

        def rows_of(s):
            return 64 if s == 0 else T

        def scores_pe(pe, a, p):
            if p >= 2:
                pe.wait_ge(sem("at_sub"), 8 * a + p - 1)
            S = PH[:, p % 2, :]
            for s in range(2):
                b, r = 2 * p + s, rows_of(s)
                o = S[64 * s:64 * s + r, :]
                if a == 0:
                    last = pe.matmul(o[:, 0:QH * T], QT[0:96, 0, b * T:b * T + r],
                                     KB[0:96, :, :, :].rearrange("p c b n -> p (c b n)")[:, b * QH * T:(b + 1) * QH * T],
                                     start=True, stop=True, skip_group_check=True)
                elif a == 1:
                    for c in range(4):
                        last = pe.matmul(o[:, 2 * c * T:2 * (c + 1) * T], QT[:, c, b * T:b * T + r],
                                         KM[:, c, b, :], start=True, stop=True, skip_group_check=True)
                else:
                    for c in range(2):
                        last = pe.matmul(o[:, c * 6 * T:(c + 1) * 6 * T], QT[0:96, c, b * T:b * T + r],
                                         KB[0:96, c, b, :], start=True, stop=True, skip_group_check=True)
            last.then_inc(sem("at_scores"), 1)

        def values_pe(pe, a, p):
            if p >= 1:
                pe.wait_ge(sem("at_vb"), 8 * a + p)
            hg, w = HG_[a], HEADS[a] * DV[a]
            for s in range(2):
                b = 2 * p + s
                o = PY[0:hg * T, 2, s * D:s * D + w]

                if a == 0:
                    last = pe.matmul(o, REP(a, 0)[:, b, :], ident[0:96, 0:96], start=True, stop=True,
                                     skip_group_check=True)
                else:
                    for c in range(2):
                        w_ = wv[:, c, :] if a == 1 else wqkv[:, c, 2 * D:3 * D]
                        last = pe.matmul(o, REP(a, c)[:, b, :], w_, start=(c == 0), stop=(a == 1 and c == 1),
                                         skip_group_check=True)
                    if a == 2:
                        last = pe.matmul(o, ones_row[0:1, 0:hg * T], bv[0:1, :], start=False, stop=True,
                                         skip_group_check=True)
            last.then_inc(sem("at_values"), 1)

        def turn_probs_pe(pe, a, p):
            pe.wait_ge(sem("at_exp"), 8 * a + p + 1)
            if p >= 2:
                pe.wait_ge(sem("at_pts"), 8 * a + p - 1)
            g = HG_[a] * T
            for q in range(GROUPS):
                last = pe.transpose(PH[0:g, 2 + p % 2, q * P:q * P + R2], PM[0:R2, p % 2, q * g:(q + 1) * g],
                                    ident[0:R2, 0:R2])
            last.then_inc(sem("at_pt"), 1)

        def mix_pe(pe, a, p):
            pe.wait_ge(sem("at_pts"), 8 * a + p + 1)
            pe.wait_ge(sem("at_vb"), 8 * a + p + 1)
            if p >= 2:
                pe.wait_ge(sem("at_osb"), 8 * a + p - 1)
            g, w = HG_[a] * T, HG_[a] * DV[a]
            for s in range(2):
                b, r = 2 * p + s, rows_of(s)
                for q in range(GROUPS):
                    last = pe.matmul(PY[64 * s:64 * s + r, p % 2, q * w:(q + 1) * w],
                                     PTS[0:g, p % 2, q * P + 64 * s:q * P + 64 * s + r],
                                     VB[0:g, b, q * w:(q + 1) * w], start=True, stop=True, skip_group_check=True)
            last.then_inc(sem("at_o"), 1)

        def turn_out_pe(pe, a, p):
            pe.wait_ge(sem("at_osb"), 8 * a + p + 1)
            if p >= 1:
                pe.wait_ge(sem("at_ot"), 8 * a + p)
            for c in range(1 if a == 0 else 2):
                last = pe.transpose(PG[0:96, c * P:c * P + R2], OSB[0:R2, p % 2, c * 96:(c + 1) * 96], ident[0:R2, 0:R2])
            last.then_inc(sem("at_turned"), 1)

        def REP(a, c):
            n, at = B * HG_[a] * T, 2 * LH * NREL if a == 1 else 0
            flat = hT[0:96].rearrange("p a n -> p (a n)")[:, at + c * n:at + (c + 1) * n]
            return flat.rearrange("p (b n) -> p b n", b=B)

        def repeat_act(act, a):
            for c in range(1 if a == 0 else 2):
                src = (QT[0:96, 0, 0:N] if a == 0 else xT[0:96, c, :]).rearrange("p (b j) -> p b j", j=T)
                act.activation(REP(a, c).rearrange("p b (g j) -> p b g j", j=T),
                               src.unsqueeze(2).to_broadcast([96, B, HG_[a], T]), ACT.Copy).then_inc(sem("at_rep"), 1)

        def pairs_pe(pe, a):
            pe.wait_ge(sem("at_rep"), [1, 3, 5][a])
            for p in range(PAIRS + 3):
                if p < PAIRS:
                    values_pe(pe, a, p)
                    scores_pe(pe, a, p)
                if 0 <= p - 1 < PAIRS:
                    turn_probs_pe(pe, a, p - 1)
                if 0 <= p - 2 < PAIRS:
                    mix_pe(pe, a, p - 2)
                if 0 <= p - 3 < PAIRS:
                    turn_out_pe(pe, a, p - 3)
            pe.wait_ge(sem("at_ot"), 8 * (a + 1))

        def pairs_v(v, a):
            H, hg, dv = HEADS[a], HG_[a], DV[a]
            mask = mask8 if a == 1 else mask12

            def heads(ap):
                return ap.rearrange("p (h j) -> p h j", j=T)

            def over(ap, n):
                return ap.unsqueeze(2).to_broadcast([R2, H, n])

            for p in range(PAIRS + 2):
                if p < PAIRS:
                    v.wait_ge(sem("at_values"), 8 * a + p + 1)
                    for s in range(2):
                        last = v.tensor_tensor(
                            VB[0:hg * T, 2 * p + s, 0:H * dv].rearrange("p (g h d) -> p g h d", g=GROUPS, h=hg),
                            PY[0:hg * T, 2, s * D:s * D + H * dv].rearrange("p (g h d) -> p g h d", g=GROUPS, h=hg),
                            mask[:, :].unsqueeze(1).unsqueeze(3).to_broadcast([hg * T, GROUPS, hg, dv]), ALU.mult)
                    last.then_inc(sem("at_vb"), 1)
                    v.wait_ge(sem("at_scores"), 8 * a + p + 1)
                    if p >= 2:
                        v.wait_ge(sem("at_pt"), 8 * a + p - 1)
                    S, M = PH[0:R2, p % 2, 0:H * T], PM[0:R2, p % 2, 0:H * T]
                    if a == 1:
                        v.wait_ge(sem("rel_in"), 16 * B)
                        link(v, v.tensor_tensor(M, S, RB8[0:R2, p, :], ALU.add))
                        S = M
                    link(v, v.tensor_reduce(amax[0:R2, p % 2, 0:H], heads(S), AX.X, ALU.max))
                    v.tensor_tensor(heads(M), heads(S), over(amax[0:R2, p % 2, 0:H], T), ALU.subtract)\
                        .then_inc(sem("at_sub"), 1)
                if 0 <= p - 1 < PAIRS:
                    q = p - 1
                    v.wait_ge(sem("at_exp"), 8 * a + q + 1)
                    link(v, v.tensor_reduce(asum[0:R2, q % 2, 0:H], heads(PM[0:R2, q % 2, 0:H * T]), AX.X, ALU.add))
                    link(v, v.reciprocal(arinv[0:R2, q % 2, 0:H], asum[0:R2, q % 2, 0:H]))
                if 0 <= p - 2 < PAIRS:
                    q = p - 2
                    v.wait_ge(sem("at_o"), 8 * a + q + 1)
                    if q >= 2:
                        v.wait_ge(sem("at_turned"), 8 * a + q - 1)
                    v.tensor_tensor(OSB[0:R2, q % 2, 0:H * dv].rearrange("p (h d) -> p h d", d=dv),
                                    PY[0:R2, q % 2, 0:H * dv].rearrange("p (h d) -> p h d", d=dv),
                                    over(arinv[0:R2, q % 2, 0:H], dv), ALU.mult).then_inc(sem("at_osb"), 1)

        def pairs_act(act, a):
            g, nc_ = HG_[a] * T, 1 if a == 0 else 2
            for p in range(PAIRS + 3):
                if p < PAIRS:
                    M = PM[0:R2, p % 2, 0:HEADS[a] * T]
                    act.wait_ge(sem("at_sub"), 8 * a + p + 1)
                    act.activation(M, M, ACT.Exp, scale=ESCALE[a]).then_inc(sem("at_exp"), 1)
                if 0 <= p - 1 < PAIRS:
                    q = p - 1
                    act.wait_ge(sem("at_pt"), 8 * a + q + 1)
                    if q >= 2:
                        act.wait_ge(sem("at_o"), 8 * a + q - 1)
                    act.activation(PTS[0:g, q % 2, :].rearrange("p (q r) -> p q r", q=GROUPS)[:, :, 0:R2],
                                   PH[0:g, 2 + q % 2, :].rearrange("p (q r) -> p q r", q=GROUPS)[:, :, 0:R2],
                                   ACT.Copy).then_inc(sem("at_pts"), 1)
                if 0 <= p - 3 < PAIRS:
                    q = p - 3
                    act.wait_ge(sem("at_turned"), 8 * a + q + 1)
                    for c in range(nc_):
                        last = act.activation(
                            OT[0:96, c, q * 2 * T:(q + 1) * 2 * T].rearrange("p (s j) -> p s j", s=2),
                            PG[0:96, c * P:(c + 1) * P].rearrange("p (s j) -> p s j", s=2)[:, :, 0:T], ACT.Copy)
                    last.then_inc(sem("at_ot"), 1)

        def project_pe(pe, a, w, bias):
            for t in range(NT):
                n = 1 if a == 0 else 2
                for c in range(n):
                    last = pe.matmul(ytile(t), OT[0:96, c, t * P:t * P + ROWS[t]], w[0:96, c, :] if n > 1 else w[:, :],
                                     start=(c == 0), stop=(bias is None and c == n - 1), skip_group_check=True)
                if bias is not None:
                    last = pe.matmul(ytile(t), ones_row[0:1, 0:ROWS[t]], bias[0:1, :], start=False, stop=True,
                                     skip_group_check=True)
            last.then_inc(sem("projected"), 1)

        TWO_PI = 2 * np.pi
        C1 = 6.28125
        C2 = float(np.float32(np.round((TWO_PI - C1) * 2 ** 20) / 2 ** 20))
        C3 = TWO_PI - C1 - C2
        ROUND = 1.5 * 2 ** 23
        XTH = CX.rearrange("p a n -> p (a n)")[:, 0:N + 1]
        KTH = QV.rearrange("p a n -> p (a n)")[0:96, 0:N + 1]
        SINS = QV.rearrange("p a n -> p (a n)")[0:96, N + 1:2 * N + 2]

        def cos_pe(pe):
            turn_pe(pe, 3, 4, XN)
            pe.wait_ge(sem("q_ready"), 1)
            pairs_pe(pe, 0)
            project_pe(pe, 0, w_comb, None)

        def cos_act(act):
            turn_act(act, 3)
            act.wait_ge(sem("angles"), 1)
            act.activation(SINS, XTH, ACT.Sin).then_inc(sem("sines"), 1)
            act.wait_ge(sem("q_made"), 1)
            repeat_act(act, 0)
            pairs_act(act, 0)

        def cos_v(v):
            norm_v(v, 4, X, XN, 1e-5, True)
            turn_v(v, 3)
            xT_ready(v, 3)
            v.tensor_copy(XTH[:, 0:N], xT[0:96, 0, :])
            link(v, v.tensor_copy(XTH[:, N:N + 1], theta[:, :]))
            link(v, v.tensor_scalar(KTH, XTH, 1.0 / TWO_PI, ROUND, ALU.mult, ALU.add))
            link(v, v.tensor_scalar(KTH, KTH, -ROUND, None, ALU.add))
            for cc in (C1, C2, C3):
                link(v, v.scalar_tensor_tensor(XTH, KTH, -cc, XTH, ALU.mult, ALU.add))
            link(v, v.scalar_tensor_tensor(XTH, XTH, -1.0, XTH, ALU.mult, ALU.min))
            v.tensor_scalar(XTH, XTH, np.pi / 2, None, ALU.add).then_inc(sem("angles"), 1)
            v.wait_ge(sem("sines"), 1)
            link(v, v.tensor_copy(cth[:, 0:1], SINS[:, N:N + 1]))
            v.tensor_scalar(QT[0:96, 0, 0:N], SINS[:, 0:N], cth[:, 0:1], None, ALU.mult).then_inc(sem("q_made"), 1)
            v.wait_ge(sem("q_made"), 1)
            v.tensor_tensor(KB[0:96].rearrange("p c b n -> p (c b n)").rearrange("p (b h j) -> p b h j", b=B, h=QH),
                            QT[0:96, 0, 0:N].rearrange("p (b j) -> p b j", j=T).unsqueeze(2).to_broadcast([96, B, QH, T]),
                            khead12[:, :].unsqueeze(1).unsqueeze(3).to_broadcast([96, B, QH, T]), ALU.mult)\
                .then_inc(sem("q_ready"), 1)
            pairs_v(v, 0)
            v.wait_ge(sem("projected"), 1)
            link(v, add_to(v, X, X))

        RB8, _r = view(b_, [PAIRS, LH * T])
        assert _r <= LATE

        def rel_pe(pe):
            turn_pe(pe, 5, 8, XR)
            xT_ready(pe, 5)
            for c in range(4):
                last = pe.matmul(PG[:, c * P:c * P + NREL], wposT[:, c * P:(c + 1) * P], basis[:, :], start=True, stop=True,
                                 skip_group_check=True)
            last.then_inc(sem("wr_ready"), 1)
            for q in range(8):
                w, c = (wq, wk)[q // 4], q % 4
                if q >= 2:
                    pe.wait_ge(sem("qk_moved"), q - 1)
                for h in range(2):
                    for k in range(2):
                        last = pe.matmul(PH[:, 2 * (q % 2) + h, 0:HF], w[:, k, c * P:(c + 1) * P],
                                         xT[0:KD, k, h * HF:(h + 1) * HF], start=(k == 0), stop=(k == 1))
                last.then_inc(sem("qk_ready"), 1)
            pe.wait_ge(sem("wr_moved"), 1)
            for t in range(NT):
                pe.wait_ge(sem("qk_moved"), 8)
                if t >= 2:
                    pe.wait_ge(sem("rel_moved"), t - 1)
                for c in range(4):
                    o = PH[0:ROWS[t], 2 * (t % 2) + c // 2, (c % 2) * 2 * NREL:(c % 2 + 1) * 2 * NREL]
                    last = pe.matmul(o, QV8[:, c, t * P:t * P + ROWS[t]], WR[:, c, :],
                                     start=True, stop=True, skip_group_check=True)
                last.then_inc(sem("rel_ready"), 1)
            pe.wait_ge(sem("rel_moved"), NT)
            pairs_pe(pe, 1)
            project_pe(pe, 1, wo, bo)
            turn_pe(pe, 6, 9, XR)
            xT_ready(pe, 6)
            for m in range(NFH):
                if m >= 2:
                    pe.wait_ge(sem("ffn_hid"), m - 1)
                for h in range(2):
                    for c in range(2):
                        last = pe.matmul(PH[:, 2 * (m % 2) + h, 0:HF], fw1[:, c, m * P:(m + 1) * P],
                                         xT[0:KD, c, h * HF:(h + 1) * HF], start=(c == 0), stop=(c == 1))
                last.then_inc(sem("ffn_up"), 1)
            for m in range(NFH):
                pe.wait_ge(sem("ffn_hid"), m + 1)
                for t in range(NT):
                    pe.matmul(ytile(t), hT[:, m, t * P:t * P + ROWS[t]], fw2[:, m, :], start=(m == 0 and t % 2 == 0),
                              stop=False, skip_group_check=True)
            for t in range(NT):
                last = pe.matmul(ytile(t), ones_row[0:1, 0:ROWS[t]], fb2[0:1, :], start=False, stop=True,
                                 skip_group_check=True)
            last.then_inc(sem("ffn_out"), 1)

        def rel_act(act):
            turn_act(act, 5, norm1_w)
            for q in range(4):
                act.wait_ge(sem("qk_ready"), q + 1)
                act.activation(two(QV8[:, q, 0:N]), halves(q % 2), ACT.Identity, bias=v_par[:, q:q + 1]).then_inc(sem("qv_moved"), 1)
            xT_ready(act, 5)
            repeat_act(act, 1)
            pairs_act(act, 1)
            turn_act(act, 6, norm2_w)
            for m in range(NFH):
                act.wait_ge(sem("ffn_up"), m + 1)
                act.activation(two(hT[:, m, :]), halves(m % 2), ACT.Gelu, bias=fb1[:, m:m + 1]).then_inc(sem("ffn_hid"), 1)

        def rel_v(v):
            norm_v(v, 7, X, XN, 1e-5, True)
            v.wait_ge(sem("normed"), 8)
            norm_v(v, 8, XN, XR, 1e-5, False)
            turn_v(v, 5, norm1_w)
            v.memset(KM[:], 0.0)
            v.memset(WR[:], 0.0)
            v.memset(RB8[32:64], 0.0).then_inc(sem("rel_clear"), 1)
            v.wait_ge(sem("rel_clear"), 1)
            v.wait_ge(sem("wr_ready"), 1)
            for z in range(2):
                last = v.tensor_copy(WR[64 * z:64 * z + 64, :, z * NREL:(z + 1) * NREL],
                                     PG[64 * z:64 * z + 64, :].rearrange("p (c r) -> p c r", c=4)[:, :, 0:NREL])
            last.then_inc(sem("wr_moved"), 1)
            for q in range(8):
                v.wait_ge(sem("qk_ready"), q + 1)
                if q < 4:
                    v.wait_ge(sem("qv_moved"), q + 1)
                    v.tensor_scalar(two(QT[:, q, 0:N]), halves(q % 2), u_par[:, q:q + 1], None, ALU.add).then_inc(sem("qk_moved"), 1)
                else:
                    for z in range(2):
                        last = v.tensor_copy(
                            KM[64 * z:64 * z + 64, q - 4, :, z * T:(z + 1) * T].rearrange("p (h b) j -> p h b j", h=2),
                            halves(q % 2)[64 * z:64 * z + 64].rearrange("p h (b j) -> p h b j", j=T))
                    last.then_inc(sem("qk_moved"), 1)
            for t in range(NT):
                v.wait_ge(sem("rel_ready"), t + 1)
                if t >= 2:
                    v.wait_ge(sem(f"rel_out{t % 2}"), 16 * (t // 2))
                v.tensor_copy(RSB[0:ROWS[t], t % 2, :].rearrange("p (a n) -> p a n", a=2),
                              PH[0:ROWS[t], 2 * (t % 2):2 * (t % 2) + 2, 0:4 * NREL]).then_inc(sem("rel_moved"), 1)
            pairs_v(v, 1)
            v.wait_ge(sem("projected"), 2)
            link(v, add_to(v, X2, XN))
            norm_v(v, 9, X2, XR, 1e-5, False)
            link(v, v.tensor_tensor(X[:], X[:], X2[:], ALU.add))
            turn_v(v, 6, norm2_w)
            v.wait_ge(sem("ffn_out"), 1)
            link(v, add_to(v, X, X))

        def rel_sp(sp):
            for t in range(NT):
                sp.wait_ge(sem("rel_moved"), t + 1)
                sp.dma_start(rel_dram[t * P:t * P + ROWS[t], :], RSB[0:ROWS[t], t % 2, :]).then_inc(sem(f"rel_out{t % 2}"), 16)
            sp.wait_ge(sem("rel_out0"), 16 * 3)
            sp.wait_ge(sem("rel_out1"), 16 * 2)
            sp.wait_ge(sem("rel_clear"), 1)
            for b in range(B):
                src = bass.AP(tensor=rel_dram.tensor, offset=b * T * LH * NREL + T - 1,
                              ap=[[LH * NREL - 1, T], [NREL, LH], [1, T]])
                sp.dma_start(RB8[64 * (b % 2):64 * (b % 2) + T, b // 2, :].rearrange("p (h j) -> p h j", j=T), src)\
                    .then_inc(sem("rel_in"), 16)

        def plain_pe(pe):
            turn_pe(pe, 8, 11, XN)
            xT_ready(pe, 8)
            for q in range(4):
                if q >= 2:
                    pe.wait_ge(sem("pqk_moved"), q - 1)
                for h in range(2):
                    for k in range(2):
                        last = pe.matmul(PH[0:96, 2 * (q % 2) + h, 0:HF], wqkv[:, k, q * 96:(q + 1) * 96],
                                         xT[0:KD, k, h * HF:(h + 1) * HF], start=(k == 0), stop=(k == 1))
                last.then_inc(sem("pqk_ready"), 1)
            pe.wait_ge(sem("pqk_moved"), 4)
            pairs_pe(pe, 2)
            project_pe(pe, 2, wo3, bo3)

        def plain_act(act):
            turn_act(act, 8)
            xT_ready(act, 8)
            repeat_act(act, 2)
            pairs_act(act, 2)

        def plain_v(v):
            norm_v(v, 11, X, XN, 1e-5, True)
            turn_v(v, 8)
            for q in range(4):
                v.wait_ge(sem("pqk_ready"), q + 1)
                if q < 2:
                    last = v.tensor_scalar(two(QT[0:96, q, 0:N]), halves(q % 2, 96), bqk[:, q:q + 1], float(16) ** -0.5,
                                           ALU.add, ALU.mult)
                else:
                    for h in range(6):
                        last = v.tensor_scalar(
                            KB[0:96, q - 2, :, h * T:(h + 1) * T].rearrange("p (h b) j -> p h b j", h=2),
                            halves(q % 2, 96).rearrange("p h (b j) -> p h b j", j=T),
                            bqk[:, q:q + 1], khead24[:, h:h + 1], ALU.add, ALU.mult)
                last.then_inc(sem("pqk_moved"), 1)
            pairs_v(v, 2)
            v.wait_ge(sem("projected"), 3)
            link(v, add_to(v, X, X))

        @block.sync
        def _(sp):
            sp.dma_start(patches[:], io["patches"]).then_inc(sem("patches_in"), 16)
            sp.dma_start(tokW[:], kt("tokW", P, KP, D)).then_inc(sem("patches_in"), 16)
            for group in range(3):
                if group == 2:
                    sp.wait_ge(sem("mamba_out"), 1)
                for dst, src, g in loads:
                    if g == group:
                        sp.dma_start(dst, src).then_inc(sem(f"weights{g}"), 16)
            experts_sp(sp, 0, 2, XR, [("m0_w1", 0), ("m0_w3", FF)])
            experts_sp(sp, 1, 3, XN, [("m1_up", 0)])
            experts_sp(sp, 2, 6, XR, [("m2_up", 0)])
            rel_sp(sp)
            experts_sp(sp, 3, 10, XN, [("m3_up", 0)])
            experts_sp(sp, 4, 12, XN, [("m4_up", 0)])
            sp.wait_ge(sem("done"), 1)
            sp.dma_start(out[0:FULL * P, :].rearrange("(t p) d -> p t d", p=P), X[:, 0:FULL, :]).then_inc(sem("out_written"), 16)
            sp.dma_start(out[FULL * P:N, :], X[0:LASTROWS, FULL, :]).then_inc(sem("out_written"), 16)
            sp.wait_ge(sem("out_written"), 32)

        @block.tensor
        def _(pe):
            tokens_pe(pe)
            mamba_pe(pe)
            moe0_pe(pe)
            moe1_pe(pe)
            cos_pe(pe)
            moe2_pe(pe)
            rel_pe(pe)
            moe3_pe(pe)
            plain_pe(pe)
            moe4_pe(pe)

        @block.vector
        def _(v):
            v.memset(xT[KD:KD + 1, :, :], 1.0)
            v.memset(ones[:], 1.0)
            v.memset(XIN[:], 0.0)
            v.memset(minus_half[:], -0.5)
            v.memset(X2[:, NT - 1, :], 0.0)
            link(v, v.memset(SC[:], 0.0))
            tokens_v(v)
            mamba_v(v)
            moe0_v(v)
            moe1_v(v)
            cos_v(v)
            moe2_v(v)
            rel_v(v)
            moe3_v(v)
            plain_v(v)
            moe4_v(v)
            v.memset(zeros[0:1, :], 0.0).then_inc(sem("done"), 1)

        @block.scalar
        def _(act):
            mamba_act(act)
            moe0_act(act)
            moe1_act(act)
            cos_act(act)
            moe2_act(act)
            rel_act(act)
            moe3_act(act)
            plain_act(act)
            moe4_act(act)

        @block.gpsimd
        def _(p):
            for name in COUNTED_FROM_FREE:
                p.sem_inc(sem(name), FREE)
            p.memset(zeros[:], 0.0).then_inc(sem("zeros"), 1)
            p.wait_ge(sem("zeros"), 1)
            p.dma_start(YD.rearrange("(b p) d -> p b d", p=P), zeros[:].unsqueeze(1).to_broadcast([P, 4 * NT, D]))\
                .then_inc(sem("zeroed"), 16)
            mamba_pool(p)
            norm_pool(p, 2)
            experts_pool(p, 0)
            norm_pool(p, 3)
            experts_pool(p, 1)
            norm_pool(p, 4)
            norm_pool(p, 5)
            norm_pool(p, 6)
            experts_pool(p, 2)
            norm_pool(p, 7)
            norm_pool(p, 8)
            norm_pool(p, 9)
            norm_pool(p, 10)
            experts_pool(p, 3)
            norm_pool(p, 11)
            norm_pool(p, 12)
            experts_pool(p, 4, lambda b, s: m4_rstd(p, b, s))


def prepare(i):
    f = {k: np.asarray(v) for k, v in i.items()}
    c = np.ascontiguousarray
    a = {}
    x = f["x"].reshape(B, 6, 16, 6, 16, 3).transpose(2, 4, 5, 0, 1, 3).reshape(PATCH, B, T - 1)
    pt = np.zeros((PATCH, NPAD), np.float32)
    pt[:, :N].reshape(PATCH, B, T)[:, :, 1:] = x
    a["patches"] = c(pt.reshape(KP, P, NPAD).transpose(1, 0, 2))
    a["tokW"] = f["L0_tok_W"]
    oh = np.zeros((T + 1, NPAD), np.float32)
    for n in range(N):
        oh[n % T, n] = 1
        if n % T == 0:
            oh[T, n] = 1
    a["tok_onehot"] = oh
    a["postab"] = np.concatenate([f["L0_tok_pos_emb"][0], f["L0_tok_class_emb"][0]], 0)
    a["ident"] = np.eye(P, dtype=np.float32)
    a["rev_iota"] = np.tile(np.arange(16, 0, -1, dtype=np.float32), (P, 1))
    a["before"] = np.triu(np.ones((P, P), np.float32), 1)
    a["steps128"] = np.tile(np.arange(NT, dtype=np.float32) * P, (P, 1))
    a["iota"] = np.tile(np.arange(P, dtype=np.float32), (P, 1))
    row = np.arange(4 * NPAD).reshape(4, NT, P).transpose(2, 0, 1)
    a["row_less_empty"] = (row[:, 0:3, :] - EMPTY).astype(np.float32)
    a["shared_rows"] = row[:, 3, :].astype(np.int32)
    a["head_mask12"] = np.kron(np.eye(3), np.ones((T, 1))).astype(np.float32)
    a["head_mask8"] = np.kron(np.eye(2), np.ones((T, 1))).astype(np.float32)
    a["khead12"] = np.kron(np.eye(12), np.ones((8, 1))).astype(np.float32)
    a["khead24"] = np.kron(np.eye(6), np.ones((16, 1))).astype(np.float32)
    one = np.float32
    rate = np.exp(np.log(one((T + 1) / 2.0)) / one(NPOS // 2))
    width = rate ** np.arange(1, NPOS // 2 + 1, dtype=np.float32)
    dist = np.arange(-(T - 1), T, dtype=np.float32)
    unsigned = (np.abs(dist)[None, :] <= width[:, None]).astype(np.float32)
    a["rel_basis"] = np.concatenate([unsigned, np.sign(dist)[None, :] * unsigned], 0)

    def colsof(v, p):
        return c(v.reshape(-1, p).T)

    L = "L0_attn_"
    a["g_mamba"] = colsof(f[L + "g_mamba"], KD)
    a["w_in"] = f[L + "w_in"]
    a["conv_w"] = c(f[L + "conv_w"].reshape(NC_I, P, DCONV).transpose(1, 0, 2))
    a["conv_b"] = colsof(f[L + "conv_b"], P)
    a["w_xproj"] = f[L + "w_xproj"]
    a["w_dt"] = f[L + "w_dt"]
    a["b_dt"] = colsof(f[L + "b_dt"], P)
    a["A_log"] = c(f[L + "A_log"].reshape(NC_I, P, DS).transpose(1, 0, 2))
    a["D_skip"] = colsof(f[L + "D_skip"], P)
    a["w_out"] = f[L + "w_out"]
    a["g_moe"] = colsof(f[L + "g_moe"], KD)
    a["router0"] = f[L + "w_router"]
    a["m0_cols"] = c(f[L + "g_exp"].reshape(8, 2, KD).transpose(0, 2, 1))
    a["m0_w1"], a["m0_w3"], a["m0_down"] = f[L + "w1"], f[L + "w3"], f[L + "w2"]
    L = "L0_ffn_"
    a["gate1"] = c(f[L + "gate_w"].T)
    a["gate1_b"] = f[L + "gate_b"][None]
    a["m1_cols"] = c(f[L + "b_fc"].reshape(8, NCH, P).transpose(0, 2, 1))
    a["m1_up"] = c(f[L + "w_fc"].transpose(0, 2, 1))
    a["m1_down"] = c(f[L + "w_proj"].transpose(0, 2, 1))
    a["b_proj"] = f[L + "b_proj"]
    a["theta"] = f["L1_attn_theta"][:, None]
    a["w_comb"] = c(f["L1_attn_W_combine"].T)
    a["ln_w1"] = colsof(f["L1_ffn_ln_w"], KD)
    a["router2"] = f["L1_ffn_w_router"]
    a["m2_up"], a["m2_down"] = f["L1_ffn_wi"], f["L1_ffn_wo"]
    L = "L2_attn_"
    a["norm1_w"], a["norm2_w"] = colsof(f[L + "norm1_w"], KD), colsof(f[L + "norm2_w"], KD)
    a["wq"], a["wk"], a["wv"], a["wo"] = (f[L + k] for k in ("wq", "wk", "wv", "wo"))
    a["bo"] = f[L + "bo"][None]
    a["u_param"] = colsof(f[L + "u_param"].reshape(-1), P)
    a["v_param"] = colsof(f[L + "v_param"].reshape(-1), P)
    a["w_posT"] = c(f[L + "w_pos"].reshape(LH * LDK, NPOS).T)
    a["L2w1"], a["L2w2"] = f[L + "w1"], f[L + "w2"]
    a["L2b1"] = colsof(f[L + "b1"], P)
    a["L2b2"] = f[L + "b2"][None]
    L = "L2_ffn_"
    a["gate3"] = f[L + "w_gate"]
    a["m3_up"] = c(f[L + "w_fc"].reshape(D, FF, 8).transpose(2, 0, 1))
    a["m3_down"] = c(f[L + "w_proj"].reshape(FF, D, 8).transpose(2, 0, 1))
    L = "L3_attn_"
    a["wqkv"] = c(f[L + "w_qkv"].T)
    a["bqk"] = colsof(f[L + "b_qkv"][:2 * D], KD)
    a["bv"] = f[L + "b_qkv"][None, 2 * D:]
    a["wo3"] = c(f[L + "w_out"].T)
    a["bo3"] = f[L + "b_out"][None]
    L = "L3_ffn_"
    a["gate4"] = f[L + "gate_w"]
    a["gate4_b"] = f[L + "gate_b"][None]
    a["m4_up"], a["m4_down"] = f[L + "fc1_w"], f[L + "fc2_w"]
    a["m4_up_b"] = f[L + "fc1_b"]
    a["m4_cols"] = c(np.concatenate([f[L + k].reshape(16, NFH, P) for k in ("ln_w", "ln_b")], 1).transpose(0, 2, 1))
    a["fc2_b"] = f[L + "fc2_b"]
    return {k: c(v) for k, v in a.items()}


def kernel(**inputs):
    import concourse.bacc as _bacc
    from concourse import mybir as _mybir
    from concourse.bass_utils import run_bass_kernel_spmd as _run

    nc = _bacc.Bacc("TRN2", target_bir_lowering=False, num_devices=1)
    arrays = {f"in_{k}": v for k, v in prepare(inputs).items()}
    io = {k[3:]: nc.dram_tensor(k, v.shape, _mybir.dt.from_np(v.dtype), kind="ExternalInput").ap()
          for k, v in arrays.items()}
    out = nc.dram_tensor("out_0", (N, D), F32, kind="ExternalOutput").ap()
    build(nc, io, out)
    r = _run(nc, [arrays], core_ids=[0])
    return r.results[0]["out_0"].reshape(B, T, D)
```

```python
from contextlib import ExitStack

import numpy as np

import concourse.bass as bass
from concourse import mybir

F32 = mybir.dt.float32
BF16 = mybir.dt.bfloat16
ALU = mybir.AluOpType
ACT = mybir.ActivationFunctionType
AX = mybir.AxisListType

B, T, D = 16, 37, 192
N = B * T
P = 128
NT = (N + P - 1) // P
ROWS = [min(P, N - P * t) for t in range(NT)]
FULL = sum(r == P for r in ROWS)
LASTROWS = ROWS[-1]
NPAD = NT * P
HF = N // 2
KD = D // 2
PATCH = 768
KP = PATCH // P

DI, DS, DCONV = 384, 16, 4
NC_I = DI // P
FF = 768
NCH = FF // P
FH = 384
NFH = FH // P
NEG = -1e30
WARM_TURN = [16, 16, 16, 16, 16, 16, 16, 16, 16, 16]
WARM_GATE = [8, 8, 8, 8, 8]
WARM_FILL = [10, 10, 10, 10, 10]
BIG = 1.5 * 2 ** 30
ARENA, LATE = 28000, 19848

PAIRS = B // 2
R2 = 64 + T
EXPERTS = [8, 8, 16, 8, 16]
PICKS = [2, 2, 1, 2, 3]
CHUNKS = [NCH, NCH, NCH, NCH, NFH]
CPB = 3
BUFS = 4
NBLK = [(N * PICKS[j] - EXPERTS[j]) // P + EXPERTS[j] for j in range(4)] + [(N * 3 - 15) // P + 15 + NT]
FIRST = [sum(NBLK[0:j]) for j in range(5)]
COPIES = [2, 2, 1, 2, 4]
UP_DMAS, DOWN_DMAS = [3, 1, 1, 1, 2], [1, 2, 1, 1, 2]
UP_BANKS = [2, 2, 2, 2, 1]
EMPTY = 4096
QH = 12
LH, LDK, LDV = 8, 64, 24
NPOS = 32
NREL = 2 * T - 1

CONSTS = ["ident", "before", "steps128", "iota", "own_row", "tile_no", "shared_rows", "tok_onehot", "rev_iota", "head_mask12", "head_mask8", "khead12", "khead24", "rel_basis"]


def build(nc, io, out):
    with ExitStack() as ctx:
        def sb(name, shape, dtype=F32):
            return ctx.enter_context(nc.sbuf_tensor(name, shape, dtype))

        sems = {}

        def sem(name):
            if name not in sems:
                sems[name] = ctx.enter_context(nc.semaphore(name))
            return sems[name]

        X = sb("X", [P, NT, D])
        XN = sb("XN", [P, NT, D])
        XR = sb("XR", [P, NT, D])
        X2 = sb("X2", [P, NT, D])
        xT = sb("xT", [KD + 1, 2, N])
        xTg = sb("xTg", [KD, 2, 2, N])
        hT = sb("hT", [P, NCH, N])
        SIL = sb("SIL", [P, 2, N])
        out_rows = sb("out_rows", [P, BUFS, D])
        XGT = sb("XGT", [KD + 1, BUFS, 2, P])
        ECOLS = sb("ECOLS", [P, BUFS, 6])
        hstats = sb("hstats", [P, BUFS, 6])
        hwork = sb("hwork", [P, BUFS, 5])
        hmean = sb("hmean", [P, BUFS, 1])
        hvar = sb("hvar", [P, BUFS, 1])
        hrstd = sb("hrstd", [P, BUFS, 1])
        zeros = sb("zeros", [P, D])
        XIN = sb("XIN", [P, BUFS, D])
        stats = sb("stats", [P, NT, 6])
        meanvar = sb("meanvar", [P, NT, 2])
        var_eps = sb("var_eps", [P, NT])
        meansq = sb("meansq", [P, NT])
        rstd = sb("rstd", [P, NT])
        minus_half = sb("minus_half", [P, NT])
        ident = sb("ident", [P, P])
        arena = sb("arena", [P, ARENA])

        SC = sb("SC", [P, NT, 16])
        W1_ = sb("gate_work", [P, NT, 16])
        EQ = sb("gate_eq", [P, NT, 16])
        OH = sb("gate_onehot", [P, 3, NT, 16])
        MX = sb("gate_max", [P, 4, NT])
        TOPV = sb("gate_top", [P, 6, NT])
        COMB = sb("COMB", [P, NT, 16])
        CT = sb("combT", [16, N])
        rev = sb("rev", [P, 16])
        PW = sb("pick_weight", [P, 3, NT])
        MS = sb("picks_sum", [P, NT, 16])
        OVER = sb("over_steps", [P, 16, NT])
        RANK = sb("RANK", [P, NT, 16])
        OHR = sb("onehot_rank", [P, 3, NT, 16])
        nblk = sb("nblk", [P, 16])
        blkend = sb("blkend", [P, 16])
        blkbase = sb("blkbase", [P, 16])
        block_f = sb("block_f", [1, NBLK[4]])
        block_e = sb("block_e", [1, NBLK[4]], mybir.dt.int32)
        slot_f = sb("slot_f", [P, 3, NT])
        blk_f = sb("blk_f", [P, 3, NT])
        place_f = sb("place_f", [P, 3, NT])
        rows_of_blk = sb("rows_of_blk", [P, NBLK[4]], mybir.dt.uint32)
        shared_rows = sb("shared_rows", [P, NT], mybir.dt.int32)
        low_part = sb("low_part", [P, NBLK[4]])
        in_row = sb("in_row", [P, BUFS], mybir.dt.uint32)
        out_row = sb("out_row", [P, BUFS], mybir.dt.uint32)
        own_row = sb("own_row", [P, 1])
        tile_no = sb("tile_no", [P, 3, NT])
        iota = sb("iota", [P, P])
        minus_iota = sb("minus_iota", [P, P], BF16)
        blk_start = sb("blk_start", [P, NBLK[4]])
        before = sb("before", [P, P], BF16)
        ones = sb("ones", [P, P])
        ones_b = sb("ones_b", [P, P], BF16)
        MB = sb("picks_sum_b", [P, NT, 16], BF16)
        steps128 = sb("steps128", [P, NT])

        PH = ctx.enter_context(nc.psum_tensor("PH", [P, 4, 512], F32))
        PY = ctx.enter_context(nc.psum_tensor("PY", [P, 3, 512], F32))
        PG = ctx.enter_context(nc.psum_tensor("PG", [P, 512], F32))
        wide = [PH[:, 2 * c:2 * c + 2, :].rearrange("p a b -> p (a b)") for c in range(2)]

        def halves(buf, rows=P):
            return PH[0:rows, 2 * buf:2 * buf + 2, 0:HF]

        def two(ap):
            return ap.rearrange("p (h n) -> p h n", h=2)

        def ytile(t):
            return PY[0:ROWS[t], t // 2, (t % 2) * D:(t % 2) * D + D]

        def per_tile_groups(buf):
            full = buf[:, 0:FULL, :].rearrange("p (a b) d -> p a (b d)", b=2)
            return [(PY[:, 0:FULL // 2, 0:2 * D], full), (ytile(NT - 1), buf[0:LASTROWS, NT - 1, :])]

        loads = []

        late, early = [LATE], [24400]

        def place(name, shape, group):
            if group in (1, 2):
                return sb(name, shape)
            n = int(np.prod(shape[1:]))
            at = late if group == 3 else early
            v = arena[0:shape[0], at[0]:at[0] + n]
            at[0] += n
            if len(shape) == 3:
                v = v.rearrange("p (a b) -> p a b", b=shape[2])
            return v

        def resident(name, shape, src, dst=None, group=0):
            buf = place(name, shape, group)
            loads.append((dst(buf) if dst else buf[:], src, group))
            return buf

        def kt(name, p, k, n):
            return io[name].rearrange("(k p) n -> p k n", p=p)

        def with_bias(name, n, matrix, bias, at, group):
            w = place(name, [KD + 1, 2, n], group)
            loads.append((w[0:KD], kt(matrix, KD, 2, n), group))
            loads.append((w[KD:KD + 1, 1, at], bias, group))
            return w

        def cols(name, p):
            return io[name]

        loads.append((ident[:], io["ident"], 0))
        loads.append((rev[:], io["rev_iota"], 0))
        before_f = arena[:, early[0]:early[0] + P]
        early[0] += P
        loads.append((before_f, io["before"], 0))
        loads.append((steps128[:], io["steps128"], 2))
        loads.append((iota[:], io["iota"], 2))
        loads.append((own_row[:], io["own_row"], 2))
        loads.append((tile_no[:], io["tile_no"], 2))
        loads.append((shared_rows[:], io["shared_rows"], 2))
        onehot = resident("tok_onehot_s", [T + 1, NPAD], io["tok_onehot"])
        postab = resident("postab_s", [T + 1, D], io["postab"])
        g_mamba = resident("g_mamba_s", [KD, 2], io["g_mamba"], group=1)
        w_in = resident("w_in_s", [KD, 2, 2 * DI], kt("w_in", KD, 2, 2 * DI), group=0)
        conv_w = resident("conv_w_s", [P, NC_I, DCONV], io["conv_w"], group=1)
        conv_b = resident("conv_b_s", [P, NC_I], io["conv_b"], group=1)
        w_xproj = resident("w_xproj_s", [P, NC_I, 2 * DS + 1], kt("w_xproj", P, NC_I, 33), group=1)
        w_dt = resident("w_dt_s", [2 * DS + 1, DI], io["w_dt"], dst=lambda b: b[2 * DS:2 * DS + 1, :], group=1)
        b_dt = resident("b_dt_s", [P, NC_I], io["b_dt"], group=1)
        A_log = resident("A_log_s", [P, NC_I, DS], io["A_log"], group=1)
        D_skip = resident("D_skip_s", [P, NC_I], io["D_skip"], group=1)
        w_out0 = resident("w_out0_s", [P, NC_I, D], kt("w_out", P, NC_I, D), group=1)
        g_moe = resident("g_moe_s", [KD, 2], io["g_moe"], group=2)
        gate0 = resident("gate0_s", [KD, 2, 8], kt("router0", KD, 2, 8), group=2)
        gate1 = place("gate1_s", [KD + 1, 2, 8], 2)
        loads.append((gate1[0:KD], kt("gate1", KD, 2, 8), 2))
        loads.append((gate1[KD:KD + 1, 1, :], io["gate1_b"], 2))
        b_proj = resident("b_proj_s", [8, D], io["b_proj"], group=2)
        theta = resident("theta_s", [96, 1], io["theta"], group=2)
        w_comb = resident("w_comb_s", [96, D], io["w_comb"], group=2)
        mask12 = resident("mask12_s", [3 * T, 3], io["head_mask12"], group=2)
        mask8 = resident("mask8_s", [2 * T, 2], io["head_mask8"], group=2)
        khead12 = resident("khead12_s", [96, 12], io["khead12"], group=2)
        khead24 = resident("khead24_s", [96, 6], io["khead24"], group=2)
        ln_w1 = resident("ln_w1_s", [KD, 2], io["ln_w1"], group=2)
        gate2 = resident("gate2_s", [KD, 2, 16], kt("router2", KD, 2, 16), group=2)
        norm1_w = resident("norm1_w_s", [KD, 2], io["norm1_w"], group=2)
        norm2_w = resident("norm2_w_s", [KD, 2], io["norm2_w"], group=2)
        wq = resident("wq_s", [KD, 2, LH * LDK], kt("wq", KD, 2, 512), group=2)
        wk = resident("wk_s", [KD, 2, LH * LDK], kt("wk", KD, 2, 512), group=2)
        wv = resident("wv_s", [KD, 2, D], kt("wv", KD, 2, D), group=2)
        wo = with_bias("wo_s", D, "wo", io["bo"], slice(0, D), 2)
        u_par = resident("u_par_s", [P, 4], io["u_param"], group=2)
        v_par = resident("v_par_s", [P, 4], io["v_param"], group=2)
        wposT = resident("wposT_s", [NPOS, LH * LDK], io["w_posT"], group=2)
        basis = resident("basis_s", [NPOS, NREL], io["rel_basis"], group=2)
        fw1 = resident("fw1_s", [KD, 2, FH], kt("L2w1", KD, 2, FH), group=2)
        fb1 = resident("fb1_s", [P, NFH], io["L2b1"], group=2)
        fw2 = resident("fw2_s", [P, NFH, D], kt("L2w2", P, NFH, D), group=2)
        fb2 = resident("fb2_s", [1, D], io["L2b2"], group=2)
        gate3 = resident("gate3_s", [KD, 2, 8], kt("gate3", KD, 2, 8), group=2)
        wqkv = with_bias("wqkv_s", 3 * D, "wqkv", io["bv"], slice(2 * D, 3 * D), 3)
        bqk = resident("bqk_s", [KD, 4], io["bqk"], group=2)
        bk_head = sb("bk_head", [96, 6])
        wo3 = with_bias("wo3_s", D, "wo3", io["bo3"], slice(0, D), 3)
        gate4 = place("gate4_s", [KD + 1, 2, 16], 2)
        loads.append((gate4[0:KD], kt("gate4", KD, 2, 16), 2))
        loads.append((gate4[KD:KD + 1, 1, :], io["gate4_b"], 2))
        b_fc2 = resident("b_fc2_s", [16, D], io["fc2_b"], group=2)
        ones_row = ones[0:1, :]
        NLOAD = [16 * sum(g == k for _, _, g in loads) for k in range(4)]

        def view(at, shape, rows=P):
            n = int(np.prod(shape))
            v = arena[0:rows, at:at + n]
            if len(shape) == 2:
                v = v.rearrange("p (a b) -> p a b", b=shape[1])
            elif len(shape) == 3:
                v = v.rearrange("p (a b c) -> p a b c", b=shape[1], c=shape[2])
            return v, at + n

        patches, a_ = view(0, [KP, NPAD])
        tokW, a_ = view(a_, [KP, D])
        BC, a_ = view(0, [2 * DS, N])
        DT, a_ = view(a_, [NC_I, N])
        DTX, a_ = view(a_, [NC_I, N])
        XC = hT[:, 0:NC_I, :]
        SZ = hT[:, NC_I:2 * NC_I, :]
        AN, a_ = view(a_, [NC_I, DS])
        YT, a_ = view(a_, [NC_I, N])
        PAR = xTg[0:33, 0, 0, :]
        assert a_ <= ARENA
        XS, a0 = view(0, [NC_I, B, T + 3])
        XCP, a0 = view(a0, [NC_I, N])
        AB = SIL
        SP_U, a1 = view(a_, [NC_I, N])
        SP_L, a1 = view(a1, [NC_I, N])
        SP_E, SP_D = DTX, YT
        assert a1 <= ARENA
        BU, a_ = view(a_, [2, N])
        HS, a_ = view(a_, [2, N])
        HC, a_ = view(a_, [2, N])
        assert a_ <= ARENA

        QT, b_ = view(0, [4, NPAD])
        KB, b_ = view(b_, [2, B, 6 * T])
        KM, _ = view(4 * NPAD, [4, B, 2 * T])
        VB, b_ = view(b_, [B, D])
        PM, b_ = view(b_, [2, QH * T])
        PTS, b_ = view(b_, [2, 512])
        OSB, b_ = view(b_, [2, D])
        OT, b_ = view(b_, [2, N])
        amax, b_ = view(b_, [2, QH])
        asum, b_ = view(b_, [2, QH])
        arinv, b_ = view(b_, [2, QH])
        CX, b2 = view(b_, [3, N], rows=96)
        QV, b2 = view(b2, [3, N], rows=P)
        cth = sb("cth", [96, 4])
        assert b2 <= LATE and late[0] <= ARENA, (b2, late)
        QV8, c_ = view(4 * NPAD + 8 * N, [4, N])
        assert c_ == 4 * NPAD + 2 * B * 6 * T
        WR, _ = view(c_, [4, 2 * NREL])
        RSB = hT.rearrange("p a n -> p (a n)")[:, 0:2 * LH * NREL].rearrange("p (a n) -> p a n", a=2)

        w_up, w_down, YK, PLACE, EQ_BLK, IN_BLK = [], [], [], [], [], []
        for j in range(5):
            width = [2 * FF, FF, FF, FF, FH][j]
            v_, d_ = view(0, [BUFS, 2, width], rows=KD + 1)
            w_up.append(v_)
            v_, d_ = view(d_, [BUFS, CHUNKS[j], D])
            w_down.append(v_)
            kt_ = PICKS[j] * NT
            PLACE.append(arena[:, d_:d_ + kt_ * P // 2].bitcast(BF16).rearrange("p (q n) -> p q n", n=P))
            v_, e_ = view(d_ + kt_ * P // 2, [kt_, NBLK[j]])
            EQ_BLK.append(v_)
            IN_BLK.append(arena[:, e_:e_ + kt_ * NBLK[j]].bitcast(BF16).rearrange("p (q a b) -> p q a b", a=2, b=NBLK[j]))
            assert e_ + kt_ * NBLK[j] <= d_ + COPIES[j] * NT * D
            v_, d_ = view(d_, [COPIES[j], NT, D])
            YK.append(v_)
            assert d_ <= LATE
        HID = hT.rearrange("p a n -> p (a n)")[:, 0:BUFS * NCH * P].rearrange("p (s m n) -> p s m n", s=BUFS, m=NCH)
        HG, d_ = view(d_, [BUFS, FH])
        assert d_ <= LATE
        BELOW = arena[0:1, 0:NBLK[4] * 16].rearrange("p (b e) -> p b e", e=16)
        XD = nc.dram_tensor("moe_inputs", (4 * NPAD, D), F32, kind="Internal").ap()
        YD = nc.dram_tensor("moe_outputs", (4 * NPAD, D), F32, kind="Internal").ap()
        bc_dram = nc.dram_tensor("bc_rows", (2 * DS, N), F32, kind="Internal").ap()
        rel_dram = nc.dram_tensor("rel_scratch", (NPAD, LH * NREL), F32, kind="Internal").ap()

        block = ctx.enter_context(nc.Block())

        chain = {"v": 0}

        def link(v, ins):
            chain["v"] += 1
            ins.then_inc(sem("v_chain"), 1)
            v.wait_ge(sem("v_chain"), chain["v"])

        def blocks(eng, first, end, step, bufs=BUFS):
            groups = (end - first) // bufs
            if groups:
                with eng.Fori(0, groups) as i:
                    for k in range(bufs):
                        step(i * bufs + (first + k), (first + k) % bufs)
            for b in range(first + groups * bufs, end):
                step(b, b % bufs)

        def keep_warm(pe, bank, n):
            for _ in range(n):
                pe.matmul(bank, ones_b[:], ones_b[:, 0:1].to_broadcast([P, 512]), start=True, stop=True,
                          skip_group_check=True)

        def norm_v(v, n, src, dst, eps, centred):
            for t in range(NT):
                last = v.bn_stats(stats[:, t, :], src[:, t, :])
            link(v, last)
            for t in range(NT):
                last = v.bn_aggr(meanvar[:, t, :], stats[:, t, :])
            link(v, last)
            if centred:
                v.tensor_scalar(var_eps[:], meanvar[:, :, 1], eps, None, ALU.add).then_inc(sem("var_ready"), 1)
            else:
                link(v, v.tensor_tensor(meansq[:], meanvar[:, :, 0], meanvar[:, :, 0], ALU.mult))
                v.scalar_tensor_tensor(var_eps[:], meansq[:], eps, meanvar[:, :, 1], ALU.add, ALU.add)\
                    .then_inc(sem("var_ready"), 1)
            v.wait_ge(sem("rstd_ready"), n + 1)
            for t in range(NT):
                if centred:
                    last = v.tensor_scalar(dst[:, t, :], src[:, t, :], meanvar[:, t, 0:1], rstd[:, t:t + 1],
                                           ALU.subtract, ALU.mult)
                else:
                    last = v.tensor_scalar(dst[:, t, :], src[:, t, :], rstd[:, t:t + 1], None, ALU.mult)
                last.then_inc(sem("normed"), 1)

        def norm_pool(p, n):
            p.wait_ge(sem("var_ready"), n + 1)
            p.tensor_tensor(rstd[:], var_eps[:], minus_half[:], ALU.pow).then_inc(sem("rstd_ready"), 1)

        def turn_pe(pe, m, n, src):
            keep_warm(pe, PH[:, 3, :], WARM_TURN[m])
            for t in range(NT):
                pe.wait_ge(sem("normed"), NT * n + t + 1)
                for c in range(2):
                    last = pe.transpose(wide[c][0:KD, t * P:t * P + ROWS[t]], src[0:ROWS[t], t, c * KD:(c + 1) * KD],
                                        ident[0:ROWS[t], 0:ROWS[t]])
                    if t == NT - 1:
                        last.then_inc(sem("turned"), 1)

        def turn_v(v, m, g=None):
            v.wait_ge(sem("turned"), 2 * m + 1)
            if g is None:
                v.tensor_copy(xT[0:KD, 0, :], wide[0][0:KD, 0:N]).then_inc(sem("xT_v"), 1)
            else:
                v.tensor_scalar(xT[0:KD, 0, :], wide[0][0:KD, 0:N], g[:, 0:1], None, ALU.mult).then_inc(sem("xT_v"), 1)

        def turn_act(act, m, g=None):
            act.wait_ge(sem("turned"), 2 * m + 2)
            act.activation(xT[0:KD, 1, :], wide[1][0:KD, 0:N], ACT.Copy,
                           scale=1.0 if g is None else g[:, 1:2]).then_inc(sem("xT_a"), 1)

        def xT_ready(eng, m):
            eng.wait_ge(sem("xT_v"), m + 1)
            eng.wait_ge(sem("xT_a"), m + 1)

        def tokens_pe(pe):
            def token_mm(t, lhsT, rhs, start, stop):
                return pe.matmul(PY[:, t // 2, (t % 2) * D:(t % 2) * D + D], lhsT, rhs, start=start, stop=stop,
                                 skip_group_check=True)
            for k in range(KP):
                pe.wait_ge(sem(f"patches_in{k // 2}"), 16 * 2)
                for t in range(NT):
                    token_mm(t, patches[:, k, t * P:(t + 1) * P], tokW[:, k, :], k == 0 and t % 2 == 0, False)
            pe.wait_ge(sem("weights0"), NLOAD[0])
            pe.wait_ge(sem("ones_set"), 1)
            for t in range(NT):
                last = token_mm(t, onehot[:, t * P:(t + 1) * P], postab[:, :], False, True)
            last.then_inc(sem("tokens_ready"), 1)

        def tokens_v(v):
            v.wait_ge(sem("tokens_ready"), 1)
            v.tensor_copy(before[:], before_f)
            v.tensor_copy(X[:, 0:FULL, :].rearrange("p (a b) d -> p a (b d)", b=2), PY[:, 0:FULL // 2, 0:2 * D])
            link(v, v.tensor_copy(X[:, NT - 1, :], PY[:, 2, 0:D]))

        def ysum(c):
            return halves(1 - c % 2)

        diag_D = XR.rearrange("p t d -> p (t d)")[:, 0:NC_I * P].rearrange("p (c n) -> p c n", n=P)
        DTP = [halves(1), halves(0), PY[:, 0:2, 0:HF]]

        def first_states(c, s):
            return c == 0 and isinstance(s, int) and s < 2

        def states(eng, c, end, step, bufs=2):
            if c > 0:
                blocks(eng, 0, end, step, bufs)
                return
            eng.wait_ge(sem("bc_in0"), 32)
            for s in range(2):
                step(s, s)
            blocks(eng, 2, DS // 2, step, bufs)
            eng.wait_ge(sem("bc_in1"), 32)
            blocks(eng, DS // 2, end, step, bufs)

        def mamba_sp(sp):
            sp.wait_ge(sem("params_moved"), 1)
            sp.dma_start(bc_dram, PAR[0:2 * DS, :]).then_inc(sem("bc_stored"), 16)
            sp.wait_ge(sem("bc_stored"), 16)
            for g in range(2):
                for first in (g * DS // 2, DS + g * DS // 2):
                    rows = bc_dram[first:first + DS // 2, :].unsqueeze(0).to_broadcast([P, DS // 2, N])
                    sp.dma_start(BC[:, first:first + DS // 2, :], rows).then_inc(sem(f"bc_in{g}"), 16)

        def mamba_pe(pe):
            turn_pe(pe, 0, 1, XR)
            xT_ready(pe, 0)
            for q in range(2 * NC_I):
                if q in (2, 3, 4):
                    pe.wait_ge(sem("xs_moved"), q - 1)
                if q == 5:
                    pe.wait_ge(sem("z_moved"), 1)
                for h in range(2):
                    for k in range(2):
                        last = pe.matmul(PH[:, 2 * (q % 2) + h, 0:HF], w_in[:, k, q * P:(q + 1) * P],
                                         xT[0:KD, k, h * HF:(h + 1) * HF], start=(k == 0), stop=(k == 1))
                last.then_inc(sem("xz_ready"), 1)
            pe.wait_ge(sem("z_moved"), 2)
            pe.wait_ge(sem("z_moved"), 3)
            pe.wait_ge(sem("xc_ready"), NC_I)
            for h in range(2):
                for c in range(NC_I):
                    last = pe.matmul(PH[0:33, h, 0:HF], w_xproj[:, c, :], XC[:, c, h * HF:(h + 1) * HF],
                                     start=(c == 0), stop=(c == NC_I - 1))
            last.then_inc(sem("params_ready"), 1)
            pe.wait_ge(sem("params_moved"), 1)
            for c in range(NC_I):
                for h in range(2):
                    o = [PH[:, 2 + h, 0:HF], PH[:, h, 0:HF], PY[:, h, 0:HF]][c]
                    last = pe.matmul(o, w_dt[32:33, c * P:(c + 1) * P], PAR[32:33, h * HF:(h + 1) * HF],
                                     start=True, stop=True)
                last.then_inc(sem("dt_ready"), 1)
            def mamba_out(c):
                if c == 0:
                    pe.wait_ge(sem("dt_final"), NC_I)
                pe.wait_ge(sem("y_gated"), c + 1)
                for t in range(NT):
                    last = pe.matmul(ytile(t), YT[:, c, t * P:t * P + ROWS[t]], w_out0[:, c, :],
                                     start=(c == 0 and t % 2 == 0), stop=(c == NC_I - 1), skip_group_check=True)
                if c == NC_I - 1:
                    last.then_inc(sem("mamba_out"), 1)

            pe.wait_ge(sem("diag_ready"), 1)
            for c in range(NC_I):
                if c < 2:
                    pe.wait_ge(sem("dt_final"), c + 1)
                else:
                    pe.wait_ge(sem("y_gated"), c - 1)
                o = [ysum(c)[:, h, :] for h in range(2)]
                for h in range(2):
                    pe.matmul(o[h], diag_D[:, c, :], XC[:, c, h * HF:(h + 1) * HF], start=True, stop=False,
                              skip_group_check=True)
                with pe.Fori(0, DS // 2) as i:
                    for k in range(2):
                        pe.wait_ge(sem("hc_ready"), i * 2 + (c * DS + k + 1))
                        for h in range(2):
                            last = pe.matmul(o[h], ident[:, :], HC[:, k, h * HF:(h + 1) * HF], start=False, stop=True,
                                             skip_group_check=True)
                        last.then_inc(sem("y_summed"), 1)
                if c == 1:
                    mamba_out(0)
            for c in range(1, NC_I):
                mamba_out(c)

        def mamba_v(v):
            v.wait_ge(sem("weights1"), NLOAD[1])
            norm_v(v, 0, X, XN, 1e-5, True)
            link(v, v.memset(XS[:, :, :, 0:3], 0.0))
            v.wait_ge(sem("normed"), 1 * NT)
            norm_v(v, 1, XN, XR, 1e-6, False)
            turn_v(v, 0, g_mamba)
            v.memset(AB[:, :, :], 0.0).then_inc(sem("ab_zeroed"), 1)
            for c in range(NC_I):
                v.wait_ge(sem("xz_ready"), c + 1)
                v.tensor_copy(XS[:, c, :, 3:].rearrange("p (h b) t -> p h b t", h=2),
                              halves(c % 2).rearrange("p h (b t) -> p h b t", t=T)).then_inc(sem("xs_moved"), 1)
                v.wait_ge(sem("xs_moved"), c + 1)
                xc = XCP[:, c, :].rearrange("p (b t) -> p b t", t=T)
                link(v, v.tensor_scalar(xc, XS[:, c, :, 0:T], conv_w[:, c, 0:1], None, ALU.mult))
                for k in range(1, DCONV):
                    last = v.scalar_tensor_tensor(xc, XS[:, c, :, k:k + T], conv_w[:, c, k:k + 1], xc, ALU.mult, ALU.add)
                    if k < DCONV - 1:
                        link(v, last)
                last.then_inc(sem("conv_ready"), 1)
            v.wait_ge(sem("turned"), 2)
            for c in range(NC_I):
                last = v.tensor_scalar(diag_D[:, c, :], ident[:], D_skip[:, c:c + 1], None, ALU.mult)
            last.then_inc(sem("diag_ready"), 1)
            v.wait_ge(sem("params_ready"), 1)
            v.tensor_copy(two(PAR), halves(0, 33)).then_inc(sem("params_moved"), 1)
            v.wait_ge(sem("a_exp"), 1)
            v.tensor_scalar(AN[:], AN[:], -1.0, None, ALU.mult).then_inc(sem("a_ready"), 1)
            for c in range(NC_I):
                v.wait_ge(sem("sp_exp"), c + 1)
                v.tensor_scalar(SP_U[:, c, :], SP_E[:, c, :], 1.0, None, ALU.add).then_inc(sem("sp_u"), 1)
            for c in range(NC_I):
                v.wait_ge(sem("sp_u"), c + 1)
                last = v.scalar_tensor_tensor(SP_D[:, c, :], SP_U[:, c, :], -1.0, SP_E[:, c, :], ALU.add, ALU.subtract)
            link(v, last)
            for c in range(NC_I):
                v.wait_ge(sem("sp_inverse"), c + 1)
                link(v, v.tensor_tensor(two(SP_D[:, c, :]), two(SP_D[:, c, :]), DTP[c], ALU.mult))
                link(v, v.tensor_tensor(SP_L[:, c, :], SP_L[:, c, :], SP_D[:, c, :], ALU.subtract))
                v.tensor_tensor(DT[:, c, :], SP_L[:, c, :], DT[:, c, :], ALU.add).then_inc(sem("dt_final"), 1)
            v.wait_ge(sem("dt_final"), NC_I)
            scans = [HS[:, 0, :], HS[:, 1, :], XIN.rearrange("p s d -> p (s d)")[:, 0:N],
                     out_rows.rearrange("p s d -> p (s d)")[:, 0:N]]

            def scan(c, s, k):
                q = s + c * DS
                if not (c == 0 and isinstance(s, int) and s < 4):
                    v.wait_ge(sem("hc_ready"), q - 3)
                v.wait_ge(sem("ab_ready"), q + 1)
                v.wait_ge(sem("bu_ready"), q + 1)
                v.tensor_tensor_scan(scans[k], AB[:, k % 2, :], BU[:, k % 2, :], 0.0, ALU.mult, ALU.add)\
                    .then_inc(sem("scanned"), 1)

            def times_c(c, s, k):
                q = s + c * DS
                v.wait_ge(sem("scanned"), q + 1)
                if not first_states(c, s):
                    v.wait_ge(sem("y_summed"), q - 1)
                v.tensor_tensor(HC[:, k % 2, :], scans[k], BC[:, bass.ds(s + DS, 1), :].rearrange("p a n -> p (a n)"),
                                ALU.mult).then_inc(sem("hc_ready"), 1)

            for c in range(NC_I):
                def step(s, k):
                    scan(c, s + 1, (k + 1) % 4)
                    times_c(c, s, k)

                scan(c, 0, 0)
                states(v, c, DS - 1, step, 4)
                times_c(c, DS - 1, 3)
                v.wait_ge(sem("y_summed"), (c + 1) * DS)
                v.tensor_tensor(two(YT[:, c, :]), ysum(c), two(SZ[:, c, :]), ALU.mult).then_inc(sem("y_gated"), 1)
            v.wait_ge(sem("mamba_out"), 1)
            for ps, xn, x2 in zip([g[0] for g in per_tile_groups(XN)], [g[1] for g in per_tile_groups(XN)],
                                  [g[1] for g in per_tile_groups(X2)]):
                last = v.tensor_tensor(x2, ps, xn, ALU.add)
            link(v, last)

        def mamba_act(act):
            act.wait_ge(sem("weights1"), NLOAD[1])
            turn_act(act, 0, g_mamba)
            act.activation(AN[:], A_log[:], ACT.Exp).then_inc(sem("a_exp"), 1)
            for c in range(NC_I):
                act.wait_ge(sem("conv_ready"), c + 1)
                act.activation(XC[:, c, :], XCP[:, c, :], ACT.Silu, bias=conv_b[:, c:c + 1]).then_inc(sem("xc_ready"), 1)
                act.wait_ge(sem("xz_ready"), NC_I + c + 1)
                act.activation(two(SZ[:, c, :]), halves((NC_I + c) % 2), ACT.Silu).then_inc(sem("z_moved"), 1)
            for c in range(NC_I):
                act.wait_ge(sem("dt_ready"), c + 1)
                act.activation(two(SP_U[:, c, :]), DTP[c], ACT.Abs, bias=b_dt[:, c:c + 1]).then_inc(sem("dt_abs"), 1)
                act.activation(two(DT[:, c, :]), DTP[c], ACT.Relu, bias=b_dt[:, c:c + 1])
            for c in range(NC_I):
                act.wait_ge(sem("dt_abs"), c + 1)
                act.activation(SP_E[:, c, :], SP_U[:, c, :], ACT.Exp, scale=-1.0).then_inc(sem("sp_exp"), 1)
            for c in range(NC_I):
                act.wait_ge(sem("sp_u"), c + 1)
                act.activation(SP_L[:, c, :], SP_U[:, c, :], ACT.Ln).then_inc(sem("sp_ln"), 1)
            for c in range(NC_I):
                act.wait_ge(sem("sp_ln"), c + 1)
                act.activation(DTP[c], two(SP_L[:, c, :]), ACT.Exp, scale=-1.0).then_inc(sem("sp_inverse"), 1)
            act.wait_ge(sem("a_ready"), 1)
            act.wait_ge(sem("ab_zeroed"), 1)
            for c in range(NC_I):
                act.wait_ge(sem("dt_final"), c + 1)
                dt = DT[:, c, :].rearrange("p (b t) -> p b t", t=T)[:, :, 1:T]

                def coefficient(s, k):
                    if not first_states(c, s):
                        act.wait_ge(sem("scanned"), s + (c * DS - 1))
                    act.activation(AB[:, k, :].rearrange("p (b t) -> p b t", t=T)[:, :, 1:T], dt, ACT.Exp,
                                   scale=AN[:, c, bass.ds(s, 1)]).then_inc(sem("ab_ready"), 1)
                if c == 0:
                    for s in range(2):
                        coefficient(s, s)
                blocks(act, 0 if c else 2, DS, coefficient, 2)

        def mamba_pool(p):
            norm_pool(p, 0)
            norm_pool(p, 1)
            for c in range(NC_I):
                p.wait_ge(sem("dt_final"), c + 1)
                p.tensor_tensor(DTX[:, c, :], DT[:, c, :], XC[:, c, :], ALU.mult).then_inc(sem("dtx"), 1)
                p.wait_ge(sem("dtx"), c + 1)

                def driven(s, k):
                    if not first_states(c, s):
                        p.wait_ge(sem("scanned"), s + (c * DS - 1))
                    p.tensor_tensor(BU[:, k, :], DTX[:, c, :], BC[:, bass.ds(s, 1), :].rearrange("p a n -> p (a n)"),
                                    ALU.mult).then_inc(sem("bu_ready"), 1)
                states(p, c, DS, driven)

        SOFT_PAIR, SOFT_TOP2, SOFT_TOP1, SHARED_TOP3 = range(4)

        def gate_pe(pe, j, E, w, src, bias):
            for t in range(NT):
                for k in range(2):
                    kk = KD + 1 if bias and k == 1 else KD
                    last = pe.matmul(PG[0:ROWS[t], t * 16:t * 16 + E], src[0:kk, k, t * P:t * P + ROWS[t]],
                                     w[0:kk, k, :], start=(k == 0), stop=(k == 1), skip_group_check=True)
            last.then_inc(sem("logits"), 1)

        def gate_act(act, j, kind):
            act.wait_ge(sem("gate_shifted"), j + 1)
            if kind == SOFT_PAIR:
                act.activation(TOPV[:, 1, :], TOPV[:, 0, :], ACT.Exp).then_inc(sem("gate_exp"), 1)
            else:
                act.activation(W1_[:], W1_[:], ACT.Exp).then_inc(sem("gate_exp"), 1)

        def gate_v(v, j, E, kind):
            pg = PG[:, 0:16 * NT].rearrange("p (t e) -> p t e", e=16)
            sc, wk_, eq = SC[:, :, 0:E], W1_[:, :, 0:E], EQ[:, :, 0:E]

            def over(ap):
                return ap.unsqueeze(2).to_broadcast([P, NT, E])

            v.wait_ge(sem("logits"), j + 1)
            v.tensor_copy(SC[:, 0:FULL, 0:E], pg[:, 0:FULL, 0:E])
            link(v, v.tensor_copy(SC[0:LASTROWS, NT - 1, 0:E], pg[0:LASTROWS, NT - 1, 0:E]))
            if kind == SHARED_TOP3:
                link(v, v.memset(SC[:, :, 0:1], -1e9))
            if kind == SOFT_PAIR:
                link(v, v.tensor_copy(wk_, sc))
            else:
                link(v, v.tensor_reduce(MX[:, 3, :], sc, AX.X, ALU.max))
                v.tensor_tensor(wk_, sc, over(MX[:, 3, :]), ALU.subtract).then_inc(sem("gate_shifted"), 1)
                v.wait_ge(sem("gate_exp"), j + 1)
                link(v, v.tensor_reduce(TOPV[:, 0, :], wk_, AX.X, ALU.add))
                link(v, v.reciprocal(TOPV[:, 1, :], TOPV[:, 0, :]))
                link(v, v.tensor_tensor(wk_, wk_, over(TOPV[:, 1, :]), ALU.mult))
            if kind == SHARED_TOP3:
                link(v, v.memset(W1_[:, :, 0:1], -1.0))
            picks = {SOFT_PAIR: 2, SOFT_TOP2: 2, SOFT_TOP1: 1, SHARED_TOP3: 3}[kind]
            for r in range(picks):
                oh = OH[:, r, :, 0:E]
                link(v, v.tensor_reduce(MX[:, r, :], wk_, AX.X, ALU.max))
                link(v, v.tensor_tensor(eq, wk_, over(MX[:, r, :]), ALU.is_equal))
                link(v, v.tensor_tensor(eq, eq, rev[:, 0:E].unsqueeze(1).to_broadcast([P, NT, E]), ALU.mult))
                link(v, v.tensor_reduce(MX[:, 3, :], eq, AX.X, ALU.max))
                last = v.tensor_tensor(oh, eq, over(MX[:, 3, :]), ALU.is_equal)
                if r < picks - 1:
                    link(v, last)
                    link(v, v.scalar_tensor_tensor(wk_, oh, NEG, wk_, ALU.mult, ALU.add))
            link(v, last)

        def weights_v(v, j, E, kind):
            eq, picks = EQ[:, :, 0:E], PICKS[j]

            def over(ap):
                return ap.unsqueeze(2).to_broadcast([P, NT, E])

            if kind == SOFT_PAIR:
                v.tensor_tensor(TOPV[:, 0, :], MX[:, 1, :], MX[:, 0, :], ALU.subtract).then_inc(sem("gate_shifted"), 1)
                v.wait_ge(sem("gate_exp"), j + 1)
                link(v, v.tensor_scalar(TOPV[:, 2, :], TOPV[:, 1, :], 1.0, None, ALU.add))
                link(v, v.reciprocal(PW[:, 0, :], TOPV[:, 2, :]))
                last = v.tensor_tensor(PW[:, 1, :], TOPV[:, 1, :], PW[:, 0, :], ALU.mult)
            elif kind == SOFT_TOP2:
                link(v, v.tensor_tensor(TOPV[:, 2, :], MX[:, 0, :], MX[:, 1, :], ALU.add))
                link(v, v.reciprocal(TOPV[:, 3, :], TOPV[:, 2, :]))
                v.tensor_tensor(PW[:, 0, :], MX[:, 0, :], TOPV[:, 3, :], ALU.mult)
                last = v.tensor_tensor(PW[:, 1, :], MX[:, 1, :], TOPV[:, 3, :], ALU.mult)
            else:
                last = v.tensor_copy(PW[:, 0:picks, :], MX[:, 0:picks, :])
            if j not in (1, 4):
                link(v, last)
                return
            link(v, last)
            weight = [PW[:, r, :] for r in range(picks)]
            comb = COMB[:, :, 0:E]
            last = v.tensor_tensor(comb, OH[:, 0, :, 0:E], over(weight[0]), ALU.mult)
            for r in range(1, picks):
                link(v, last)
                link(v, v.tensor_tensor(eq, OH[:, r, :, 0:E], over(weight[r]), ALU.mult))
                last = v.tensor_tensor(comb, comb, eq, ALU.add)
            if kind == SHARED_TOP3:
                link(v, last)
                last = v.tensor_scalar(COMB[:, :, 0:1], COMB[:, :, 0:1], 1.0, None, ALU.add)
            last.then_inc(sem("comb_ready"), 1)

        def outbias_pe(pe, n, j, E, bias):
            pe.wait_ge(sem("comb_ready"), n + 1)
            for t in range(NT):
                last = pe.transpose(wide[1][0:E, t * P:t * P + ROWS[t]], COMB[0:ROWS[t], t, 0:E],
                                    ident[0:ROWS[t], 0:ROWS[t]])
            last.then_inc(sem("comb_turned"), 1)
            pe.wait_ge(sem("combT_ready"), n + 1)
            for t in range(NT):
                last = pe.matmul(ytile(t), CT[0:E, t * P:t * P + ROWS[t]], bias[0:E, :], start=True, stop=True,
                                 skip_group_check=True)
            last.then_inc(sem("outbias"), 1)
            pe.wait_ge(sem("bias_added"), n + 1)

        def add_to(v, dst, other):
            for (ps, o), (_, d) in zip(per_tile_groups(other), per_tile_groups(dst)):
                last = v.tensor_tensor(d, ps, o, ALU.add)
            return last

        def outbias_v(v, n, E):
            v.wait_ge(sem("comb_turned"), n + 1)
            v.tensor_copy(CT[0:E, :], wide[1][0:E, 0:N]).then_inc(sem("combT_ready"), 1)
            v.wait_ge(sem("outbias"), n + 1)
            add_to(v, X, X).then_inc(sem("bias_added"), 1)
            v.wait_ge(sem("bias_added"), n + 1)

        def older(b, n):
            return not isinstance(b, int) or b >= n

        def arrived(eng, name, per, j, b, s):
            base = sum(16 * per[i] * ((NBLK[i] - s + BUFS - 1) // BUFS) for i in range(j))
            n = 16 * per[j]
            if isinstance(b, int):
                eng.wait_ge(sem(f"{name}{s}"), base + n * (b // BUFS + 1))
            else:
                eng.wait_ge(sem(f"{name}{s}"), (b - s) * (n // BUFS) + (base + n))

        def count_pe(pe, j, E):
            keep_warm(pe, PH[:, 3, :], WARM_GATE[j])
            pe.wait_ge(sem("picked"), j + 1)
            pg = PG[:, 0:16 * (NT + 1)].rearrange("p (t e) -> p t e", e=16)
            m = MB
            pe.matmul(pg[:, 0:FULL, 0:E], before[:], m[:, 0:FULL, 0:E], start=True, stop=False, skip_group_check=True)
            pe.matmul(pg[:, FULL, 0:E], before[0:LASTROWS, :], m[0:LASTROWS, FULL, 0:E], start=False, stop=False,
                      skip_group_check=True)
            for d in range(1, NT):
                pe.matmul(pg[:, d:NT, 0:E], ones_b[:], m[:, 0:NT - d, 0:E], start=False, stop=False, skip_group_check=True)
            for t in range(NT):
                last = pe.matmul(pg[:, NT, 0:E], ones_b[0:ROWS[t], :], m[0:ROWS[t], t, 0:E], start=False,
                                 stop=(t == NT - 1), skip_group_check=True)
            last.then_inc(sem("counted"), 1)

        def slots_v(v, j, E):
            K, nb = PICKS[j], NBLK[j]
            if K == 1:
                v.tensor_copy(MB[:, :, 0:E], OH[:, 0, :, 0:E]).then_inc(sem("picked"), 1)
            for r in range(1, K):
                a = OH[:, 0, :, 0:E] if r == 1 else MS[:, :, 0:E]
                last = v.tensor_tensor((MB if r == K - 1 else MS)[:, :, 0:E], a, OH[:, r, :, 0:E], ALU.add)
                if r == K - 1:
                    last.then_inc(sem("picked"), 1)
                else:
                    link(v, last)
            v.wait_ge(sem("counted"), j + 1)
            pg = PG[:, 0:16 * (NT + 1)].rearrange("p (t e) -> p t e", e=16)
            link(v, v.tensor_tensor(OVER[:, 0:E, :], pg[:, NT, 0:E].unsqueeze(2).to_broadcast([P, E, NT]),
                                    steps128[:].unsqueeze(1).to_broadcast([P, E, NT]), ALU.is_gt))
            link(v, v.tensor_reduce(nblk[:, 0:E], OVER[:, 0:E, :], AX.X, ALU.add))
            if j == 4:
                link(v, v.memset(nblk[:, 0:1], float(NT)))
            link(v, v.tensor_tensor_scan(blkend[:, 0:E], ones[:, 0:E], nblk[:, 0:E], 0.0, ALU.mult, ALU.add))
            v.tensor_tensor(BELOW[0:1, 0:nb, 0:E], blkend[0:1, 0:E].unsqueeze(1).to_broadcast([1, nb, E]),
                            iota[0:1, 0:nb].unsqueeze(2).to_broadcast([1, nb, E]), ALU.is_le)
            link(v, v.tensor_tensor(blkbase[:, 0:E], blkend[:, 0:E], nblk[:, 0:E], ALU.subtract))
            v.tensor_reduce(block_f[0:1, 0:nb], BELOW[0:1, 0:nb, 0:E], AX.X, ALU.add)
            link(v, v.scalar_tensor_tensor(RANK[:, :, 0:E], blkbase[:, 0:E].unsqueeze(1).to_broadcast([P, NT, E]),
                                           float(P), pg[:, 0:NT, 0:E], ALU.mult, ALU.add))
            v.tensor_scalar(block_e[0:1, 0:nb], block_f[0:1, 0:nb], float(E - 1), None, ALU.min)\
                .then_inc(sem("blocks_known"), 1)
            link(v, v.tensor_tensor(OHR[:, 0:K, :, 0:E], OH[:, 0:K, :, 0:E],
                                    RANK[:, :, 0:E].unsqueeze(1).to_broadcast([P, K, NT, E]), ALU.mult))
            link(v, v.tensor_reduce(slot_f[:, 0:K, :], OHR[:, 0:K, :, 0:E], AX.X, ALU.add))
            link(v, v.tensor_scalar(blk_f[:, 0:K, :], slot_f[:, 0:K, :], -63.5, BIG, ALU.add, ALU.add))
            v.scalar_tensor_tensor(place_f[:, 0:K, :], blk_f[:, 0:K, :], BIG, slot_f[:, 0:K, :],
                                   ALU.subtract, ALU.subtract)
            blk, tile = (a[:, 0:K, :].rearrange("p k t -> p (k t)").unsqueeze(2).to_broadcast([P, K * NT, nb])
                         for a in (blk_f, tile_no))
            link(v, v.tensor_tensor(EQ_BLK[j][:], blk_start[:, 0:nb].unsqueeze(1).to_broadcast([P, K * NT, nb]), blk,
                                    ALU.is_equal))
            v.tensor_tensor(IN_BLK[j][:, :, 0, :], EQ_BLK[j][:], tile, ALU.mult)
            v.tensor_scalar(IN_BLK[j][:, :, 1, :], EQ_BLK[j][:], own_row[:], None, ALU.mult)
            for r in range(K):
                for t in range(NT):
                    v.tensor_scalar(PLACE[j][:, r * NT + t, :], minus_iota[:], place_f[:, r, t:t + 1], None, ALU.is_equal)\
                        .then_inc(sem("placed"), 1)
            if j == 4:
                v.tensor_copy(rows_of_blk[:, 0:NT], shared_rows[:])
            v.wait_ge(sem("filled"), j + 1)
            lo = first_blk(j)
            link(v, v.tensor_scalar(low_part[:, lo:nb], PG[:, P + nb + lo:P + 2 * nb], float(EMPTY), None, ALU.add))
            v.scalar_tensor_tensor(rows_of_blk[:, lo:nb], PG[:, P + lo:P + nb], float(P), low_part[:, lo:nb],
                                   ALU.mult, ALU.add).then_inc(sem("rows_known"), 1)

        def first_blk(j):
            return NT if j == 4 else 0

        def fill_pe(pe, j):
            K, nb = PICKS[j], NBLK[j]
            for q in range(K * NT):
                pe.wait_ge(sem("placed"), NT * sum(PICKS[0:j]) + q + 1)
                n = ROWS[q % NT]
                last = pe.matmul(PG[:, P:P + 2 * nb], PLACE[j][0:n, q, :],
                                 IN_BLK[j][0:n, q, :, :].rearrange("p a b -> p (a b)"), start=(q == 0),
                                 stop=(q == K * NT - 1))
            last.then_inc(sem("filled"), 1)
            keep_warm(pe, PH[:, 3, :], WARM_FILL[j])

        def experts_sp(sp, j, n, src, ups):
            nb, chunks = NBLK[j], CHUNKS[j]
            WU, WD = w_up[j], w_down[j]
            lag = 2 if j == 4 else 1

            def expert(b):
                return sp.value_load(block_e[0:1, bass.ds(b, 1)], min_val=0, max_val=EXPERTS[j] - 1)

            def load_cols(e, s, done):
                rows, n = io[f"m{j}_cols"].shape[1:]
                sp.dma_start(ECOLS[0:rows, s, 0:n], io[f"m{j}_cols"][bass.ds(e, 1)].rearrange("e p n -> (e p) n"))\
                    .then_inc(done, 16)

            def load_up(b, s):
                e = expert(b)
                if older(b, BUFS):
                    sp.wait_ge(sem(f"m{j}_up" if j else "m0_upb"), (b - (BUFS - 1)) * UP_BANKS[j])
                for name, at in ups:
                    n = io[name].shape[2]
                    sp.dma_start(WU[0:KD, s, :, at:at + n],
                                 io[name][bass.ds(e, 1)].rearrange("e (k p) n -> p (e k) n", p=KD))\
                        .then_inc(sem(f"up_in{s}"), 16)
                if j == 4:
                    sp.dma_start(WU[KD:KD + 1, s, 1, :], io["m4_up_b"][bass.ds(e, 1), :]).then_inc(sem(f"up_in{s}"), 16)
                if j == 0:
                    load_cols(e, s, sem(f"up_in{s}"))

            def load_down(b, s):
                e = expert(b)
                if older(b, BUFS):
                    sp.wait_ge(sem("down_ready"), (b - (BUFS - 1)) + FIRST[j])
                if j in (1, 4):
                    load_cols(e, s, sem(f"down_in{s}"))
                sp.dma_start(WD[:, s, :, :], io[f"m{j}_down"][bass.ds(e, 1)].rearrange("e (k p) n -> p (e k) n", p=P))\
                    .then_inc(sem(f"down_in{s}"), 16)

            def step(b, s):
                load_up(b, s)
                load_down(b - lag, (s - lag) % BUFS)

            sp.wait_ge(sem("normed"), NT * (n + 1))
            for r in range(COPIES[j]):
                sp.dma_start(XD[r * NPAD:(r + 1) * NPAD, :].rearrange("(t p) d -> p t d", p=P), src[:])\
                    .then_inc(sem("x_stored"), 16)
            sp.wait_ge(sem("blocks_known"), j + 1)
            for b in range(BUFS):
                if b == 1:
                    arrived(sp, "rows_in", [1] * 5, j, 0, 0)
                load_up(b, b)
                if b >= lag:
                    load_down(b - lag, b - lag)
            for b in range(BUFS, BUFS + lag):
                step(b, b % BUFS)
            blocks(sp, BUFS + lag, nb, step)
            for b in range(nb - lag, nb):
                load_down(b, b % BUFS)
            for s in range(BUFS):
                last = [b for b in range(nb) if b % BUFS == s][-1]
                arrived(sp, "y_stored", [1] * 5, j, last, s)
            for r in range(COPIES[j]):
                sp.dma_start(YK[j][:, r, :, :], YD[r * NPAD:(r + 1) * NPAD, :].rearrange("(t p) d -> p t d", p=P))\
                    .then_inc(sem(f"y_back{r}"), 16)

        def experts_pool(p, j, rstd_of=None):
            nb, base = NBLK[j], FIRST[j]

            def gather(b, s):
                p.tensor_copy(in_row[:, s:s + 1], rows_of_blk[:, bass.ds(b, 1)]).then_inc(sem("in_row"), 1)
                p.wait_ge(sem("in_row"), b + (base + 1))
                p.sem_inc(sem("waited"), 1)
                p.indirect_dma_start(out=XIN[:, s, :], out_offset=None, in_=XD[0:COPIES[j] * NPAD, :],
                                     in_offset=bass.IndirectOffsetOnAxis(in_row[:, s:s + 1], 0),
                                     bounds_check=4 * NPAD - 1, oob_is_err=False).then_inc(sem(f"rows_in{s}"), 16)

            def scatter(b, s):
                p.wait_ge(sem("out_ready"), (b + 1) + FIRST[j])
                p.tensor_copy(out_row[:, s:s + 1], rows_of_blk[:, bass.ds(b, 1)]).then_inc(sem("out_row"), 1)
                p.wait_ge(sem("out_row"), b + (base + 1))
                p.sem_inc(sem("waited"), 1)
                p.indirect_dma_start(out=YD, out_offset=bass.IndirectOffsetOnAxis(out_row[:, s:s + 1], 0),
                                     in_=out_rows[:, s, :], in_offset=None,
                                     bounds_check=4 * NPAD - 1, oob_is_err=False).then_inc(sem(f"y_stored{s}"), 16)

            lead = 2 if j == 4 else 1

            def step(b, s):
                if not (isinstance(b, int) and b + lead + BUFS >= nb):
                    p.wait_ge(sem("rows_turned"), (b + (lead + 1)) + FIRST[j])
                    gather(b + (lead + BUFS), (s + lead) % BUFS)
                if rstd_of and not (isinstance(b, int) and b + 2 >= nb):
                    rstd_of(b + 2, (s + 2) % BUFS)
                scatter(b, s)

            p.wait_ge(sem("x_stored"), 16 * sum(COPIES[0:j + 1]))
            p.wait_ge(sem("rows_known"), j + 1)
            if j == 0:
                p.wait_ge(sem("zeroed"), 16)
            for b in range(BUFS):
                gather(b, b)
            for b in range(BUFS, BUFS + lead):
                p.wait_ge(sem("rows_turned"), (b - (BUFS - 1)) + FIRST[j])
                gather(b, b % BUFS)
                if rstd_of:
                    rstd_of(b - BUFS, b - BUFS)
            blocks(p, 0, nb - BUFS - lead, step)
            for b in range(nb - BUFS - lead, nb):
                step(b, b % BUFS)

        def scale_act(act, j):
            for r in range(1, PICKS[j]):
                act.wait_ge(sem(f"y_back{r}"), 16 * sum(c > r for c in COPIES[0:j + 1]))
                for t in range(NT):
                    last = act.activation(YK[j][:, r, t, :], YK[j][:, r, t, :], ACT.Copy, scale=PW[:, r, t:t + 1])
                last.then_inc(sem("y_scaled"), 1)

        def combine_v(v, j):
            v.wait_ge(sem("y_back0"), 16 * (j + 1))
            for t in range(NT):
                last = v.scalar_tensor_tensor(X[:, t, :], YK[j][:, 0, t, :], PW[:, 0, t:t + 1], X[:, t, :],
                                              ALU.mult, ALU.add)
            link(v, last)
            if j == 4:
                v.wait_ge(sem("y_back3"), 16)
                link(v, v.tensor_tensor(X[:], X[:], YK[j][:, 3, :, :], ALU.add))
            for r in range(1, PICKS[j]):
                v.wait_ge(sem("y_scaled"), sum(PICKS[0:j]) - j + r)
                link(v, v.tensor_tensor(X[:], X[:], YK[j][:, r, :, :], ALU.add))

        def turned_block(b):
            return (PG if b % 2 == 0 else PY[:, 2, :])[0:KD, 0:2 * P]

        def turn_block_pe(pe, j, b, s):
            arrived(pe, "rows_in", [1] * 5, j, b, s)
            if older(b, 2):
                pe.wait_ge(sem("input_ready"), (b - 1) + FIRST[j])
            for c in range(2):
                last = pe.transpose(turned_block(s)[:, c * P:(c + 1) * P], XIN[:, s, c * KD:(c + 1) * KD], ident[:, :])
            last.then_inc(sem("rows_turned"), 1)

        def block_input(eng, j, b, s, gain):
            eng.wait_ge(sem("rows_turned"), (b + 1) + FIRST[j])
            src = turned_block(s)
            if gain is None:
                last = eng.tensor_copy(XGT[0:KD, s, :, :].rearrange("p c n -> p (c n)"), src)
            else:
                for c in range(2):
                    last = eng.tensor_scalar(XGT[0:KD, s, c, :], src[:, c * P:(c + 1) * P], gain[:, c:c + 1], None, ALU.mult)
            last.then_inc(sem("input_ready"), 1)

        def up_bank(pe, j, bank, s, at):
            for q in range(CPB):
                for c in range(2):
                    last = pe.matmul(PH[:, bank, q * P:(q + 1) * P], w_up[j][0:KD, s, c, at + q * P:at + (q + 1) * P],
                                     XGT[0:KD, s, c, :], start=(c == 0), stop=(c == 1), skip_group_check=True)
            return last

        def down_block(pe, j, b, s, ready):
            if older(b, 2):
                pe.wait_ge(sem("out_ready"), (b - 1) + FIRST[j])
            arrived(pe, "down_in", DOWN_DMAS, j, b, s)
            pe.wait_ge(sem(f"m{j}_hid"), ready)
            for m in range(CHUNKS[j]):
                last = pe.matmul(PY[:, s % 2, 0:D], HID[:, s, m, :], w_down[j][:, s, m, :], start=(m == 0),
                                 stop=(m == CHUNKS[j] - 1))
            last.then_inc(sem("down_ready"), 1)

        def out_block(v, j, b, s):
            if older(b, BUFS):
                arrived(v, "y_stored", [1] * 5, j, b - BUFS, s)
            v.wait_ge(sem("down_ready"), (b + 1) + FIRST[j])
            v.tensor_copy(out_rows[:, s, :], PY[:, s % 2, 0:D])\
                .then_inc(sem("out_ready"), 1)

        def up_block(pe, j, b, s):
            arrived(pe, "up_in", UP_DMAS, j, b, s)
            pe.wait_ge(sem("input_ready"), (b + 1) + FIRST[j])
            for h in range(2):
                if older(b, 2):
                    pe.wait_ge(sem(f"m{j}_hid"), b * 2 + (h - 3))
                up_bank(pe, j, 2 * (s % 2) + h, s, h * CPB * P).then_inc(sem(f"m{j}_up"), 1)

        def experts_pe(pe, j, after_first_up=None):
            nb = NBLK[j]

            def step(b, s):
                if not (isinstance(b, int) and b + 2 >= nb):
                    turn_block_pe(pe, j, b + 2, (s + 2) % BUFS)
                if not (isinstance(b, int) and b + 1 >= nb):
                    up_block(pe, j, b + 1, (s + 1) % BUFS)
                down_block(pe, j, b, s, b * 2 + 2)

            turn_block_pe(pe, j, 0, 0)
            up_block(pe, j, 0, 0)
            if after_first_up:
                after_first_up()
            turn_block_pe(pe, j, 1, 1)
            for b in range(2):
                step(b, b)
            blocks(pe, 2, nb - 2, step)
            for b in range(nb - 2, nb):
                step(b, b % BUFS)

        def experts_act(act, j, func, bias=False):
            def step(b, s):
                if bias:
                    arrived(act, "down_in", DOWN_DMAS, j, b, s)
                for h in range(2):
                    act.wait_ge(sem(f"m{j}_up"), b * 2 + (h + 1))
                    src = PH[:, 2 * (s % 2) + h, 0:CPB * P]
                    if bias:
                        for q in range(CPB):
                            m = h * CPB + q
                            last = act.activation(HID[:, s, m, :], src[:, q * P:(q + 1) * P], func,
                                                  bias=ECOLS[:, s, m:m + 1])
                    else:
                        last = act.activation(HID[:, s, h * CPB:(h + 1) * CPB, :].rearrange("p m n -> p (m n)"), src, func)
                    last.then_inc(sem(f"m{j}_hid"), 1)
            blocks(act, 0, NBLK[j], step)
            scale_act(act, j)

        def experts_v(v, j, gain=None, after_first_input=None):
            nb = NBLK[j]

            def step(b, s):
                if not (isinstance(b, int) and b + 2 >= nb):
                    block_input(v, j, b + 2, (s + 2) % BUFS, gain)
                out_block(v, j, b, s)

            for b in range(2):
                block_input(v, j, b, b, gain)
                if b == 0 and after_first_input:
                    after_first_input()
            for b in range(BUFS):
                step(b, b)
            blocks(v, BUFS, nb - 2, step)
            for b in range(nb - 2, nb):
                step(b, b % BUFS)

        def moe0_pe(pe):
            turn_pe(pe, 1, 2, XR)
            pe.wait_ge(sem("weights2"), NLOAD[2])
            pe.wait_ge(sem("gate0_in"), 1)
            gate_pe(pe, 0, 8, gate0, xTg[:, 1, :, :], False)
            count_pe(pe, 0, 8)
            fill_pe(pe, 0)
            nb = NBLK[0]

            def up(b, s):
                arrived(pe, "up_in", UP_DMAS, 0, b, s)
                pe.wait_ge(sem("input_ready"), (b + 1) + FIRST[0])
                for h in range(2):
                    if older(b, 1):
                        pe.wait_ge(sem("m0_silu"), b * 2 + (h - 1))
                    up_bank(pe, 0, 2 * h, s, h * CPB * P).then_inc(sem("m0_upa"), 1)
                    if older(b, 1):
                        pe.wait_ge(sem("m0_hid"), b * 2 + (h - 1))
                    up_bank(pe, 0, 2 * h + 1, s, FF + h * CPB * P).then_inc(sem("m0_upb"), 1)

            def step(b, s):
                if not (isinstance(b, int) and b + 2 >= nb):
                    turn_block_pe(pe, 0, b + 2, (s + 2) % BUFS)
                if not (isinstance(b, int) and b + 1 >= nb):
                    up(b + 1, (s + 1) % BUFS)
                down_block(pe, 0, b, s, b * 2 + 2)

            turn_block_pe(pe, 0, 0, 0)
            up(0, 0)
            turn_block_pe(pe, 0, 1, 1)
            for b in range(2):
                step(b, b)
            blocks(pe, 2, nb - 2, step)
            for b in range(nb - 2, nb):
                step(b, b % BUFS)

        def moe0_act(act):
            act.wait_ge(sem("weights2"), NLOAD[2])
            turn_act(act, 1)
            gate_act(act, 0, SOFT_PAIR)

            def step(b, s):
                for h in range(2):
                    act.wait_ge(sem("m0_upa"), b * 2 + (h + 1))
                    if older(b, 1):
                        act.wait_ge(sem("m0_hid"), b * 2 + (h - 1))
                    act.activation(SIL[:, h, 0:CPB * P], PH[:, 2 * h, 0:CPB * P], ACT.Silu).then_inc(sem("m0_silu"), 1)
            for b in range(2):
                step(b, b)
            blocks(act, 2, NBLK[0], step)
            scale_act(act, 0)

        def moe0_v(v):
            v.wait_ge(sem("weights2"), NLOAD[2])
            v.tensor_scalar(minus_iota[:], iota[:], -1.0, None, ALU.mult)
            link(v, v.tensor_scalar(blk_start[:], iota[:, 0:NBLK[4]], float(P), BIG, ALU.mult, ALU.add))
            norm_v(v, 2, X2, XR, 1e-6, False)
            turn_v(v, 1)
            xT_ready(v, 1)
            for c in range(2):
                last = v.tensor_scalar(xTg[:, 1, c, :], xT[0:KD, c, :], g_moe[:, c:c + 1], None, ALU.mult)
            last.then_inc(sem("gate0_in"), 1)
            gate_v(v, 0, 8, SOFT_PAIR)
            slots_v(v, 0, 8)
            weights_v(v, 0, 8, SOFT_PAIR)
            link(v, v.tensor_tensor(TOPV[:, 0, :], PW[:, 0, :], PW[:, 1, :], ALU.add))
            for t in range(NT):
                last = v.scalar_tensor_tensor(X[:, t, :], X2[:, t, :], TOPV[:, 0, t:t + 1], X[:, t, :], ALU.mult, ALU.add)
            link(v, last)
            nb = NBLK[0]

            def scaled_input(b, s):
                arrived(v, "up_in", UP_DMAS, 0, b, s)
                block_input(v, 0, b, s, ECOLS[0:KD, s, 0:2])

            def products(b, s):
                for h in range(2):
                    v.wait_ge(sem("m0_upb"), b * 2 + (h + 1))
                    v.wait_ge(sem("m0_silu"), b * 2 + (h + 1))
                    v.tensor_tensor(HID[:, s, h * CPB:(h + 1) * CPB, :].rearrange("p m n -> p (m n)"),
                                    PH[:, 2 * h + 1, 0:CPB * P], SIL[:, h, 0:CPB * P], ALU.mult).then_inc(sem("m0_hid"), 1)

            def step(b, s):
                if not (isinstance(b, int) and b + 2 >= nb):
                    scaled_input(b + 2, (s + 2) % BUFS)
                if not (isinstance(b, int) and b + 1 >= nb):
                    products(b + 1, (s + 1) % BUFS)
                out_block(v, 0, b, s)

            scaled_input(0, 0)
            products(0, 0)
            scaled_input(1, 1)
            for b in range(BUFS):
                step(b, b)
            blocks(v, BUFS, nb - 2, step)
            for b in range(nb - 2, nb):
                step(b, b % BUFS)
            combine_v(v, 0)

        def moe1_pe(pe):
            turn_pe(pe, 2, 3, XN)
            xT_ready(pe, 2)
            gate_pe(pe, 1, 8, gate1, xT, True)
            count_pe(pe, 1, 8)
            fill_pe(pe, 1)
            experts_pe(pe, 1, lambda: outbias_pe(pe, 0, 1, 8, b_proj))

        def moe1_act(act):
            turn_act(act, 2)
            gate_act(act, 1, SOFT_PAIR)
            experts_act(act, 1, ACT.Gelu_apprx_tanh, bias=True)

        def moe1_v(v):
            norm_v(v, 3, X, XN, 1e-5, True)
            turn_v(v, 2)
            gate_v(v, 1, 8, SOFT_PAIR)
            slots_v(v, 1, 8)
            weights_v(v, 1, 8, SOFT_PAIR)
            experts_v(v, 1, after_first_input=lambda: outbias_v(v, 0, 8))
            combine_v(v, 1)

        def moe2_pe(pe):
            turn_pe(pe, 4, 6, XR)
            xT_ready(pe, 4)
            gate_pe(pe, 2, 16, gate2, xT, False)
            count_pe(pe, 2, 16)
            fill_pe(pe, 2)
            experts_pe(pe, 2)

        def moe2_act(act):
            turn_act(act, 4, ln_w1)
            gate_act(act, 2, SOFT_TOP1)
            experts_act(act, 2, ACT.Relu)

        def moe2_v(v):
            norm_v(v, 5, X, XN, 1e-5, True)
            v.wait_ge(sem("normed"), 6 * NT)
            norm_v(v, 6, XN, XR, 1e-6, False)
            link(v, v.tensor_tensor(X[:], X[:], XN[:], ALU.add))
            turn_v(v, 4, ln_w1)
            gate_v(v, 2, 16, SOFT_TOP1)
            slots_v(v, 2, 16)
            weights_v(v, 2, 16, SOFT_TOP1)
            experts_v(v, 2, ln_w1)
            combine_v(v, 2)

        def moe3_pe(pe):
            turn_pe(pe, 7, 10, XN)
            xT_ready(pe, 7)
            gate_pe(pe, 3, 8, gate3, xT, False)
            count_pe(pe, 3, 8)
            fill_pe(pe, 3)
            experts_pe(pe, 3)

        def moe3_act(act):
            turn_act(act, 7)
            gate_act(act, 3, SOFT_TOP2)
            experts_act(act, 3, ACT.Gelu_apprx_tanh)

        def moe3_v(v):
            norm_v(v, 10, X, XN, 1e-5, True)
            turn_v(v, 7)
            gate_v(v, 3, 8, SOFT_TOP2)
            slots_v(v, 3, 8)
            weights_v(v, 3, 8, SOFT_TOP2)
            experts_v(v, 3)
            combine_v(v, 3)

        def m4_up(pe, b, s):
            arrived(pe, "up_in", UP_DMAS, 4, b, s)
            pe.wait_ge(sem("input_ready"), (b + 1) + FIRST[4])
            if older(b, 2):
                pe.wait_ge(sem("m4_gelu"), b - 1)
            for c in range(2):
                kk = KD + c
                last = pe.matmul(PH[:, s % 2, 0:FH], XGT[0:kk, s, c, :], w_up[4][0:kk, s, c, :],
                                 start=(c == 0), stop=(c == 1))
            last.then_inc(sem("m4_up"), 1)

        def m4_turn(pe, b, s):
            pe.wait_ge(sem("m4_normed"), b + 1)
            if older(b, 2):
                pe.wait_ge(sem("m4_hid"), b - 1)
            for m in range(NFH):
                last = pe.transpose(PH[:, 2 + s % 2, m * P:(m + 1) * P], HG[:, s, m * P:(m + 1) * P], ident[:, :])
            last.then_inc(sem("m4_turned"), 1)

        def m4_norm(v, b, s):
            v.wait_ge(sem("m4_gelu"), b + 1)
            v.bn_stats(hstats[:, s, :], HG[:, s, :]).then_inc(sem("m4_stats"), 1)
            v.wait_ge(sem("m4_stats"), b + 1)
            half = [hstats[:, s, q:q + 1] for q in range(6)]
            v.tensor_tensor(hwork[:, s, 0:1], half[1], half[4], ALU.add)
            v.tensor_tensor(hwork[:, s, 1:2], half[1], half[4], ALU.subtract)
            v.tensor_tensor(hwork[:, s, 2:3], half[2], half[5], ALU.add).then_inc(sem("m4_sums"), 1)
            v.wait_ge(sem("m4_sums"), b + 1)
            v.tensor_scalar(hmean[:, s, :], hwork[:, s, 0:1], 0.5, None, ALU.mult)
            v.tensor_tensor(hwork[:, s, 3:4], hwork[:, s, 1:2], hwork[:, s, 1:2], ALU.mult)
            v.tensor_scalar(hwork[:, s, 4:5], hwork[:, s, 2:3], 1.0 / FH, 1e-5, ALU.mult, ALU.add)\
                .then_inc(sem("m4_scaled"), 1)
            v.wait_ge(sem("m4_scaled"), b + 1)
            v.scalar_tensor_tensor(hvar[:, s, :], hwork[:, s, 3:4], 0.25, hwork[:, s, 4:5], ALU.mult, ALU.add)\
                .then_inc(sem("m4_var"), 1)

        def m4_normalise(v, b, s):
            v.wait_ge(sem("m4_rstd"), b + 1)
            v.tensor_scalar(HG[:, s, :], HG[:, s, :], hmean[:, s, :], hrstd[:, s, :], ALU.subtract, ALU.mult)\
                .then_inc(sem("m4_normed"), 1)

        def m4_hidden(v, b, s):
            arrived(v, "down_in", DOWN_DMAS, 4, b, s)
            v.wait_ge(sem("m4_turned"), b + 1)
            for m in range(NFH):
                last = v.tensor_scalar(HID[:, s, m, :], PH[:, 2 + s % 2, m * P:(m + 1) * P], ECOLS[:, s, m:m + 1],
                                       ECOLS[:, s, NFH + m:NFH + m + 1], ALU.mult, ALU.add)
            last.then_inc(sem("m4_hid"), 1)

        def moe4_pe(pe):
            turn_pe(pe, 9, 12, XN)
            xT_ready(pe, 9)
            gate_pe(pe, 4, 16, gate4, xT, True)
            count_pe(pe, 4, 16)
            fill_pe(pe, 4)
            nb = NBLK[4]

            def step(b, s):
                m4_turn(pe, b, s)
                if not (isinstance(b, int) and b + 3 >= nb):
                    turn_block_pe(pe, 4, b + 3, (s + 3) % BUFS)
                if not (isinstance(b, int) and b + 2 >= nb):
                    m4_up(pe, b + 2, (s + 2) % BUFS)
                down_block(pe, 4, b, s, b + 1)

            turn_block_pe(pe, 4, 0, 0)
            m4_up(pe, 0, 0)
            outbias_pe(pe, 1, 4, 16, b_fc2)
            turn_block_pe(pe, 4, 1, 1)
            m4_up(pe, 1, 1)
            turn_block_pe(pe, 4, 2, 2)
            for b in range(3):
                step(b, b)
            blocks(pe, 3, nb - 3, step)
            for b in range(nb - 3, nb):
                step(b, b % BUFS)

        def moe4_act(act):
            turn_act(act, 9)
            gate_act(act, 4, SHARED_TOP3)
            nb = NBLK[4]

            def input_(b, s):
                act.wait_ge(sem("rows_turned"), (b + 1) + FIRST[4])
                act.activation(XGT[0:KD, s, :, :].rearrange("p c n -> p (c n)"), turned_block(s), ACT.Copy)\
                    .then_inc(sem("input_ready"), 1)

            def gelu(b, s):
                act.wait_ge(sem("m4_up"), b + 1)
                act.activation(HG[:, s, :], PH[:, s % 2, 0:FH], ACT.Gelu).then_inc(sem("m4_gelu"), 1)

            def step(b, s):
                if not (isinstance(b, int) and b + 3 >= nb):
                    input_(b + 3, (s + 3) % BUFS)
                if not (isinstance(b, int) and b + 2 >= nb):
                    gelu(b + 2, (s + 2) % BUFS)

            input_(0, 0)
            gelu(0, 0)
            input_(1, 1)
            gelu(1, 1)
            input_(2, 2)
            blocks(act, 0, nb - 3, step)
            step(nb - 3, (nb - 3) % BUFS)
            scale_act(act, 4)

        def moe4_v(v):
            norm_v(v, 12, X, XN, 1e-5, True)
            v.memset(XGT[KD:KD + 1, :, :, :], 1.0)
            turn_v(v, 9)
            gate_v(v, 4, 16, SHARED_TOP3)
            slots_v(v, 4, 16)
            weights_v(v, 4, 16, SHARED_TOP3)
            outbias_v(v, 1, 16)
            nb = NBLK[4]

            def step(b, s):
                m4_hidden(v, b, s)
                if not (isinstance(b, int) and b + 1 >= nb):
                    m4_normalise(v, b + 1, (s + 1) % BUFS)
                if not (isinstance(b, int) and b + 2 >= nb):
                    m4_norm(v, b + 2, (s + 2) % BUFS)
                out_block(v, 4, b, s)

            m4_norm(v, 0, 0)
            m4_normalise(v, 0, 0)
            m4_norm(v, 1, 1)
            for b in range(BUFS):
                step(b, b)
            blocks(v, BUFS, nb - 2, step)
            for b in range(nb - 2, nb):
                step(b, b % BUFS)
            combine_v(v, 4)

        def m4_rstd(p, b, s):
            p.wait_ge(sem("m4_var"), b + 1)
            p.tensor_tensor(hrstd[:, s, :], hvar[:, s, :], minus_half[:, 0:1], ALU.pow).then_inc(sem("m4_rstd"), 1)

        HEADS, HG_, DV = [12, 8, 12], [3, 2, 3], [8, 24, 16]
        ESCALE = [float(8) ** -0.5, float(LDK) ** -0.5, 1.0]
        GROUPS = 4

        def rows_of(s):
            return 64 if s == 0 else T

        def scores_pe(pe, a, p):
            if p >= 2:
                pe.wait_ge(sem("at_sub"), 8 * a + p - 1)
            S = PH[:, p % 2, :]
            for s in range(2):
                b, r = 2 * p + s, rows_of(s)
                o = S[64 * s:64 * s + r, :]
                if a == 0:
                    pe.wait_ge(sem("q_ready" if p < 2 else "more_keys"), p + 1 if p < 2 else p - 1)
                    last = pe.matmul(o[:, 0:QH * T], QT[0:96, 0, b * T:b * T + r],
                                     KB[0:96, :, :, :].rearrange("p c b n -> p (c b n)")[:, b * QH * T:(b + 1) * QH * T],
                                     start=True, stop=True, skip_group_check=True)
                elif a == 1:
                    for c in range(4):
                        last = pe.matmul(o[:, 2 * c * T:2 * (c + 1) * T], QT[:, c, b * T:b * T + r],
                                         KM[:, c, b, :], start=True, stop=True, skip_group_check=True)
                else:
                    for c in range(2):
                        last = pe.matmul(o[:, c * 6 * T:(c + 1) * 6 * T], QT[0:96, c, b * T:b * T + r],
                                         KB[0:96, c, b, :], start=True, stop=True, skip_group_check=True)
            last.then_inc(sem("at_scores"), 1)

        def values_pe(pe, a, p):
            if p >= 1:
                pe.wait_ge(sem("at_vb"), 8 * a + p)
            hg, w = HG_[a], HEADS[a] * DV[a]
            for s in range(2):
                b = 2 * p + s
                o = PY[0:hg * T, 2, s * D:s * D + w]

                if a == 0:
                    last = pe.matmul(o, REP(a, 0)[0:96, b, :], ident[0:96, 0:96], start=True, stop=True,
                                     skip_group_check=True)
                else:
                    for c in range(2):
                        w_ = wv[:, c, :] if a == 1 else wqkv[:, c, 2 * D:3 * D]
                        kk = KD + 1 if a == 2 and c == 1 else KD
                        last = pe.matmul(o, REP(a, c)[0:kk, b, :], w_[0:kk], start=(c == 0), stop=(c == 1),
                                         skip_group_check=True)
            last.then_inc(sem("at_values"), 1)

        def turn_probs_pe(pe, a, p):
            pe.wait_ge(sem("at_exp"), 8 * a + p + 1)
            if p >= 2:
                pe.wait_ge(sem("at_pts"), 8 * a + p - 1)
            g = HG_[a] * T
            for q in range(GROUPS):
                last = pe.transpose(PH[0:g, 2 + p % 2, q * P:q * P + R2], PM[0:R2, p % 2, q * g:(q + 1) * g],
                                    ident[0:R2, 0:R2])
            last.then_inc(sem("at_pt"), 1)

        def mix_pe(pe, a, p):
            pe.wait_ge(sem("at_pts"), 8 * a + p + 1)
            pe.wait_ge(sem("at_vb"), 8 * a + p + 1)
            if p >= 2:
                pe.wait_ge(sem("at_osb"), 8 * a + p - 1)
            g, w = HG_[a] * T, HG_[a] * DV[a]
            for q in range(GROUPS):
                last = pe.matmul(PY[0:R2, p % 2, 2 * q * w:2 * (q + 1) * w], PTS[0:g, p % 2, q * P:q * P + R2],
                                 VB[0:g, 2 * p:2 * p + 2, q * w:(q + 1) * w], start=True, stop=True, skip_group_check=True)
            last.then_inc(sem("at_o"), 1)

        def turn_out_pe(pe, a, p):
            pe.wait_ge(sem("at_osb"), 8 * a + p + 1)
            if p >= 1:
                pe.wait_ge(sem("at_ot"), 8 * a + p)
            for c in range(1 if a == 0 else 2):
                last = pe.transpose(PG[0:96, c * P:c * P + R2], OSB[0:R2, p % 2, c * 96:(c + 1) * 96], ident[0:R2, 0:R2])
            last.then_inc(sem("at_turned"), 1)

        def REP(a, c):
            n, at = B * HG_[a] * T, 2 * LH * NREL if a == 1 else 0
            flat = hT[0:97].rearrange("p a n -> p (a n)")[:, at + c * n:at + (c + 1) * n]
            return flat.rearrange("p (b n) -> p b n", b=B)

        def repeat_act(act, a):
            for c in range(1 if a == 0 else 2):
                kk = KD + 1 if a == 2 and c == 1 else KD
                src = (QT[0:kk, 0, 0:N] if a == 0 else xT[0:kk, c, :]).rearrange("p (b j) -> p b j", j=T)
                act.activation(REP(a, c)[0:kk].rearrange("p b (g j) -> p b g j", j=T),
                               src.unsqueeze(2).to_broadcast([kk, B, HG_[a], T]), ACT.Copy).then_inc(sem("at_rep"), 1)

        def pairs_pe(pe, a):
            pe.wait_ge(sem("at_rep"), [1, 3, 5][a])
            for p in range(PAIRS + 3):
                if p < PAIRS:
                    values_pe(pe, a, p)
                    scores_pe(pe, a, p)
                if 0 <= p - 1 < PAIRS:
                    turn_probs_pe(pe, a, p - 1)
                if 0 <= p - 2 < PAIRS:
                    mix_pe(pe, a, p - 2)
                if 0 <= p - 3 < PAIRS:
                    turn_out_pe(pe, a, p - 3)
            pe.wait_ge(sem("at_ot"), 8 * (a + 1))

        def pairs_v(v, a):
            H, hg, dv = HEADS[a], HG_[a], DV[a]
            mask = mask8 if a == 1 else mask12

            def heads(ap):
                return ap.rearrange("p (h j) -> p h j", j=T)

            def over(ap, n):
                return ap.unsqueeze(2).to_broadcast([R2, H, n])

            for p in range(PAIRS + 2):
                if p < PAIRS:
                    v.wait_ge(sem("at_values"), 8 * a + p + 1)
                    for s in range(2):
                        last = v.tensor_tensor(
                            VB[0:hg * T, 2 * p + s, 0:H * dv].rearrange("p (g h d) -> p g h d", g=GROUPS, h=hg),
                            PY[0:hg * T, 2, s * D:s * D + H * dv].rearrange("p (g h d) -> p g h d", g=GROUPS, h=hg),
                            mask[:, :].unsqueeze(1).unsqueeze(3).to_broadcast([hg * T, GROUPS, hg, dv]), ALU.mult)
                    last.then_inc(sem("at_vb"), 1)
                    v.wait_ge(sem("at_scores"), 8 * a + p + 1)
                    if p >= 2:
                        v.wait_ge(sem("at_pt"), 8 * a + p - 1)
                    S, M = PH[0:R2, p % 2, 0:H * T], PM[0:R2, p % 2, 0:H * T]
                    if a == 1:
                        v.wait_ge(sem("rel_in"), 16 * B)
                        link(v, v.tensor_tensor(M, S, RB8[0:R2, p, :], ALU.add))
                        S = M
                    link(v, v.tensor_reduce(amax[0:R2, p % 2, 0:H], heads(S), AX.X, ALU.max))
                    v.tensor_tensor(heads(M), heads(S), over(amax[0:R2, p % 2, 0:H], T), ALU.subtract)\
                        .then_inc(sem("at_sub"), 1)
                if 0 <= p - 1 < PAIRS:
                    q = p - 1
                    v.wait_ge(sem("at_exp"), 8 * a + q + 1)
                    link(v, v.tensor_reduce(asum[0:R2, q % 2, 0:H], heads(PM[0:R2, q % 2, 0:H * T]), AX.X, ALU.add))
                    link(v, v.reciprocal(arinv[0:R2, q % 2, 0:H], asum[0:R2, q % 2, 0:H]))
                if 0 <= p - 2 < PAIRS:
                    q = p - 2
                    v.wait_ge(sem("at_o"), 8 * a + q + 1)
                    if q >= 2:
                        v.wait_ge(sem("at_turned"), 8 * a + q - 1)
                    o = PY[0:R2, q % 2, 0:2 * H * dv].rearrange("p (g s h d) -> p g s h d", g=GROUPS, s=2, h=hg)
                    osb = OSB[0:R2, q % 2, 0:H * dv].rearrange("p (g h d) -> p g h d", g=GROUPS, h=hg)
                    scale = arinv[0:R2, q % 2, 0:H].rearrange("p (g h) -> p g h", g=GROUPS).unsqueeze(3)\
                        .to_broadcast([R2, GROUPS, hg, dv])
                    for s in range(2):
                        rows = slice(0, 64) if s == 0 else slice(64, R2)
                        last = v.tensor_tensor(osb[rows], o[rows, :, s], scale[rows], ALU.mult)
                    last.then_inc(sem("at_osb"), 1)

        def pairs_act(act, a):
            g, nc_ = HG_[a] * T, 1 if a == 0 else 2
            for p in range(PAIRS + 3):
                if p < PAIRS:
                    M = PM[0:R2, p % 2, 0:HEADS[a] * T]
                    act.wait_ge(sem("at_sub"), 8 * a + p + 1)
                    act.activation(M, M, ACT.Exp, scale=ESCALE[a]).then_inc(sem("at_exp"), 1)
                if 0 <= p - 1 < PAIRS:
                    q = p - 1
                    act.wait_ge(sem("at_pt"), 8 * a + q + 1)
                    if q >= 2:
                        act.wait_ge(sem("at_o"), 8 * a + q - 1)
                    act.activation(PTS[0:g, q % 2, :].rearrange("p (q r) -> p q r", q=GROUPS)[:, :, 0:R2],
                                   PH[0:g, 2 + q % 2, :].rearrange("p (q r) -> p q r", q=GROUPS)[:, :, 0:R2],
                                   ACT.Copy).then_inc(sem("at_pts"), 1)
                if 0 <= p - 3 < PAIRS:
                    q = p - 3
                    act.wait_ge(sem("at_turned"), 8 * a + q + 1)
                    for c in range(nc_):
                        last = act.activation(
                            OT[0:96, c, q * 2 * T:(q + 1) * 2 * T].rearrange("p (s j) -> p s j", s=2),
                            PG[0:96, c * P:(c + 1) * P].rearrange("p (s j) -> p s j", s=2)[:, :, 0:T], ACT.Copy)
                    last.then_inc(sem("at_ot"), 1)

        def project_pe(pe, a, w, bias):
            for t in range(NT):
                n = 1 if a == 0 else 2
                for c in range(n):
                    kk = KD + 1 if bias and c == 1 else KD
                    last = pe.matmul(ytile(t), OT[0:kk, c, t * P:t * P + ROWS[t]], w[0:kk, c, :] if n > 1 else w[:, :],
                                     start=(c == 0), stop=(c == n - 1), skip_group_check=True)
            last.then_inc(sem("projected"), 1)

        TWO_PI = 2 * np.pi
        C1 = 6.28125
        C2 = float(np.float32(np.round((TWO_PI - C1) * 2 ** 20) / 2 ** 20))
        C3 = TWO_PI - C1 - C2
        ROUND = 1.5 * 2 ** 23
        XTH = CX.rearrange("p a n -> p (a n)")[:, 0:N + 1]
        KTH = QV.rearrange("p a n -> p (a n)")[0:96, 0:N + 1]
        SINS = QV.rearrange("p a n -> p (a n)")[0:96, N + 1:2 * N + 2]

        def cos_pe(pe):
            turn_pe(pe, 3, 4, XN)
            xT_ready(pe, 3)
            keep_warm(pe, PH[:, 3, :], 20)
            pairs_pe(pe, 0)
            project_pe(pe, 0, w_comb, False)

        def cos_act(act):
            turn_act(act, 3)
            act.wait_ge(sem("angles"), 1)
            act.activation(SINS, XTH, ACT.Sin).then_inc(sem("sines"), 1)
            act.wait_ge(sem("q_made"), 1)
            repeat_act(act, 0)
            pairs_act(act, 0)

        def cos_pool(p):
            p.wait_ge(sem("q_made"), 1)
            for pair in range(2, PAIRS):
                cos_keys(p, pair, "more_keys")

        def cos_keys(v, p, done="q_ready"):
            v.tensor_tensor(KB[0:96].rearrange("p c b n -> p (c b n)")[:, 2 * p * QH * T:2 * (p + 1) * QH * T]
                            .rearrange("p (b h j) -> p b h j", b=2, h=QH),
                            QT[0:96, 0, 2 * p * T:2 * (p + 1) * T].rearrange("p (b j) -> p b j", j=T).unsqueeze(2)
                            .to_broadcast([96, 2, QH, T]),
                            khead12[:, :].unsqueeze(1).unsqueeze(3).to_broadcast([96, 2, QH, T]), ALU.mult)\
                .then_inc(sem(done), 1)

        def cos_v(v):
            norm_v(v, 4, X, XN, 1e-5, True)
            turn_v(v, 3)
            xT_ready(v, 3)
            v.tensor_copy(XTH[:, 0:N], xT[0:96, 0, :])
            link(v, v.tensor_copy(XTH[:, N:N + 1], theta[:, :]))
            link(v, v.tensor_scalar(KTH, XTH, 1.0 / TWO_PI, ROUND, ALU.mult, ALU.add))
            link(v, v.tensor_scalar(KTH, KTH, -ROUND, None, ALU.add))
            for cc in (C1, C2, C3):
                link(v, v.scalar_tensor_tensor(XTH, KTH, -cc, XTH, ALU.mult, ALU.add))
            link(v, v.scalar_tensor_tensor(XTH, XTH, -1.0, XTH, ALU.mult, ALU.min))
            v.tensor_scalar(XTH, XTH, np.pi / 2, None, ALU.add).then_inc(sem("angles"), 1)
            v.wait_ge(sem("sines"), 1)
            link(v, v.tensor_copy(cth[:, 0:1], SINS[:, N:N + 1]))
            v.tensor_scalar(QT[0:96, 0, 0:N], SINS[:, 0:N], cth[:, 0:1], None, ALU.mult).then_inc(sem("q_made"), 1)
            v.wait_ge(sem("q_made"), 1)
            for p in range(2):
                cos_keys(v, p)
            pairs_v(v, 0)
            v.wait_ge(sem("projected"), 1)
            link(v, add_to(v, X, X))

        RB8, _r = view(b_, [PAIRS, LH * T])
        assert _r <= LATE

        def rel_pe(pe):
            turn_pe(pe, 5, 8, XR)
            xT_ready(pe, 5)
            for c in range(4):
                last = pe.matmul(PG[:, c * P:c * P + NREL], wposT[:, c * P:(c + 1) * P], basis[:, :], start=True, stop=True,
                                 skip_group_check=True)
            last.then_inc(sem("wr_ready"), 1)
            for q in range(8):
                w, c = (wq, wk)[q // 4], q % 4
                if q >= 2:
                    pe.wait_ge(sem("qk_moved"), q - 1)
                for h in range(2):
                    for k in range(2):
                        last = pe.matmul(PH[:, 2 * (q % 2) + h, 0:HF], w[:, k, c * P:(c + 1) * P],
                                         xT[0:KD, k, h * HF:(h + 1) * HF], start=(k == 0), stop=(k == 1))
                last.then_inc(sem("qk_ready"), 1)
            pe.wait_ge(sem("wr_moved"), 1)
            for t in range(NT):
                pe.wait_ge(sem("qk_moved"), 8)
                if t >= 2:
                    pe.wait_ge(sem("rel_moved"), t - 1)
                for c in range(4):
                    o = PH[0:ROWS[t], 2 * (t % 2) + c // 2, (c % 2) * 2 * NREL:(c % 2 + 1) * 2 * NREL]
                    last = pe.matmul(o, QV8[:, c, t * P:t * P + ROWS[t]], WR[:, c, :],
                                     start=True, stop=True, skip_group_check=True)
                last.then_inc(sem("rel_ready"), 1)
            pe.wait_ge(sem("rel_moved"), NT)
            pairs_pe(pe, 1)
            project_pe(pe, 1, wo, True)
            turn_pe(pe, 6, 9, XR)
            xT_ready(pe, 6)
            for m in range(NFH):
                if m >= 2:
                    pe.wait_ge(sem("ffn_hid"), m - 1)
                for h in range(2):
                    for c in range(2):
                        last = pe.matmul(PH[:, 2 * (m % 2) + h, 0:HF], fw1[:, c, m * P:(m + 1) * P],
                                         xT[0:KD, c, h * HF:(h + 1) * HF], start=(c == 0), stop=(c == 1))
                last.then_inc(sem("ffn_up"), 1)
            for m in range(NFH):
                pe.wait_ge(sem("ffn_hid"), m + 1)
                for t in range(NT):
                    pe.matmul(ytile(t), hT[:, m, t * P:t * P + ROWS[t]], fw2[:, m, :], start=(m == 0 and t % 2 == 0),
                              stop=False, skip_group_check=True)
            for t in range(NT):
                last = pe.matmul(ytile(t), ones_row[0:1, 0:ROWS[t]], fb2[0:1, :], start=False, stop=True,
                                 skip_group_check=True)
            last.then_inc(sem("ffn_out"), 1)

        def rel_act(act):
            turn_act(act, 5, norm1_w)
            for q in range(4):
                act.wait_ge(sem("qk_ready"), q + 1)
                act.activation(two(QV8[:, q, 0:N]), halves(q % 2), ACT.Identity, bias=v_par[:, q:q + 1]).then_inc(sem("qv_moved"), 1)
            xT_ready(act, 5)
            repeat_act(act, 1)
            pairs_act(act, 1)
            turn_act(act, 6, norm2_w)
            for m in range(NFH):
                act.wait_ge(sem("ffn_up"), m + 1)
                act.activation(two(hT[:, m, :]), halves(m % 2), ACT.Gelu, bias=fb1[:, m:m + 1]).then_inc(sem("ffn_hid"), 1)

        def rel_v(v):
            norm_v(v, 7, X, XN, 1e-5, True)
            v.wait_ge(sem("normed"), 8 * NT)
            norm_v(v, 8, XN, XR, 1e-5, False)
            turn_v(v, 5, norm1_w)
            v.memset(OT[KD:KD + 1, 1, :], 1.0)
            v.wait_ge(sem("rel_clear"), 1)
            v.wait_ge(sem("wr_ready"), 1)
            for z in range(2):
                last = v.tensor_copy(WR[64 * z:64 * z + 64, :, z * NREL:(z + 1) * NREL],
                                     PG[64 * z:64 * z + 64, :].rearrange("p (c r) -> p c r", c=4)[:, :, 0:NREL])
            last.then_inc(sem("wr_moved"), 1)
            for q in range(8):
                v.wait_ge(sem("qk_ready"), q + 1)
                if q == 4:
                    v.wait_ge(sem("rel_clear"), 2)
                if q < 4:
                    v.wait_ge(sem("qv_moved"), q + 1)
                    v.tensor_scalar(two(QT[:, q, 0:N]), halves(q % 2), u_par[:, q:q + 1], None, ALU.add).then_inc(sem("qk_moved"), 1)
                else:
                    for z in range(2):
                        last = v.tensor_copy(
                            KM[64 * z:64 * z + 64, q - 4, :, z * T:(z + 1) * T].rearrange("p (h b) j -> p h b j", h=2),
                            halves(q % 2)[64 * z:64 * z + 64].rearrange("p h (b j) -> p h b j", j=T))
                    last.then_inc(sem("qk_moved"), 1)
            for t in range(NT):
                v.wait_ge(sem("rel_ready"), t + 1)
                if t >= 2:
                    v.wait_ge(sem(f"rel_out{t % 2}"), 16 * (t // 2))
                v.tensor_copy(RSB[0:ROWS[t], t % 2, :].rearrange("p (a n) -> p a n", a=2),
                              PH[0:ROWS[t], 2 * (t % 2):2 * (t % 2) + 2, 0:4 * NREL]).then_inc(sem("rel_moved"), 1)
            pairs_v(v, 1)
            v.wait_ge(sem("projected"), 2)
            link(v, add_to(v, X2, XN))
            norm_v(v, 9, X2, XR, 1e-5, False)
            link(v, v.tensor_tensor(X[:], X[:], X2[:], ALU.add))
            turn_v(v, 6, norm2_w)
            v.wait_ge(sem("ffn_out"), 1)
            link(v, add_to(v, X, X))

        def rel_sp(sp):
            def stored(t):
                sp.wait_ge(sem("rel_out0"), 16 * (t // 2 + 1))
                if t >= 1:
                    sp.wait_ge(sem("rel_out1"), 16 * ((t + 1) // 2))
                for b in range(B):
                    if ((b + 1) * T - 1) // P != t:
                        continue
                    src = bass.AP(tensor=rel_dram.tensor, offset=b * T * LH * NREL + T - 1,
                                  ap=[[LH * NREL - 1, T], [NREL, LH], [1, T]])
                    sp.dma_start(RB8[64 * (b % 2):64 * (b % 2) + T, b // 2, :].rearrange("p (h j) -> p h j", j=T), src)\
                        .then_inc(sem("rel_in"), 16)

            for t in range(NT):
                sp.wait_ge(sem("rel_moved"), t + 1)
                sp.dma_start(rel_dram[t * P:t * P + ROWS[t], :], RSB[0:ROWS[t], t % 2, :]).then_inc(sem(f"rel_out{t % 2}"), 16)
                if t == 0:
                    sp.wait_ge(sem("rel_clear"), 3)
                if t >= 1:
                    stored(t - 1)
            stored(NT - 1)

        def plain_pe(pe):
            pe.wait_ge(sem("weights3"), NLOAD[3])
            turn_pe(pe, 8, 11, XN)
            xT_ready(pe, 8)
            for q in range(4):
                if q >= 2:
                    pe.wait_ge(sem("pqk_moved"), q - 1)
                for h in range(2):
                    for k in range(2):
                        last = pe.matmul(PH[0:96, 2 * (q % 2) + h, 0:HF], wqkv[0:KD, k, q * 96:(q + 1) * 96],
                                         xT[0:KD, k, h * HF:(h + 1) * HF], start=(k == 0), stop=(k == 1))
                last.then_inc(sem("pqk_ready"), 1)
            pe.wait_ge(sem("pqk_moved"), 3)
            pe.wait_ge(sem("pkeys_act"), 1)
            pairs_pe(pe, 2)
            project_pe(pe, 2, wo3, True)

        def key_rows(q):
            return halves(q % 2, 96).rearrange("p h (b j) -> p h b j", j=T)

        def head_keys(q, h):
            return KB[0:96, q - 2, :, h * T:(h + 1) * T].rearrange("p (h b) j -> p h b j", h=2)

        def plain_act(act):
            turn_act(act, 8)
            act.wait_ge(sem("bk_ready"), 1)
            xT_ready(act, 8)
            repeat_act(act, 2)
            act.wait_ge(sem("pqk_ready"), 4)
            for h in range(6):
                last = act.activation(head_keys(3, h), key_rows(3), ACT.Identity, bias=bk_head[:, h:h + 1],
                                      scale=khead24[:, h:h + 1])
            last.then_inc(sem("pkeys_act"), 1)
            pairs_act(act, 2)

        def plain_v(v):
            norm_v(v, 11, X, XN, 1e-5, True)
            turn_v(v, 8)
            v.memset(OT[KD:KD + 1, 1, :], 1.0)
            v.tensor_scalar(bk_head[:], khead24[:], bqk[:, 3:4], None, ALU.mult).then_inc(sem("bk_ready"), 1)
            for q in range(3):
                v.wait_ge(sem("pqk_ready"), q + 1)
                if q < 2:
                    last = v.tensor_scalar(two(QT[0:96, q, 0:N]), halves(q % 2, 96), bqk[:, q:q + 1], float(16) ** -0.5,
                                           ALU.add, ALU.mult)
                else:
                    for h in range(6):
                        last = v.tensor_scalar(head_keys(q, h), key_rows(q), bqk[:, q:q + 1], khead24[:, h:h + 1],
                                               ALU.add, ALU.mult)
                last.then_inc(sem("pqk_moved"), 1)
            pairs_v(v, 2)
            v.wait_ge(sem("projected"), 3)
            link(v, add_to(v, X, X))

        @block.sync
        def _(sp):
            for g in range(KP // 2):
                k = slice(2 * g, 2 * g + 2)
                sp.dma_start(patches[:, k, :], io["patches"][:, k, :]).then_inc(sem(f"patches_in{g}"), 16)
                sp.dma_start(tokW[:, k, :], kt("tokW", P, KP, D)[:, k, :]).then_inc(sem(f"patches_in{g}"), 16)
            def load_group(group):
                for dst, src, g in loads:
                    if g == group:
                        sp.dma_start(dst, src).then_inc(sem(f"weights{g}"), 16)
            for group in range(3):
                load_group(group)
            mamba_sp(sp)
            experts_sp(sp, 0, 2, XR, [("m0_w1", 0), ("m0_w3", FF)])
            load_group(3)
            experts_sp(sp, 1, 3, XN, [("m1_up", 0)])
            experts_sp(sp, 2, 6, XR, [("m2_up", 0)])
            rel_sp(sp)
            experts_sp(sp, 3, 10, XN, [("m3_up", 0)])
            experts_sp(sp, 4, 12, XN, [("m4_up", 0)])
            sp.wait_ge(sem("done"), 1)
            sp.dma_start(out[0:FULL * P, :].rearrange("(t p) d -> p t d", p=P), X[:, 0:FULL, :]).then_inc(sem("out_written"), 16)
            sp.dma_start(out[FULL * P:N, :], X[0:LASTROWS, FULL, :]).then_inc(sem("out_written"), 16)
            sp.wait_ge(sem("out_written"), 32)

        @block.tensor
        def _(pe):
            tokens_pe(pe)
            mamba_pe(pe)
            moe0_pe(pe)
            moe1_pe(pe)
            cos_pe(pe)
            moe2_pe(pe)
            rel_pe(pe)
            moe3_pe(pe)
            plain_pe(pe)
            moe4_pe(pe)

        @block.vector
        def _(v):
            v.memset(xT[KD:KD + 1, :, :], 1.0)
            v.memset(ones[:], 1.0)
            v.memset(ones_b[:], 1.0).then_inc(sem("ones_set"), 1)
            v.memset(XIN[:], 0.0)
            v.memset(minus_half[:], -0.5)
            v.memset(X2[:, NT - 1, :], 0.0)
            link(v, v.memset(SC[:], 0.0))
            tokens_v(v)
            mamba_v(v)
            moe0_v(v)
            moe1_v(v)
            cos_v(v)
            moe2_v(v)
            rel_v(v)
            moe3_v(v)
            plain_v(v)
            moe4_v(v)
            v.memset(zeros[0:1, :], 0.0).then_inc(sem("done"), 1)

        @block.scalar
        def _(act):
            mamba_act(act)
            moe0_act(act)
            moe1_act(act)
            cos_act(act)
            moe2_act(act)
            rel_act(act)
            moe3_act(act)
            plain_act(act)
            moe4_act(act)

        @block.gpsimd
        def _(p):
            p.memset(zeros[:], 0.0).then_inc(sem("zeros"), 1)
            p.wait_ge(sem("zeros"), 1)
            p.dma_start(YD.rearrange("(b p) d -> p b d", p=P), zeros[:].unsqueeze(1).to_broadcast([P, 4 * NT, D]))\
                .then_inc(sem("zeroed"), 16)
            mamba_pool(p)
            norm_pool(p, 2)
            experts_pool(p, 0)
            norm_pool(p, 3)
            experts_pool(p, 1)
            norm_pool(p, 4)
            cos_pool(p)
            norm_pool(p, 5)
            norm_pool(p, 6)
            experts_pool(p, 2)
            norm_pool(p, 7)
            p.memset(WR[:], 0.0).then_inc(sem("rel_clear"), 1)
            p.wait_ge(sem("rel_clear"), 1)
            norm_pool(p, 8)
            p.memset(KM[:], 0.0).then_inc(sem("rel_clear"), 1)
            p.wait_ge(sem("rel_clear"), 2)
            p.memset(RB8[32:64], 0.0).then_inc(sem("rel_clear"), 1)
            norm_pool(p, 9)
            norm_pool(p, 10)
            experts_pool(p, 3)
            norm_pool(p, 11)
            norm_pool(p, 12)
            experts_pool(p, 4, lambda b, s: m4_rstd(p, b, s))


def prepare(i):
    f = {k: np.asarray(v) for k, v in i.items()}
    c = np.ascontiguousarray
    a = {}
    x = f["x"].reshape(B, 6, 16, 6, 16, 3).transpose(2, 4, 5, 0, 1, 3).reshape(PATCH, B, T - 1)
    pt = np.zeros((PATCH, NPAD), np.float32)
    pt[:, :N].reshape(PATCH, B, T)[:, :, 1:] = x
    a["patches"] = c(pt.reshape(KP, P, NPAD).transpose(1, 0, 2))
    a["tokW"] = f["L0_tok_W"]
    oh = np.zeros((T + 1, NPAD), np.float32)
    for n in range(N):
        oh[n % T, n] = 1
        if n % T == 0:
            oh[T, n] = 1
    a["tok_onehot"] = oh
    a["postab"] = np.concatenate([f["L0_tok_pos_emb"][0], f["L0_tok_class_emb"][0]], 0)
    a["ident"] = np.eye(P, dtype=np.float32)
    a["rev_iota"] = np.tile(np.arange(16, 0, -1, dtype=np.float32), (P, 1))
    a["before"] = np.triu(np.ones((P, P), np.float32), 1)
    a["steps128"] = np.tile(np.arange(NT, dtype=np.float32) * P, (P, 1))
    a["iota"] = np.tile(np.arange(P, dtype=np.float32), (P, 1))
    row = np.arange(4 * NPAD).reshape(4, NT, P).transpose(2, 0, 1)
    a["own_row"] = np.arange(P, dtype=np.float32)[:, None]
    a["tile_no"] = np.tile((np.arange(3 * NT).reshape(3, NT) - EMPTY // P).astype(np.float32), (P, 1, 1))
    a["shared_rows"] = row[:, 3, :].astype(np.int32)
    a["head_mask12"] = np.kron(np.eye(3), np.ones((T, 1))).astype(np.float32)
    a["head_mask8"] = np.kron(np.eye(2), np.ones((T, 1))).astype(np.float32)
    a["khead12"] = np.kron(np.eye(12), np.ones((8, 1))).astype(np.float32)
    a["khead24"] = np.kron(np.eye(6), np.ones((16, 1))).astype(np.float32)
    one = np.float32
    rate = np.exp(np.log(one((T + 1) / 2.0)) / one(NPOS // 2))
    width = rate ** np.arange(1, NPOS // 2 + 1, dtype=np.float32)
    dist = np.arange(-(T - 1), T, dtype=np.float32)
    unsigned = (np.abs(dist)[None, :] <= width[:, None]).astype(np.float32)
    a["rel_basis"] = np.concatenate([unsigned, np.sign(dist)[None, :] * unsigned], 0)

    def colsof(v, p):
        return c(v.reshape(-1, p).T)

    L = "L0_attn_"
    a["g_mamba"] = colsof(f[L + "g_mamba"], KD)
    a["w_in"] = f[L + "w_in"]
    a["conv_w"] = c(f[L + "conv_w"].reshape(NC_I, P, DCONV).transpose(1, 0, 2))
    a["conv_b"] = colsof(f[L + "conv_b"], P)
    a["w_xproj"] = f[L + "w_xproj"]
    a["w_dt"] = f[L + "w_dt"]
    a["b_dt"] = colsof(f[L + "b_dt"], P)
    a["A_log"] = c(f[L + "A_log"].reshape(NC_I, P, DS).transpose(1, 0, 2))
    a["D_skip"] = colsof(f[L + "D_skip"], P)
    a["w_out"] = f[L + "w_out"]
    a["g_moe"] = colsof(f[L + "g_moe"], KD)
    a["router0"] = f[L + "w_router"]
    a["m0_cols"] = c(f[L + "g_exp"].reshape(8, 2, KD).transpose(0, 2, 1))
    a["m0_w1"], a["m0_w3"], a["m0_down"] = f[L + "w1"], f[L + "w3"], f[L + "w2"]
    L = "L0_ffn_"
    a["gate1"] = c(f[L + "gate_w"].T)
    a["gate1_b"] = f[L + "gate_b"][None]
    a["m1_cols"] = c(f[L + "b_fc"].reshape(8, NCH, P).transpose(0, 2, 1))
    a["m1_up"] = c(f[L + "w_fc"].transpose(0, 2, 1))
    a["m1_down"] = c(f[L + "w_proj"].transpose(0, 2, 1))
    a["b_proj"] = f[L + "b_proj"]
    a["theta"] = f["L1_attn_theta"][:, None]
    a["w_comb"] = c(f["L1_attn_W_combine"].T)
    a["ln_w1"] = colsof(f["L1_ffn_ln_w"], KD)
    a["router2"] = f["L1_ffn_w_router"]
    a["m2_up"], a["m2_down"] = f["L1_ffn_wi"], f["L1_ffn_wo"]
    L = "L2_attn_"
    a["norm1_w"], a["norm2_w"] = colsof(f[L + "norm1_w"], KD), colsof(f[L + "norm2_w"], KD)
    a["wq"], a["wk"], a["wv"], a["wo"] = (f[L + k] for k in ("wq", "wk", "wv", "wo"))
    a["bo"] = f[L + "bo"][None]
    a["u_param"] = colsof(f[L + "u_param"].reshape(-1), P)
    a["v_param"] = colsof(f[L + "v_param"].reshape(-1), P)
    a["w_posT"] = c(f[L + "w_pos"].reshape(LH * LDK, NPOS).T)
    a["L2w1"], a["L2w2"] = f[L + "w1"], f[L + "w2"]
    a["L2b1"] = colsof(f[L + "b1"], P)
    a["L2b2"] = f[L + "b2"][None]
    L = "L2_ffn_"
    a["gate3"] = f[L + "w_gate"]
    a["m3_up"] = c(f[L + "w_fc"].reshape(D, FF, 8).transpose(2, 0, 1))
    a["m3_down"] = c(f[L + "w_proj"].reshape(FF, D, 8).transpose(2, 0, 1))
    L = "L3_attn_"
    a["wqkv"] = c(f[L + "w_qkv"].T)
    a["bqk"] = colsof(f[L + "b_qkv"][:2 * D], KD)
    a["bv"] = f[L + "b_qkv"][None, 2 * D:]
    a["wo3"] = c(f[L + "w_out"].T)
    a["bo3"] = f[L + "b_out"][None]
    L = "L3_ffn_"
    a["gate4"] = f[L + "gate_w"]
    a["gate4_b"] = f[L + "gate_b"][None]
    a["m4_up"], a["m4_down"] = f[L + "fc1_w"], f[L + "fc2_w"]
    a["m4_up_b"] = f[L + "fc1_b"]
    a["m4_cols"] = c(np.concatenate([f[L + k].reshape(16, NFH, P) for k in ("ln_w", "ln_b")], 1).transpose(0, 2, 1))
    a["fc2_b"] = f[L + "fc2_b"]
    return {k: c(v) for k, v in a.items()}


def kernel(**inputs):
    import concourse.bacc as _bacc
    from concourse import mybir as _mybir
    from concourse.bass_utils import run_bass_kernel_spmd as _run

    nc = _bacc.Bacc("TRN2", target_bir_lowering=False, num_devices=1)
    arrays = {f"in_{k}": v for k, v in prepare(inputs).items()}
    io = {k[3:]: nc.dram_tensor(k, v.shape, _mybir.dt.from_np(v.dtype), kind="ExternalInput").ap()
          for k, v in arrays.items()}
    out = nc.dram_tensor("out_0", (N, D), F32, kind="ExternalOutput").ap()
    build(nc, io, out)
    r = _run(nc, [arrays], core_ids=[0])
    return r.results[0]["out_0"].reshape(B, T, D)
```
